# Optimizing a Trainium2 kernel written in Bass

```python
import numpy as np
import jax
import jax.numpy as jnp

def _softmax(x, axis=-1):
    return jax.nn.softmax(x, axis=axis)

def _gelu(x):
    return jax.nn.gelu(x, approximate=True)

def _silu(x):
    return jax.nn.silu(x)

def _sigmoid(x):
    return jax.nn.sigmoid(x)

def _layernorm(x, axis=-1, eps=1e-05):
    m = jnp.mean(x, axis=axis, keepdims=True)
    v = jnp.var(x, axis=axis, keepdims=True)
    return (x - m) / jnp.sqrt(v + eps)

def _scatter_add(tgt, idx, src, axis=0):
    return tgt.at[idx].add(src)

def _segment_sum(src, seg, n):
    return jax.ops.segment_sum(src, seg, n)
kernel_name = 'mk_macaron_d2_jaxref_r8_13ceb9'

def setup_inputs(seed: int=0):
    np.random.seed(seed)
    _w = jnp.asarray

    def _L0_attn_setup():
        import jax, jax.numpy as jnp
        import numpy as np
        B, N, C = (32, 64, 128)
        H = 16
        D = C // H
        MAX_SEQ = 64
        BASE = 10000.0

        def _rope_tables(n, d):
            position = jnp.arange(n, dtype=jnp.float32)[:, None]
            div_term = jnp.exp(jnp.arange(0, d, 2, dtype=jnp.float32) * (-np.log(BASE) / d))
            ang = position * div_term
            return (jnp.sin(ang), jnp.cos(ang))

        def _apply_rope(x, sin, cos):
            x1 = x[..., ::2]
            x2 = x[..., 1::2]
            out = jnp.stack([x1 * cos - x2 * sin, x1 * sin + x2 * cos], axis=-1)
            return out.reshape(*x.shape[:-1], -1)
        key = jax.random.key(seed)
        k1, k2, k3, k4, k5 = jax.random.split(key, 5)
        s = 0.02
        return {'x': jax.random.normal(k1, (B, N, C), dtype=jnp.float32), 'w_qkv': jax.random.normal(k2, (3 * C, C), dtype=jnp.float32) * s, 'b_qkv': jax.random.normal(k3, (3 * C,), dtype=jnp.float32) * s, 'w_lepe': jax.random.normal(k4, (C, 1, 3), dtype=jnp.float32) * s, 'b_lepe': jax.random.normal(k5, (C,), dtype=jnp.float32) * s}
    _L0_attn_in = _L0_attn_setup()

    def _L0_ffn_setup():
        import jax, jax.numpy as jnp
        import numpy as np
        B, S, D = (1, 256, 128)
        E, K, F = (64, 8, 96)
        SF = 96
        C = 64
        ROUTED_SCALE = 1.0

        def _moe_forward(x, router_w, w_gate, w_up, w_down, ws_gate_up, ws_down):
            T = x.shape[0]
            logits = x.astype(jnp.float32) @ router_w.T
            probs = jax.nn.softmax(logits, axis=-1)
            topk_w, topk_ids = jax.lax.top_k(probs, K)
            topk_w = topk_w / jnp.sum(topk_w, axis=-1, keepdims=True)
            topk_w = topk_w.astype(x.dtype)
            N = T * K
            flat_e = topk_ids.reshape(-1)
            flat_w = topk_w.reshape(-1)
            tok = jnp.arange(N) // K
            onehot = flat_e[:, None] == jnp.arange(E)[None, :]
            pos = jnp.cumsum(onehot, axis=0)[jnp.arange(N), flat_e] - 1
            valid = pos < C
            idx = jnp.where(valid, flat_e * C + pos, E * C)
            x_buf = jnp.zeros((E * C + 1, x.shape[1]), x.dtype).at[idx].set(x[tok])
            xb = x_buf[:E * C].reshape(E, C, -1)
            g = jnp.einsum('ecd,edf->ecf', xb, w_gate)
            u = jnp.einsum('ecd,edf->ecf', xb, w_up)
            h = jax.nn.silu(g) * u
            y = jnp.einsum('ecf,efd->ecd', h, w_down).reshape(E * C, -1)
            safe = jnp.where(valid, idx, 0)
            contrib = y[safe] * (flat_w * valid.astype(flat_w.dtype))[:, None]
            routed = jax.ops.segment_sum(contrib, tok, num_segments=T)
            routed = routed * ROUTED_SCALE
            gu = x @ ws_gate_up
            sg, su = (gu[:, :SF], gu[:, SF:])
            shared = jax.nn.silu(sg) * su @ ws_down
            return routed + shared
        key = jax.random.key(seed)
        ks = jax.random.split(key, 7)
        w = 0.02
        return {'hidden_states': jax.random.normal(ks[0], (B, S, D), jnp.float32), 'router_w': jax.random.normal(ks[1], (E, D), jnp.float32) * w, 'w_gate': jax.random.normal(ks[2], (E, D, F), jnp.float32) * w, 'w_up': jax.random.normal(ks[3], (E, D, F), jnp.float32) * w, 'w_down': jax.random.normal(ks[4], (E, F, D), jnp.float32) * w, 'ws_gate_up': jax.random.normal(ks[5], (D, 2 * SF), jnp.float32) * w, 'ws_down': jax.random.normal(ks[6], (SF, D), jnp.float32) * w}
    _L0_ffn_in = _L0_ffn_setup()

    def _L1_attn_setup():
        import jax, jax.numpy as jnp
        import numpy as np
        import math
        B, T, E, H, DQ, NB, MAXLEN = (4, 128, 128, 16, 64, 10, 128)
        NEG = -1000000000.0

        def _attn_forward(X, Wq, bq, Wk, Wv, Wproj, bproj, Wr, br, b_nd):
            b, t, e = X.shape
            maxlen = b_nd.shape[1]
            nb = b_nd.shape[0]
            h = H
            dq = Wq.shape[1] // h
            Q = (X @ Wq + bq).reshape(b, t, h, dq).transpose(0, 2, 1, 3)
            K = (X @ Wk).reshape(b, t, h, dq).transpose(0, 2, 1, 3)
            V = (X @ Wv).reshape(b, t, h, dq).transpose(0, 2, 1, 3)
            R = (X @ Wr + br).reshape(b, t, h, nb).transpose(0, 2, 1, 3)
            d = jnp.arange(t)[:, None] - jnp.arange(t)[None, :]
            valid = (d >= 0) & (d < maxlen)
            bias = jnp.where(valid, 0.0, NEG).astype(jnp.float32)
            D_ntT = jnp.where(valid[None, :, :], b_nd[:, jnp.clip(d, 0, maxlen - 1)], 0.0)
            extra = jnp.einsum('bhtn,ntp->bhtp', R, D_ntT)
            logits = jnp.einsum('bhtd,bhpd->bhtp', Q, K) / math.sqrt(dq) + bias + extra
            W = jax.nn.softmax(logits, axis=-1)
            A = jnp.einsum('bhtp,bhpd->bhtd', W, V)
            A = A.transpose(0, 2, 1, 3).reshape(b, t, h * dq)
            return A @ Wproj + bproj
        key = jax.random.key(seed)
        k = jax.random.split(key, 10)
        X = jax.random.normal(k[0], (B, T, E), jnp.float32)
        Wq = jax.random.normal(k[1], (E, H * DQ), jnp.float32) * (0.1 / math.sqrt(E))
        bq = jnp.zeros((H * DQ,), jnp.float32)
        Wk = jax.random.normal(k[2], (E, H * DQ), jnp.float32) * (0.2 / math.sqrt(E))
        Wv = jax.random.normal(k[3], (E, H * DQ), jnp.float32) * (1.0 / math.sqrt(E))
        Wproj = jax.random.normal(k[4], (H * DQ, E), jnp.float32) * (1.0 / math.sqrt(H * DQ))
        bproj = jnp.zeros((E,), jnp.float32)
        Wr = jax.random.normal(k[5], (E, H * NB), jnp.float32) * (0.1 / math.sqrt(E))
        br = jnp.zeros((H * NB,), jnp.float32)
        b_nd = jax.random.normal(k[6], (NB, MAXLEN), jnp.float32) * 0.2
        return dict(X=X, Wq=Wq, bq=bq, Wk=Wk, Wv=Wv, Wproj=Wproj, bproj=bproj, Wr=Wr, br=br, b_nd=b_nd)
    _L1_attn_in = _L1_attn_setup()

    def _L1_ffn_setup():
        import jax, jax.numpy as jnp
        import numpy as np
        DIM, FF, E = (128, 512, 8)
        B, S = (2, 256)
        key = jax.random.key(seed)
        ks = jax.random.split(key, 7)
        sd = 0.02
        return {'x': jax.random.normal(ks[0], (B, S, DIM), dtype=jnp.float32), 'Wg': jax.random.normal(ks[1], (DIM, E), dtype=jnp.float32) * sd, 'bg': jnp.zeros((E,), dtype=jnp.float32), 'W1': jax.random.normal(ks[2], (E, DIM, FF), dtype=jnp.float32) * sd, 'b1': jnp.zeros((E, FF), dtype=jnp.float32), 'W2': jax.random.normal(ks[3], (E, FF, DIM), dtype=jnp.float32) * sd, 'b2': jnp.zeros((E, DIM), dtype=jnp.float32)}
    _L1_ffn_in = _L1_ffn_setup()
    _d = {'L0_attn_x': _L0_attn_in['x'], 'L0_attn_w_qkv': _L0_attn_in['w_qkv'], 'L0_attn_b_qkv': _L0_attn_in['b_qkv'], 'L0_attn_w_lepe': _L0_attn_in['w_lepe'], 'L0_attn_b_lepe': _L0_attn_in['b_lepe'], 'L0_ffn_router_w': _L0_ffn_in['router_w'], 'L0_ffn_w_gate': _L0_ffn_in['w_gate'], 'L0_ffn_w_up': _L0_ffn_in['w_up'], 'L0_ffn_w_down': _L0_ffn_in['w_down'], 'L0_ffn_ws_gate_up': _L0_ffn_in['ws_gate_up'], 'L0_ffn_ws_down': _L0_ffn_in['ws_down'], 'L1_attn_Wq': _L1_attn_in['Wq'], 'L1_attn_bq': _L1_attn_in['bq'], 'L1_attn_Wk': _L1_attn_in['Wk'], 'L1_attn_Wv': _L1_attn_in['Wv'], 'L1_attn_Wproj': _L1_attn_in['Wproj'], 'L1_attn_bproj': _L1_attn_in['bproj'], 'L1_attn_Wr': _L1_attn_in['Wr'], 'L1_attn_br': _L1_attn_in['br'], 'L1_attn_b_nd': _L1_attn_in['b_nd'], 'L1_ffn_Wg': _L1_ffn_in['Wg'], 'L1_ffn_bg': _L1_ffn_in['bg'], 'L1_ffn_W1': _L1_ffn_in['W1'], 'L1_ffn_b1': _L1_ffn_in['b1'], 'L1_ffn_W2': _L1_ffn_in['W2'], 'L1_ffn_b2': _L1_ffn_in['b2']}
    _x0 = _d['L0_attn_x']
    _d['L0_attn_x'] = jax.random.normal(jax.random.fold_in(jax.random.key(seed), 1), (8, 256, 128), dtype=_x0.dtype)
    del _x0
    return _d

def reference(L0_attn_x, L0_attn_w_qkv, L0_attn_b_qkv, L0_attn_w_lepe, L0_attn_b_lepe, L0_ffn_router_w, L0_ffn_w_gate, L0_ffn_w_up, L0_ffn_w_down, L0_ffn_ws_gate_up, L0_ffn_ws_down, L1_attn_Wq, L1_attn_bq, L1_attn_Wk, L1_attn_Wv, L1_attn_Wproj, L1_attn_bproj, L1_attn_Wr, L1_attn_br, L1_attn_b_nd, L1_ffn_Wg, L1_ffn_bg, L1_ffn_W1, L1_ffn_b1, L1_ffn_W2, L1_ffn_b2):

    def _L0_attn_ref(x, w_qkv, b_qkv, w_lepe, b_lepe):
        import jax, jax.numpy as jnp
        import numpy as np
        B, N, C = (32, 64, 128)
        H = 16
        D = C // H
        MAX_SEQ = 64
        BASE = 10000.0

        def _rope_tables(n, d):
            position = jnp.arange(n, dtype=jnp.float32)[:, None]
            div_term = jnp.exp(jnp.arange(0, d, 2, dtype=jnp.float32) * (-np.log(BASE) / d))
            ang = position * div_term
            return (jnp.sin(ang), jnp.cos(ang))

        def _apply_rope(x, sin, cos):
            x1 = x[..., ::2]
            x2 = x[..., 1::2]
            out = jnp.stack([x1 * cos - x2 * sin, x1 * sin + x2 * cos], axis=-1)
            return out.reshape(*x.shape[:-1], -1)
        b, n, c = x.shape
        scale = 1.0 / np.sqrt(D)
        sin, cos = _rope_tables(n, D)
        qkv = (x @ w_qkv.T + b_qkv).reshape(b, n, 3, H, D).transpose(2, 0, 3, 1, 4)
        q, k, v = (qkv[0], qkv[1], qkv[2])
        q = jax.nn.elu(q) + 1.0
        k = jax.nn.elu(k) + 1.0
        q = _apply_rope(q, sin, cos)
        k = _apply_rope(k, sin, cos)
        attn = jnp.einsum('bhnd,bhmd->bhnm', q, k) * scale
        attn = jax.nn.softmax(attn, axis=-1)
        attn_out = jnp.einsum('bhnm,bhmd->bhnd', attn, v)
        attn_out = attn_out.transpose(0, 2, 1, 3).reshape(b, n, c)
        v_conv = v.transpose(0, 2, 1, 3).reshape(b, n, c).transpose(0, 2, 1)
        lepe = jax.lax.conv_general_dilated(v_conv, w_lepe, window_strides=(1,), padding=((1, 1),), dimension_numbers=('NCH', 'OIH', 'NCH'), feature_group_count=c) + b_lepe[None, :, None]
        lepe = lepe.transpose(0, 2, 1)
        return attn_out + lepe

    def _L0_ffn_ref(hidden_states, router_w, w_gate, w_up, w_down, ws_gate_up, ws_down):
        import jax, jax.numpy as jnp
        import numpy as np
        B, S, D = (1, 256, 128)
        E, K, F = (64, 8, 96)
        SF = 96
        C = 64
        ROUTED_SCALE = 1.0

        def _moe_forward(x, router_w, w_gate, w_up, w_down, ws_gate_up, ws_down):
            T = x.shape[0]
            logits = x.astype(jnp.float32) @ router_w.T
            probs = jax.nn.softmax(logits, axis=-1)
            topk_w, topk_ids = jax.lax.top_k(probs, K)
            topk_w = topk_w / jnp.sum(topk_w, axis=-1, keepdims=True)
            topk_w = topk_w.astype(x.dtype)
            N = T * K
            flat_e = topk_ids.reshape(-1)
            flat_w = topk_w.reshape(-1)
            tok = jnp.arange(N) // K
            onehot = flat_e[:, None] == jnp.arange(E)[None, :]
            pos = jnp.cumsum(onehot, axis=0)[jnp.arange(N), flat_e] - 1
            valid = pos < C
            idx = jnp.where(valid, flat_e * C + pos, E * C)
            x_buf = jnp.zeros((E * C + 1, x.shape[1]), x.dtype).at[idx].set(x[tok])
            xb = x_buf[:E * C].reshape(E, C, -1)
            g = jnp.einsum('ecd,edf->ecf', xb, w_gate)
            u = jnp.einsum('ecd,edf->ecf', xb, w_up)
            h = jax.nn.silu(g) * u
            y = jnp.einsum('ecf,efd->ecd', h, w_down).reshape(E * C, -1)
            safe = jnp.where(valid, idx, 0)
            contrib = y[safe] * (flat_w * valid.astype(flat_w.dtype))[:, None]
            routed = jax.ops.segment_sum(contrib, tok, num_segments=T)
            routed = routed * ROUTED_SCALE
            gu = x @ ws_gate_up
            sg, su = (gu[:, :SF], gu[:, SF:])
            shared = jax.nn.silu(sg) * su @ ws_down
            return routed + shared
        b, s, d = hidden_states.shape
        x = hidden_states.reshape(-1, d)
        out = _moe_forward(x, router_w, w_gate, w_up, w_down, ws_gate_up, ws_down)
        return out.reshape(b, s, d)

    def _L1_attn_ref(X, Wq, bq, Wk, Wv, Wproj, bproj, Wr, br, b_nd):
        import jax, jax.numpy as jnp
        import numpy as np
        import math
        B, T, E, H, DQ, NB, MAXLEN = (4, 128, 128, 16, 64, 10, 128)
        NEG = -1000000000.0

        def _attn_forward(X, Wq, bq, Wk, Wv, Wproj, bproj, Wr, br, b_nd):
            b, t, e = X.shape
            maxlen = b_nd.shape[1]
            nb = b_nd.shape[0]
            h = H
            dq = Wq.shape[1] // h
            Q = (X @ Wq + bq).reshape(b, t, h, dq).transpose(0, 2, 1, 3)
            K = (X @ Wk).reshape(b, t, h, dq).transpose(0, 2, 1, 3)
            V = (X @ Wv).reshape(b, t, h, dq).transpose(0, 2, 1, 3)
            R = (X @ Wr + br).reshape(b, t, h, nb).transpose(0, 2, 1, 3)
            d = jnp.arange(t)[:, None] - jnp.arange(t)[None, :]
            valid = (d >= 0) & (d < maxlen)
            bias = jnp.where(valid, 0.0, NEG).astype(jnp.float32)
            D_ntT = jnp.where(valid[None, :, :], b_nd[:, jnp.clip(d, 0, maxlen - 1)], 0.0)
            extra = jnp.einsum('bhtn,ntp->bhtp', R, D_ntT)
            logits = jnp.einsum('bhtd,bhpd->bhtp', Q, K) / math.sqrt(dq) + bias + extra
            W = jax.nn.softmax(logits, axis=-1)
            A = jnp.einsum('bhtp,bhpd->bhtd', W, V)
            A = A.transpose(0, 2, 1, 3).reshape(b, t, h * dq)
            return A @ Wproj + bproj
        return _attn_forward(X, Wq, bq, Wk, Wv, Wproj, bproj, Wr, br, b_nd)

    def _L1_ffn_ref(x, Wg, bg, W1, b1, W2, b2):
        import jax, jax.numpy as jnp
        import numpy as np
        DIM, FF, E = (128, 512, 8)
        B, S = (2, 256)
        probs = jax.nn.softmax(x @ Wg + bg, axis=-1)
        h = jax.nn.relu(jnp.einsum('bsd,edf->bsef', x, W1) + b1)
        all_out = jnp.einsum('bsef,efd->bsed', h, W2) + b2
        top_vals, top_idx = jax.lax.top_k(probs, 2)
        weights = top_vals / (jnp.sum(top_vals, axis=-1, keepdims=True) + 1e-09)
        selected = jnp.take_along_axis(all_out, top_idx[..., None], axis=2)
        return jnp.sum(selected * weights[..., None], axis=2)
    x = L0_attn_x
    x = x + 0.5 * _L0_ffn_ref(_layernorm(x, axis=-1), L0_ffn_router_w, L0_ffn_w_gate, L0_ffn_w_up, L0_ffn_w_down, L0_ffn_ws_gate_up, L0_ffn_ws_down)
    x = x + _L0_attn_ref(_layernorm(x, axis=-1), L0_attn_w_qkv, L0_attn_b_qkv, L0_attn_w_lepe, L0_attn_b_lepe)
    x = x + 0.5 * _L0_ffn_ref(_layernorm(x, axis=-1), L0_ffn_router_w, L0_ffn_w_gate, L0_ffn_w_up, L0_ffn_w_down, L0_ffn_ws_gate_up, L0_ffn_ws_down)
    x = x + 0.5 * _L1_ffn_ref(_layernorm(x, axis=-1), L1_ffn_Wg, L1_ffn_bg, L1_ffn_W1, L1_ffn_b1, L1_ffn_W2, L1_ffn_b2)
    x = x + _L1_attn_ref(_layernorm(x, axis=-1), L1_attn_Wq, L1_attn_bq, L1_attn_Wk, L1_attn_Wv, L1_attn_Wproj, L1_attn_bproj, L1_attn_Wr, L1_attn_br, L1_attn_b_nd)
    x = x + 0.5 * _L1_ffn_ref(_layernorm(x, axis=-1), L1_ffn_Wg, L1_ffn_bg, L1_ffn_W1, L1_ffn_b1, L1_ffn_W2, L1_ffn_b2)
    return x

_drawn_inputs = setup_inputs


def setup_inputs(seed=0):
    import zlib

    import numpy as np

    out = dict(_drawn_inputs(seed))
    spreads = {'L1_attn_bq': (0.0, 0.8),
     'L1_attn_bproj': (0.0, 0.1),
     'L1_attn_br': (0.0, 0.8),
     'L1_ffn_bg': (0.0, 0.339),
     'L1_ffn_b1': (0.0, 1.087),
     'L1_ffn_b2': (0.0, 0.323)}
    factors = {'L0_attn_w_lepe': 6.436,
     'L0_ffn_router_w': 8.0,
     'L0_ffn_w_gate': 8.0,
     'L0_ffn_w_up': 8.0,
     'L0_ffn_w_down': 8.0,
     'L0_ffn_ws_gate_up': 8.0,
     'L0_ffn_ws_down': 8.0,
     'L1_attn_Wq': 8.0,
     'L1_attn_Wk': 8.0,
     'L1_attn_Wr': 6.564,
     'L1_attn_b_nd': 4.656,
     'L0_attn_b_qkv': 2.809,
     'L0_attn_b_lepe': 2.918,
     'L1_ffn_W1': 3.556}
    for name, (base, spread) in spreads.items():
        noise = np.random.default_rng([zlib.crc32(name.encode()), seed]).standard_normal(out[name].shape)
        drawn = base * np.exp(spread * noise) if base else spread * noise
        out[name] = jnp.asarray(drawn.astype(out[name].dtype))
    for name, factor in factors.items():
        out[name] = (out[name] * factor).astype(out[name].dtype)
    return out
```

```python
from contextlib import ExitStack

import numpy as np
import concourse.bass as bass
from concourse import mybir

F32 = mybir.dt.float32
BF16 = mybir.dt.bfloat16
I32 = mybir.dt.int32
ALU = mybir.AluOpType
ACT = mybir.ActivationFunctionType
AX = mybir.AxisListType
ds = bass.ds

P = 128
BATCH = 8
SEQ = 256
TOKENS = BATCH * SEQ
TILES = TOKENS // P
BLOCK = 512
EPS = 1e-5

E0, TOP0, F0, CAPACITY = 64, 8, 96, 64
E1, F1 = 8, 512
FC1 = F1 // P


class Chain:

    def __init__(self, sem, start=0):
        self.sem, self.n = sem, start

    def on(self, ins):
        self.n += 1
        ins.then_inc(self.sem, 1)
        return self.n


class Core:

    def __init__(self, nc, ctx):
        self.nc, self.ctx = nc, ctx
        self.stage_sems = []

    def sem(self, name):
        s = self.ctx.enter_context(self.nc.semaphore(name))
        self.stage_sems.append(s)
        return s


def bcast(ap, n):
    return ap.unsqueeze(len(ap.shape)).to_broadcast(list(ap.shape) + [n])


def constants(core, act_name):
    nc, ctx = core.nc, core.ctx
    core.x = ctx.enter_context(nc.sbuf_tensor("x", [P, TILES, P], F32))
    core.ident = ctx.enter_context(nc.sbuf_tensor("ident", [P, P], F32))
    core.identb = ctx.enter_context(nc.sbuf_tensor("identb", [P, P], BF16))
    core.tri = ctx.enter_context(nc.sbuf_tensor("tri", [P, P], BF16))
    core.ones = ctx.enter_context(nc.sbuf_tensor("ones", [P, P], BF16))
    core.psum = ctx.enter_context(nc.psum_tensor("psum", [P, 8, 512], F32))
    core.bank = [core.psum[:, i, :] for i in range(8)]
    core.const_filled = core.sem("const_filled")
    core.const_ready = core.sem("const_ready")

    def pool(eng):
        eng.memset(core.ident[:, :], 0.0).then_inc(core.const_filled, 1)
        eng.memset(core.identb[:, :], 0.0).then_inc(core.const_filled, 1)
        eng.memset(core.tri[:, :], 1.0).then_inc(core.const_filled, 1)
        eng.memset(core.ones[:, :], 1.0).then_inc(core.const_ready, 1)
        eng.wait_ge(core.const_filled, 3)
        for m in (core.ident, core.identb):
            eng.affine_select(out=m[:, :], in_=m[:, :], compare_op=ALU.not_equal, fill=1.0,
                              base=0, pattern=[[-1, P]], channel_multiplier=1).then_inc(core.const_ready, 1)
        eng.affine_select(out=core.tri[:, :], in_=core.tri[:, :], compare_op=ALU.is_ge, fill=0.0,
                          base=0, pattern=[[1, P]], channel_multiplier=-1).then_inc(core.const_ready, 1)

    return pool


class LayerNorm:

    def __init__(self, core, ctx, name):
        nc = core.nc
        self.core = core
        sb = lambda n, s, d=F32: ctx.enter_context(nc.sbuf_tensor(f"{name}_{n}", s, d))
        self.xn = sb("xn", [P, TILES, P])
        self.sq = sb("sq", [P, TILES, P])
        self.xnT = sb("xnT", [P, TOKENS])
        self.stat = sb("stat", [P, 6, TILES])
        self.ps = core.bank[0:4]
        self.chain = core.sem(f"{name}_ln_chain")
        self.var_ready = core.sem(f"{name}_var_ready")
        self.std_ready = core.sem(f"{name}_std_ready")
        self.xn_ready = core.sem(f"{name}_xn_ready")
        self.turned = core.sem(f"{name}_turned")
        self.xnT_ready = core.sem(f"{name}_xnT_ready")

    def vector(self, dve):
        x, xn, sq, st = self.core.x, self.xn, self.sq, self.stat
        c = Chain(self.chain)

        def step(ins):
            dve.wait_ge(c.sem, c.on(ins))

        total, negmean, ve, rstd, t = (st[:, i, :] for i in range(5))
        step(dve.tensor_reduce(total, x[:, :, :], AX.X, ALU.add))
        step(dve.tensor_scalar(negmean, total, -1.0 / P, None, ALU.mult))
        step(dve.tensor_tensor(xn[:, :, :], x[:, :, :], bcast(negmean, P), ALU.add))
        step(dve.tensor_tensor(sq[:, :, :], xn[:, :, :], xn[:, :, :], ALU.mult))
        step(dve.tensor_reduce(total, sq[:, :, :], AX.X, ALU.add))
        step(dve.tensor_scalar(ve, total, 1.0 / P, EPS, ALU.mult, ALU.add))
        dve.sem_inc(self.var_ready, 1)
        dve.wait_ge(self.std_ready, 1)
        step(dve.reciprocal(rstd, st[:, 5, :]))
        step(dve.tensor_tensor(t, rstd, rstd, ALU.mult))
        step(dve.tensor_tensor(t, t, ve, ALU.mult))
        step(dve.tensor_scalar(t, t, -0.5, 1.5, ALU.mult, ALU.add))
        step(dve.tensor_tensor(rstd, rstd, t, ALU.mult))
        for q in range(4):
            xq = xn[:, 4 * q:4 * q + 4, :]
            dve.tensor_tensor(xq, xq, bcast(rstd[:, 4 * q:4 * q + 4], P), ALU.mult).then_inc(self.xn_ready, 1)

    def tensor(self, pe):
        for q in range(4):
            pe.wait_ge(self.xn_ready, q + 1)
            for i in range(4):
                last = pe.transpose(self.ps[q][:, P * i:P * i + P], self.xn[:, 4 * q + i, :], self.core.ident[:, :])
            last.then_inc(self.turned, 1)

    def scalar(self, act):
        act.wait_ge(self.var_ready, 1)
        act.activation(self.stat[:, 5, :], self.stat[:, 2, :], ACT.Sqrt).then_inc(self.std_ready, 1)
        for q in range(4):
            act.wait_ge(self.turned, q + 1)
            act.activation(self.xnT[:, 512 * q:512 * q + 512], self.ps[q][:, :], ACT.Copy).then_inc(self.xnT_ready, 1)


def mixture_one(core, name, ctx, w):
    nc = core.nc
    sb = lambda n, s, d=F32: ctx.enter_context(nc.sbuf_tensor(f"{name}_{n}", s, d))
    ln = LayerNorm(core, ctx, name)
    wg = sb("wg", [P, E1])
    bg = sb("bg", [P, E1])
    w1 = sb("w1", [P, E1, F1])
    w2 = sb("w2", [P, E1, FC1, P])
    b1 = sb("b1", [P, E1, FC1])
    b2 = sb("b2", [E1, P])
    logit = sb("logit", [P, TILES, E1])
    prob = sb("prob", [P, TILES, E1])
    weight = sb("weight", [P, TILES, E1])
    cmp = sb("cmp", [P, TILES, E1, E1])
    eqs = sb("eqs", [P, TILES, E1, E1])
    lower = sb("lower", [P, E1, E1])
    col = sb("col", [P, 3, TILES])
    wT = sb("wT", [E1, TILES, P])
    hT = sb("hT", [P, 2, FC1, BLOCK])
    prod = sb("prod", [P, 4, P])
    ps_h = core.bank[4:6]
    ps_y = [b.rearrange("p (t n) -> p t n", n=P) for b in core.bank[6:8]]
    ps_logit = ps_y[0]
    loaded = core.sem(f"{name}_loaded")
    w_loaded = core.sem(f"{name}_w_loaded")
    lower_filled = core.sem(f"{name}_lower_filled")
    logits_done = core.sem(f"{name}_logits_done")
    shifted = core.sem(f"{name}_shifted")
    exp_done = core.sem(f"{name}_exp_done")
    weights_ready = core.sem(f"{name}_weights_ready")
    chain = core.sem(f"{name}_chain")
    wT_turned = core.sem(f"{name}_wT_turned")
    wT_ready = core.sem(f"{name}_wT_ready")
    bias_done = core.sem(f"{name}_bias_done")
    bias_added = core.sem(f"{name}_bias_added")
    h_done = core.sem(f"{name}_h_done")
    h_ready = core.sem(f"{name}_h_ready")
    y_done = core.sem(f"{name}_y_done")
    y_read = core.sem(f"{name}_y_read")
    y_added = core.sem(f"{name}_y_added")
    NB = TOKENS // BLOCK

    def sync(sp):
        sp.dma_start(wg[:, :], w["Wg"]).then_inc(loaded, 16)
        sp.dma_start(bg[:, :], w["bg"].unsqueeze(0).to_broadcast([P, E1])).then_inc(loaded, 16)
        sp.dma_start(b2[:, :], w["b2"]).then_inc(loaded, 16)
        sp.dma_start(b1[:, :, :], w["b1"]).then_inc(loaded, 16)
        for e in range(E1):
            sp.dma_start(w1[:, e, :], w["W1"][e]).then_inc(w_loaded, 16)
            sp.dma_start(w2[:, e, :, :], w["W2"][e].rearrange("(c p) d -> p c d", p=P)).then_inc(w_loaded, 16)

    def gpsimd(pool):
        pool.memset(lower[:, :, :], 1.0).then_inc(lower_filled, 1)
        pool.wait_ge(lower_filled, 1)
        pool.affine_select(out=lower[:, :, :], in_=lower[:, :, :], compare_op=ALU.is_gt, fill=0.0,
                           base=0, pattern=[[1, E1], [-1, E1]], channel_multiplier=0).then_inc(lower_filled, 1)

    def tensor(pe):
        ln.tensor(pe)
        pe.wait_ge(loaded, 64)
        for q in range(4):
            pe.wait_ge(ln.xnT_ready, q + 1)
            for i in range(4 * q, 4 * q + 4):
                last = pe.matmul(ps_logit[:, i // 4, E1 * (i % 4):E1 * (i % 4) + E1], ln.xnT[:, P * i:P * i + P],
                                 wg[:, :], start=True, stop=True)
        last.then_inc(logits_done, 1)
        pe.wait_ge(weights_ready, 1)
        for q in range(4):
            for i in range(4):
                last = pe.transpose(ln.ps[q][0:E1, P * i:P * i + P], weight[:, 4 * q + i, :], core.ident[:, :])
            last.then_inc(wT_turned, 1)
        for q in range(4):
            pe.wait_ge(wT_ready, q + 1)
            for i in range(4):
                last = pe.matmul(ln.ps[q][:, P * i:P * i + P], wT[:, 4 * q + i, :], b2[:, :], start=True, stop=True)
            last.then_inc(bias_done, 1)
        pe.wait_ge(w_loaded, 32 * E1)
        pe.sem_inc(y_done, 2)
        with pe.Fori(0, NB) as b:
            moving = ln.xnT[:, ds(b * BLOCK, BLOCK)]

            def hidden(e):
                for c in range(FC1):
                    pe.wait_ge(h_ready, b * (E1 * FC1) + (e * FC1 + c + 1))
                    pe.matmul(ps_h[c % 2][:, :], w1[:, e, P * c:P * c + P], moving,
                              start=True, stop=True).then_inc(h_done, 1)

            hidden(0)
            for e in range(E1):
                if e + 1 < E1:
                    hidden(e + 1)
                pe.wait_ge(h_ready, b * (E1 * FC1) + (e * FC1 + FC1 + 2))
                pe.wait_ge(y_read, b * E1 + (e + 1))
                for t in range(4):
                    for c in range(FC1):
                        last = pe.matmul(ps_y[e % 2][:, t, :], hT[:, e % 2, c, P * t:P * t + P], w2[:, e, c, :],
                                         start=(c == 0), stop=(c == FC1 - 1))
                last.then_inc(y_done, 1)

    def scalar(act):
        ln.scalar(act)
        act.wait_ge(shifted, 1)
        act.activation(prob[:, :, :], logit[:, :, :], ACT.Exp).then_inc(exp_done, 1)
        for q in range(4):
            act.wait_ge(wT_turned, q + 1)
            act.activation(wT[:, 4 * q:4 * q + 4, :], ln.ps[q][0:E1, :].rearrange("p (t n) -> p t n", t=4),
                           ACT.Copy).then_inc(wT_ready, 1)
        act.sem_inc(h_ready, 2)
        with act.Fori(0, NB) as b:
            for e in range(E1):
                act.wait_ge(y_done, b * E1 + (e + 1))
                for c in range(FC1):
                    act.wait_ge(h_done, b * (E1 * FC1) + (e * FC1 + c + 1))
                    act.activation(hT[:, e % 2, c, :], ps_h[c % 2][:, :], ACT.Relu,
                                   bias=b1[:, e, c:c + 1]).then_inc(h_ready, 1)

    def vector(dve):
        ln.vector(dve)
        c = Chain(chain)

        def step(ins):
            dve.wait_ge(c.sem, c.on(ins))

        total, den, top = (col[:, i, :] for i in range(3))
        dve.wait_ge(logits_done, 1)
        step(dve.tensor_tensor(logit[:, :, :].rearrange("p (a b) e -> p a b e", b=4),
                               ps_logit[:, :, 0:4 * E1].rearrange("p a (b e) -> p a b e", b=4),
                               bg[:, :].unsqueeze(1).unsqueeze(1).to_broadcast([P, 4, 4, E1]), ALU.add))
        step(dve.tensor_reduce(total, logit[:, :, :], AX.X, ALU.max))
        dve.tensor_tensor(logit[:, :, :], logit[:, :, :], bcast(total, E1), ALU.subtract).then_inc(shifted, 1)
        dve.wait_ge(exp_done, 1)
        step(dve.tensor_reduce(total, prob[:, :, :], AX.X, ALU.add))
        step(dve.reciprocal(den, total))
        step(dve.tensor_tensor(prob[:, :, :], prob[:, :, :], bcast(den, E1), ALU.mult))
        mine = bcast(prob[:, :, :], E1)
        others = prob[:, :, :].unsqueeze(2).to_broadcast([P, TILES, E1, E1])
        step(dve.tensor_tensor(cmp[:, :, :, :], others, mine, ALU.is_gt))
        step(dve.tensor_tensor(eqs[:, :, :, :], others, mine, ALU.is_equal))
        dve.wait_ge(lower_filled, 2)
        step(dve.tensor_tensor(eqs[:, :, :, :], eqs[:, :, :, :],
                               lower[:, :, :].unsqueeze(1).to_broadcast([P, TILES, E1, E1]), ALU.mult))
        step(dve.tensor_tensor(cmp[:, :, :, :], cmp[:, :, :, :], eqs[:, :, :, :], ALU.add))
        step(dve.tensor_reduce(weight[:, :, :], cmp[:, :, :, :], AX.X, ALU.add))
        step(dve.scalar_tensor_tensor(weight[:, :, :], weight[:, :, :], 2.0, prob[:, :, :], ALU.is_lt, ALU.mult))
        step(dve.tensor_reduce(top, weight[:, :, :], AX.X, ALU.add))
        step(dve.tensor_scalar(top, top, 1e-9, None, ALU.add))
        step(dve.reciprocal(den, top))
        step(dve.tensor_scalar(den, den, 0.5, None, ALU.mult))
        step(dve.tensor_tensor(weight[:, :, :], weight[:, :, :], bcast(den, E1), ALU.mult))
        dve.sem_inc(weights_ready, 1)
        for q in range(4):
            dve.wait_ge(bias_done, q + 1)
            xq = core.x[:, 4 * q:4 * q + 4, :]
            step(dve.tensor_tensor(xq, xq, ln.ps[q][:, :].rearrange("p (t n) -> p t n", t=4), ALU.add))
        dve.sem_inc(y_read, 2)
        dve.sem_inc(y_added, 1)
        with dve.Fori(0, NB) as b:
            for e in range(E1):
                dve.wait_ge(y_done, b * E1 + (e + 3))
                dve.wait_ge(y_added, b * E1 + (e + 1))
                wcol = weight[:, ds(b * 4, 4), e:e + 1].to_broadcast([P, 4, P])
                dve.tensor_tensor(prod[:, :, :], ps_y[e % 2][:, :, :], wcol, ALU.mult).then_inc(y_read, 1)
                dve.wait_ge(y_read, b * E1 + (e + 3))
                xb = core.x[:, ds(b * 4, 4), :]
                dve.tensor_tensor(xb, xb, prod[:, :, :], ALU.add).then_inc(y_added, 1)

    return dict(sync=sync, gpsimd=gpsimd, tensor=tensor, scalar=scalar, vector=vector)


def mixture_zero(core, name, ctx, w):
    nc = core.nc
    sb = lambda n, s, d=F32: ctx.enter_context(nc.sbuf_tensor(f"{name}_{n}", s, d))
    ln = LayerNorm(core, ctx, name)
    TB = 256
    NT = TB // P
    NBLK = TOKENS // TB
    WE = 4
    ROUNDS = E0 // (2 * WE)
    wr = sb("wr", [P, E0])
    wsgu = sb("wsgu", [P, 2 * F0])
    wsd = sb("wsd", [F0, P])
    wgu = [sb(f"wgu{i}", [P, WE, 2 * F0]) for i in range(2)]
    wd = [sb(f"wd{i}", [F0, WE, P]) for i in range(2)]
    ex = sb("ex", [P, TILES, E0])
    repl = sb("repl", [P, TILES, E0])
    mask = sb("mask", [P, TILES, E0], BF16)
    weight = sb("weight", [P, TILES, E0])
    base = sb("base", [P, TILES, E0])
    top = sb("top", [P, TILES, TOP0])
    col = sb("col", [P, 2, TILES])
    room = sb("room", [1, 2, NBLK])
    count_f = sb("count_f", [1, 1])
    count = sb("count", [1, 1], I32)
    act_s = sb("act_s", [F0, 2, BLOCK])
    hT = sb("hT", [F0, 2, BLOCK])
    prod = sb("prod", [P, NT, P])
    ps_gu = core.bank[4:6]
    ps_y = core.bank[6:8]
    loaded = core.sem(f"{name}_loaded")
    logits_done = core.sem(f"{name}_logits_done")
    shifted = core.sem(f"{name}_shifted")
    exp_done = core.sem(f"{name}_exp_done")
    mask_ready = core.sem(f"{name}_mask_ready")
    counted = core.sem(f"{name}_counted")
    chain = core.sem(f"{name}_chain")
    count_ready = core.sem(f"{name}_count_ready")
    sh_gu = core.sem(f"{name}_sh_gu")
    sh_silu = core.sem(f"{name}_sh_silu")
    sh_h = core.sem(f"{name}_sh_h")
    sh_y = core.sem(f"{name}_sh_y")
    sh_added = core.sem(f"{name}_sh_added")
    w_loaded = [core.sem(f"{name}_w_loaded{i}") for i in range(2)]
    w_free = core.sem(f"{name}_w_free")
    gu_done = core.sem(f"{name}_gu_done")
    silu_done = core.sem(f"{name}_silu_done")
    h_ready = core.sem(f"{name}_h_ready")
    y_done = core.sem(f"{name}_y_done")
    y_read = core.sem(f"{name}_y_read")
    y_added = core.sem(f"{name}_y_added")

    def sync(sp):
        sp.dma_start(wr[:, :], w["router"]).then_inc(loaded, 16)
        sp.dma_start(wsgu[:, :], w["ws_gate_up"]).then_inc(loaded, 16)
        sp.dma_start(wsd[:, :], w["ws_down"]).then_inc(loaded, 16)
        sp.wait_ge(count_ready, 1)
        n = sp.value_load(count[0:1, 0:1], min_val=1, max_val=NBLK)
        with sp.Fori(0, n) as b:
            with sp.Fori(0, ROUNDS) as r:
                for s in range(2):
                    sp.wait_ge(w_free, b * (2 * ROUNDS) + r * 2 + (s + 1))
                    sp.dma_start(wgu[s][:, :, :], w["gate_up"][:, ds(r * (2 * WE) + s * WE, WE), :]).then_inc(w_loaded[s], 16)
                    sp.dma_start(wd[s][:, :, :], w["down"][:, ds(r * (2 * WE) + s * WE, WE), :]).then_inc(w_loaded[s], 16)

    def gpsimd(pool):
        pass

    def tensor(pe):
        ln.tensor(pe)
        pe.wait_ge(loaded, 48)
        for q in range(4):
            pe.wait_ge(ln.xnT_ready, q + 1)
            for i in range(4 * q, 4 * q + 4):
                last = pe.matmul(ps_gu[i // 8][:, E0 * (i % 8):E0 * (i % 8) + E0], ln.xnT[:, P * i:P * i + P],
                                 wr[:, :], start=True, stop=True)
        last.then_inc(logits_done, 1)
        pe.wait_ge(mask_ready, 1)
        for h in range(2):
            m = mask[:, 8 * h:8 * h + 8, :].rearrange("p t e -> p (t e)")
            pe.matmul(ln.ps[h][:, :], core.tri[:, :], m, start=True, stop=True)
            last = pe.matmul(ln.ps[2 + h][:, :], core.ones[:, :], m, start=True, stop=True)
        last.then_inc(counted, 1)
        for q in range(4):
            xq = ln.xnT[:, BLOCK * q:BLOCK * q + BLOCK]
            if q:
                pe.wait_ge(sh_h, q)
            pe.matmul(ps_gu[0][0:F0, :], wsgu[:, 0:F0], xq, start=True, stop=True)
            pe.matmul(ps_gu[1][0:F0, :], wsgu[:, F0:2 * F0], xq, start=True, stop=True).then_inc(sh_gu, 1)
            pe.wait_ge(sh_h, q + 1)
            if q >= 2:
                pe.wait_ge(sh_added, q - 1)
            for t in range(4):
                last = pe.matmul(ps_y[q % 2][:, P * t:P * t + P], hT[:, q % 2, P * t:P * t + P], wsd[:, :],
                                 start=True, stop=True)
            last.then_inc(sh_y, 1)
        pe.wait_ge(sh_added, 4)
        pe.sem_inc(w_free, 2)
        pe.wait_ge(count_ready, 1)
        n = pe.value_load(count[0:1, 0:1], min_val=1, max_val=NBLK)
        with pe.Fori(0, n) as b:
            moving = ln.xnT[:, ds(b * TB, TB)]
            with pe.Fori(0, ROUNDS) as r:
                at = b * E0 + r * (2 * WE)

                def gate_up(k):
                    s = k // WE
                    if k % WE == 0:
                        pe.wait_ge(w_loaded[s], b * (32 * ROUNDS) + r * 32 + 32)
                    pe.wait_ge(h_ready, at + (k + 1))
                    pe.matmul(ps_gu[k % 2][0:F0, 0:TB], wgu[s][:, k % WE, 0:F0], moving, start=True, stop=True)
                    pe.matmul(ps_gu[k % 2][0:F0, TB:2 * TB], wgu[s][:, k % WE, F0:2 * F0], moving,
                              start=True, stop=True).then_inc(gu_done, 1)

                gate_up(0)
                for k in range(2 * WE):
                    if k + 1 < 2 * WE:
                        gate_up(k + 1)
                    pe.wait_ge(h_ready, at + (k + 3))
                    pe.wait_ge(y_read, at + (k + 1))
                    for t in range(NT):
                        last = pe.matmul(ps_y[k % 2][:, P * t:P * t + P], hT[:, k % 2, P * t:P * t + P],
                                         wd[k // WE][:, k % WE, :], start=True, stop=True)
                    last.then_inc(y_done, 1)
                    if k % WE == WE - 1:
                        pe.wait_ge(y_done, at + (k + 3))
                        pe.sem_inc(w_free, 1)

    def scalar(act):
        ln.scalar(act)
        act.wait_ge(shifted, 1)
        act.activation(ex[:, :, :], ex[:, :, :], ACT.Exp).then_inc(exp_done, 1)
        for q in range(4):
            act.wait_ge(sh_gu, q + 1)
            if q >= 2:
                act.wait_ge(sh_h, q - 1)
            act.activation(act_s[:, q % 2, :], ps_gu[0][0:F0, :], ACT.Silu).then_inc(sh_silu, 1)
        act.wait_ge(count_ready, 1)
        n = act.value_load(count[0:1, 0:1], min_val=1, max_val=NBLK)
        with act.Fori(0, n) as b:
            with act.Fori(0, ROUNDS) as r:
                for k in range(2 * WE):
                    at = b * E0 + r * (2 * WE) + k
                    act.wait_ge(gu_done, at + 1)
                    act.wait_ge(h_ready, at + 1)
                    act.activation(act_s[:, k % 2, 0:TB], ps_gu[k % 2][0:F0, 0:TB], ACT.Silu).then_inc(silu_done, 1)

    def vector(dve):
        ln.vector(dve)
        c = Chain(chain)

        def step(ins):
            dve.wait_ge(c.sem, c.on(ins))

        most, den = (col[:, i, :] for i in range(2))
        dve.wait_ge(logits_done, 1)
        for h in range(2):
            lg = ps_gu[h][:, :].rearrange("p (t e) -> p t e", e=E0)
            step(dve.tensor_reduce(most[:, 8 * h:8 * h + 8], lg, AX.X, ALU.max))
            step(dve.tensor_tensor(ex[:, 8 * h:8 * h + 8, :], lg, bcast(most[:, 8 * h:8 * h + 8], E0), ALU.subtract))
        dve.sem_inc(shifted, 1)
        dve.wait_ge(exp_done, 1)
        for i in range(TILES):
            last = dve.max(top[:, i, :], ex[:, i, :])
        step(last)
        for i in range(TILES):
            last = dve.match_replace(repl[:, i, :], top[:, i, :], ex[:, i, :], -1.0)
        step(last)
        step(dve.tensor_scalar(mask[:, :, :], repl[:, :, :], 0.0, None, ALU.is_lt))
        dve.sem_inc(mask_ready, 1)
        step(dve.scalar_tensor_tensor(weight[:, :, :], repl[:, :, :], 0.0, ex[:, :, :], ALU.is_lt, ALU.mult))
        step(dve.tensor_reduce(den, top[:, :, :], AX.X, ALU.add))
        step(dve.reciprocal(den, den))
        step(dve.tensor_scalar(den, den, 0.5, None, ALU.mult))
        step(dve.tensor_tensor(weight[:, :, :], weight[:, :, :], bcast(den, E0), ALU.mult))
        dve.wait_ge(counted, 1)
        step(dve.memset(base[:, 0, :], 0.0))
        for i in range(TILES - 1):
            tot = ln.ps[2 + i // 8][:, E0 * (i % 8):E0 * (i % 8) + E0]
            step(dve.tensor_tensor(base[:, i + 1, :], base[:, i, :], tot, ALU.add))
        step(dve.tensor_reduce(room[:, 0, :], base[0:1, 0:TILES:NT, :], AX.X, ALU.min))
        step(dve.tensor_scalar(room[:, 1, :], room[:, 0, :], float(CAPACITY), None, ALU.is_lt))
        step(dve.tensor_reduce(count_f[:, :], room[:, 1, :], AX.X, ALU.add))
        step(dve.tensor_copy(count[:, :], count_f[:, :]))
        dve.sem_inc(count_ready, 1)
        for h in range(2):
            cum = ln.ps[h][:, :].rearrange("p (t e) -> p t e", e=E0)
            bh = base[:, 8 * h:8 * h + 8, :]
            step(dve.tensor_tensor(bh, bh, cum, ALU.add))
        step(dve.scalar_tensor_tensor(weight[:, :, :], base[:, :, :], float(CAPACITY), weight[:, :, :],
                                      ALU.is_le, ALU.mult))
        for q in range(4):
            dve.wait_ge(sh_silu, q + 1)
            dve.tensor_tensor(hT[:, q % 2, :], act_s[:, q % 2, :], ps_gu[1][0:F0, :], ALU.mult).then_inc(sh_h, 1)
            dve.wait_ge(sh_y, q + 1)
            xq = core.x[:, 4 * q:4 * q + 4, :]
            dve.scalar_tensor_tensor(xq, ps_y[q % 2][:, :].rearrange("p (t n) -> p t n", n=P), 0.5, xq,
                                     ALU.mult, ALU.add).then_inc(sh_added, 1)
        dve.wait_ge(sh_added, 4)
        dve.sem_inc(h_ready, 2)
        dve.sem_inc(y_read, 2)
        dve.sem_inc(y_added, 1)
        dve.sem_inc(y_done, 2)
        n = dve.value_load(count[0:1, 0:1], min_val=1, max_val=NBLK)
        with dve.Fori(0, n) as b:
            xb = core.x[:, ds(b * NT, NT), :]
            with dve.Fori(0, ROUNDS) as r:
                at = b * E0 + r * (2 * WE)

                def hidden(k):
                    dve.wait_ge(silu_done, at + (k + 1))
                    dve.wait_ge(y_done, at + (k + 1))
                    dve.tensor_tensor(hT[:, k % 2, 0:TB], act_s[:, k % 2, 0:TB], ps_gu[k % 2][0:F0, TB:2 * TB],
                                      ALU.mult).then_inc(h_ready, 1)

                hidden(0)
                for k in range(2 * WE):
                    if k + 1 < 2 * WE:
                        hidden(k + 1)
                    dve.wait_ge(y_done, at + (k + 3))
                    dve.wait_ge(y_added, at + (k + 1))
                    wcol = weight[:, ds(b * NT, NT), ds(r * (2 * WE) + k, 1)].to_broadcast([P, NT, P])
                    y = ps_y[k % 2][:, 0:TB].rearrange("p (t n) -> p t n", n=P)
                    dve.tensor_tensor(prod[:, :, :], y, wcol, ALU.mult).then_inc(y_read, 1)
                    dve.wait_ge(y_read, at + (k + 3))
                    dve.tensor_tensor(xb, xb, prod[:, :, :], ALU.add).then_inc(y_added, 1)

    return dict(sync=sync, gpsimd=gpsimd, tensor=tensor, scalar=scalar, vector=vector)


H0, D0 = 16, 8
HG = 4
VW = 32


def attention_zero(core, name, ctx, w):
    nc = core.nc
    sb = lambda n, s, d=F32: ctx.enter_context(nc.sbuf_tensor(f"{name}_{n}", s, d))
    ln = LayerNorm(core, ctx, name)
    bank = core.bank
    SCALE = float(1.0 / np.sqrt(D0))
    wqkv = sb("wqkv", [P, 3, P])
    bqkv = sb("bqkv", [P, 3, P])
    bv = sb("bv", [P, 1])
    wl = sb("wl", [P, 3])
    bl = sb("bl", [P, 1])
    cos = sb("cos", [P, 4, D0])
    sin = sb("sin", [P, 4, D0])
    rot = sb("rot", [P, 2, 4, H0, D0 // 2])
    z = sb("z", [P, 2, 4, P])
    e = sb("e", [P, 2, 4, P])
    QT = sb("QT", [P, TOKENS])
    KT = sb("KT", [P, TOKENS])
    V = sb("V", [P, TILES, P])
    vT = sb("vT", [P, BLOCK])
    lT = sb("lT", [P, TOKENS])
    head_mask = sb("head_mask", [P, H0])
    Qz = [sb(f"Qz{i}", [P, H0, SEQ]) for i in range(2)]
    Ks = [sb(f"Ks{i}", [P, SEQ]) for i in range(2)]
    Vs = [sb(f"Vs{i}", [P, 2, H0, VW]) for i in range(2)]
    lTs = [sb(f"lTs{i}", [P, SEQ]) for i in range(2)]
    select = sb("select", [P, H0, P], BF16)
    negmax = sb("negmax", [P, 2, H0])
    parts = sb("parts", [P, 2, P], BF16)
    shift = [sb(f"shift{i}", [P, SEQ], BF16) for i in range(2)]
    PT = sb("PT", [P, 2, HG, SEQ])
    OT = sb("OT", [P, 2, SEQ])
    rden = sb("rden", [P, 2, HG])
    attn = sb("attn", [P, 2, HG, D0])
    loaded = core.sem(f"{name}_loaded")
    filled = core.sem(f"{name}_filled")
    consts = core.sem(f"{name}_consts")
    qkv_done = core.sem(f"{name}_qkv_done")
    qkv_read = core.sem(f"{name}_qkv_read")
    neg_ready = core.sem(f"{name}_neg_ready")
    exp_ready = core.sem(f"{name}_exp_ready")
    rot_ready = core.sem(f"{name}_rot_ready")
    rot_turned = core.sem(f"{name}_rot_turned")
    qkT_ready = core.sem(f"{name}_qkT_ready")
    vT_done = core.sem(f"{name}_vT_done")
    vT_read = core.sem(f"{name}_vT_read")
    v_ready = core.sem(f"{name}_v_ready")
    lT_ready = core.sem(f"{name}_lT_ready")
    chain = core.sem(f"{name}_chain")
    staged = core.sem(f"{name}_staged")
    heads_done = core.sem(f"{name}_heads_done")
    s1_done = core.sem(f"{name}_s1_done")
    max_done = core.sem(f"{name}_max_done")
    parts_ready = core.sem(f"{name}_parts_ready")
    parts_hi = core.sem(f"{name}_parts_hi")
    parts_turned = core.sem(f"{name}_parts_turned")
    shift_ready = core.sem(f"{name}_shift_ready")
    s2_done = core.sem(f"{name}_s2_done")
    p_ready = core.sem(f"{name}_p_ready")
    pv_done = core.sem(f"{name}_pv_done")
    o_ready = core.sem(f"{name}_o_ready")
    o_turned = core.sem(f"{name}_o_turned")
    o_inv = core.sem(f"{name}_o_inv")
    o_scaled = core.sem(f"{name}_o_scaled")
    o_added = core.sem(f"{name}_o_added")
    l_turned = core.sem(f"{name}_l_turned")
    l_added = core.sem(f"{name}_l_added")
    UNITS = 2 * H0 // HG

    def sync(sp):
        sp.dma_start(wqkv[:, :, :], w["w_qkv"]).then_inc(loaded, 16)
        sp.dma_start(bqkv[:, :, :], w["b_qkv"].unsqueeze(0).to_broadcast([P, 3, P])).then_inc(loaded, 16)
        sp.dma_start(bv[:, :], w["b_v"]).then_inc(loaded, 16)
        sp.dma_start(wl[:, :], w["w_lepe"]).then_inc(loaded, 16)
        sp.dma_start(bl[:, :], w["b_lepe"]).then_inc(loaded, 16)
        sp.dma_start(cos[:, :, :], w["rope_cos"]).then_inc(loaded, 16)
        sp.dma_start(sin[:, :, :], w["rope_sin"]).then_inc(loaded, 16)

    def gpsimd(pool):
        pool.memset(head_mask[:, :], 1.0).then_inc(filled, 1)
        pool.memset(select[:, :, :], 0.0).then_inc(filled, 1)
        for i in range(2):
            pool.memset(Vs[i][:, :, :, :], 0.0).then_inc(filled, 1)
        pool.memset(parts[:, :, :], 0.0).then_inc(consts, 1)
        pool.wait_ge(filled, 4)
        for i in range(2):
            pool.memset(Vs[i][:, :, :, D0:D0 + 1], 1.0).then_inc(consts, 1)
        pool.affine_select(out=head_mask[:, :], in_=head_mask[:, :], compare_op=ALU.is_ge, fill=0.0, base=0,
                           pattern=[[-D0, H0]], channel_multiplier=1).then_inc(filled, 1)
        pool.affine_select(out=select[:, :, :], in_=select[:, :, :], compare_op=ALU.not_equal, fill=1.0, base=0,
                           pattern=[[-1, H0], [0, P]], channel_multiplier=1).then_inc(filled, 1)
        pool.wait_ge(filled, 6)
        pool.affine_select(out=head_mask[:, :], in_=head_mask[:, :], compare_op=ALU.is_ge, fill=0.0, base=D0 - 1,
                           pattern=[[D0, H0]], channel_multiplier=-1).then_inc(consts, 1)
        pool.affine_select(out=select[:, :, :], in_=select[:, :, :], compare_op=ALU.not_equal, fill=1.0, base=-H0,
                           pattern=[[-1, H0], [0, P]], channel_multiplier=1).then_inc(consts, 1)
        pool.wait_ge(consts, 5)
        pool.wait_ge(qkT_ready, 8)
        pool.wait_ge(v_ready, 4)
        pool.wait_ge(lT_ready, 4)
        pool.sem_inc(heads_done, 2)
        for b in range(BATCH):
            s = b % 2
            pool.wait_ge(heads_done, b + 1)
            at = b * SEQ
            pool.tensor_copy(Ks[s][:, :], KT[:, at:at + SEQ])
            pool.tensor_copy(lTs[s][:, :], lT[:, at:at + SEQ])
            pool.tensor_copy(Vs[s][:, :, :, 0:D0], V[:, 2 * b:2 * b + 2, :].rearrange("p t (h d) -> p t h d", d=D0))
            for h in range(H0):
                last = pool.tensor_scalar(Qz[s][:, h, :], QT[:, at:at + SEQ], head_mask[:, h:h + 1], None, ALU.mult)
            last.then_inc(staged, 1)

    def scores_by_query(pe, b, s, u):
        g, qt = u // 2, u % 2
        if u == 0:
            pe.wait_ge(staged, b + 1)
        pe.wait_ge(max_done, b * UNITS + (u + 1))
        for j in range(HG):
            last = pe.matmul(bank[j // 2][:, SEQ * (j % 2):SEQ * (j % 2) + SEQ],
                             Qz[s][:, HG * g + j, P * qt:P * qt + P], Ks[s][:, :], start=True, stop=True)
        last.then_inc(s1_done, 1)

    def turn_maxima(pe, b, s):
        pe.wait_ge(parts_ready, b + 2)
        pe.wait_ge(o_added, b * 4 + 1)
        pe.wait_ge(l_added, b + 1)
        for qt in range(2):
            last = pe.transpose(bank[7].bitcast(BF16)[:, P * qt:P * qt + P], parts[:, qt, :], core.identb[:, :])
        last.then_inc(parts_turned, 1)

    def tensor(pe):
        ln.tensor(pe)
        pe.wait_ge(loaded, 7 * 16)
        for q in range(4):
            pe.wait_ge(ln.xnT_ready, q + 1)
            if q:
                pe.wait_ge(qkv_read, q)
            for i in range(3):
                for t in range(4):
                    at = P * (4 * q + t)
                    last = pe.matmul(bank[4 + i][:, P * t:P * t + P], ln.xnT[:, at:at + P], wqkv[:, i, :],
                                     start=True, stop=True)
            last.then_inc(qkv_done, 1)
            if q:
                pe.wait_ge(vT_read, q)
            pe.matmul(bank[7], wqkv[:, 2, :], ln.xnT[:, BLOCK * q:BLOCK * q + BLOCK],
                      start=True, stop=True).then_inc(vT_done, 1)
            pe.wait_ge(rot_ready, q + 1)
            if q == 0:
                pe.wait_ge(ln.xnT_ready, 4)
            else:
                pe.wait_ge(qkT_ready, 2 * q)
            for i in range(2):
                for t in range(4):
                    last = pe.transpose(bank[i][:, P * t:P * t + P], z[:, i, t, :], core.ident[:, :])
                last.then_inc(rot_turned, 1)
        pe.wait_ge(qkT_ready, 8)
        pe.wait_ge(consts, 5)
        pe.wait_ge(vT_read, 4)
        pe.sem_inc(max_done, 1)
        pe.sem_inc(p_ready, 1)
        pe.sem_inc(pv_done, 2)
        pe.sem_inc(o_ready, 1)
        pe.sem_inc(o_added, 1)
        pe.sem_inc(l_added, 1)
        pe.sem_inc(shift_ready, 1)
        for u in range(UNITS):
            scores_by_query(pe, 0, 0, u)

        def values(b, s, u):
            g, kt = u // 2, u % 2
            pe.wait_ge(p_ready, b * UNITS + (u + 2))
            if kt == 0:
                pe.wait_ge(o_ready, b * 4 + (g + 1))
            for j in range(HG):
                last = pe.matmul(bank[6][VW * j:VW * j + VW, 0:SEQ], Vs[s][:, kt, HG * g + j, :],
                                 PT[:, u % 2, j, :], start=(kt == 0), stop=(kt == 1))
            last.then_inc(pv_done, 1)

        def turn_out(b, s, g):
            pe.wait_ge(o_ready, b * 4 + (g + 2))
            pe.wait_ge(o_added, b * 4 + (g + 1))
            if g == 0:
                pe.wait_ge(shift_ready, b + 2)
            for qt in range(2):
                last = pe.transpose(bank[7][:, P * qt:P * qt + P], OT[:, g % 2, P * qt:P * qt + P], core.ident[:, :])
            last.then_inc(o_turned, 1)

        def batch(b, s, following):
            turn_maxima(pe, b, s)
            pe.wait_ge(shift_ready, b + 2)
            for u in range(UNITS):
                g, kt = u // 2, u % 2
                if u % 2 == 0:
                    pe.wait_ge(p_ready, b * UNITS + (u + 1))
                else:
                    pe.wait_ge(p_ready, b * UNITS + u)
                pair = bank[2 + 2 * (u % 2):4 + 2 * (u % 2)]
                for half in range(2):
                    pe.matmul(pair[half], Ks[s][:, P * kt:P * kt + P],
                              Qz[s][:, HG * g + 2 * half:HG * g + 2 * half + 2, :].rearrange("p h n -> p (h n)"),
                              start=True, stop=False, skip_group_check=True)
                    for j in range(2):
                        last = pe.matmul(pair[half][:, SEQ * j:SEQ * j + SEQ], select[:, HG * g + 2 * half + j, :],
                                         shift[s][:, :], start=False, stop=True, skip_group_check=True)
                last.then_inc(s2_done, 1)
                if u:
                    values(b, s, u - 1)
                if u >= 3 and u % 2:
                    turn_out(b, s, (u - 3) // 2)
                if following:
                    scores_by_query(pe, b + 1, 1 - s, u)
            values(b, s, UNITS - 1)
            turn_out(b, s, 3)
            pe.wait_ge(o_added, b * 4 + 5)
            for qt in range(2):
                last = pe.transpose(bank[7][:, P * qt:P * qt + P], lTs[s][:, P * qt:P * qt + P], core.ident[:, :])
            last.then_inc(l_turned, 1)
            pe.wait_ge(l_turned, b + 1)
            pe.sem_inc(heads_done, 1)

        with pe.Fori(0, BATCH // 2 - 1) as bp:
            for s in range(2):
                batch(bp * 2 + s, s, True)
        batch(BATCH - 2, 0, True)
        batch(BATCH - 1, 1, False)

    def scalar(act):
        ln.scalar(act)
        for q in range(4):
            act.wait_ge(neg_ready, q + 1)
            act.activation(e[:, :, :, :], e[:, :, :, :], ACT.Exp).then_inc(exp_ready, 1)
            for i in range(2):
                act.wait_ge(rot_turned, 2 * q + i + 1)
                dst = (QT, KT)[i][:, BLOCK * q:BLOCK * q + BLOCK]
                act.activation(dst, bank[i], ACT.Copy).then_inc(qkT_ready, 1)

        with act.Fori(0, BATCH // 2) as bp:
            for s in range(2):
                b = bp * 2 + s
                for u in range(UNITS):
                    act.wait_ge(s2_done, b * UNITS + (u + 1))
                    act.wait_ge(pv_done, b * UNITS + (u + 1))
                    pair = core.psum[:, 2 + 2 * (u % 2):4 + 2 * (u % 2), :].rearrange("p a (h n) -> p (a h) n", n=SEQ)
                    act.activation(PT[:, u % 2, :, :], pair, ACT.Exp, scale=SCALE).then_inc(p_ready, 1)

    def vector(dve):
        ln.vector(dve)
        c = Chain(chain)

        def step(ins):
            dve.wait_ge(c.sem, c.on(ins))

        dve.wait_ge(loaded, 7 * 16)
        for q in range(4):
            dve.wait_ge(qkv_done, q + 1)
            if q:
                dve.wait_ge(rot_turned, 2 * q)
            qk = core.psum[:, 4:6, :].rearrange("p i (t n) -> p i t n", n=P)
            bias = bqkv[:, 0:2, :].unsqueeze(2).to_broadcast([P, 2, 4, P])
            for i in range(2):
                step(dve.tensor_tensor(z[:, i, :, :], bank[4 + i].rearrange("p (t n) -> p t n", n=P),
                                       bqkv[:, i, :].unsqueeze(1).to_broadcast([P, 4, P]), ALU.add))
            dve.tensor_scalar(e[:, :, :, :], z[:, :, :, :], 0.0, None, ALU.min).then_inc(neg_ready, 1)
            step(dve.tensor_tensor(V[:, 4 * q:4 * q + 4, :], bank[6].rearrange("p (t n) -> p t n", n=P),
                                   bqkv[:, 2, :].unsqueeze(1).to_broadcast([P, 4, P]), ALU.add))
            dve.sem_inc(qkv_read, 1)
            dve.sem_inc(v_ready, 1)
            dve.wait_ge(exp_ready, q + 1)
            step(dve.scalar_tensor_tensor(e[:, :, :, :].rearrange("p i t n -> p (i t n)"),
                                          z[:, :, :, :].rearrange("p i t n -> p (i t n)"), 0.0,
                                          e[:, :, :, :].rearrange("p i t n -> p (i t n)"), ALU.max, ALU.add))
            for i in range(2):
                src = e[:, i, :, :].rearrange("p t (h d) -> p t h d", d=D0)
                dst = z[:, i, :, :].rearrange("p t (h d) -> p t h d", d=D0)
                co = cos[:, :, :].unsqueeze(2).to_broadcast([P, 4, H0, D0])
                si = sin[:, :, :].unsqueeze(2).to_broadcast([P, 4, H0, D0])
                c.on(dve.tensor_tensor(dst, src, co, ALU.mult))
                for o in range(2):
                    c.on(dve.tensor_tensor(rot[:, o, :, :, :], src[:, :, :, 1 - o::2], si[:, :, :, o::2], ALU.mult))
                dve.wait_ge(c.sem, c.n)
                for o in range(2):
                    c.on(dve.tensor_tensor(dst[:, :, :, o::2], dst[:, :, :, o::2], rot[:, o, :, :, :], ALU.add))
                dve.wait_ge(c.sem, c.n)
            dve.sem_inc(rot_ready, 1)
            dve.wait_ge(vT_done, q + 1)
            step(dve.tensor_scalar(vT[:, :], bank[7], bv[:, 0:1], None, ALU.add))
            dve.sem_inc(vT_read, 1)
            lq = lT[:, BLOCK * q:BLOCK * q + BLOCK]
            step(dve.tensor_scalar(lq, vT[:, :], wl[:, 1:2], bl[:, 0:1], ALU.mult, ALU.add))
            l2 = lq.rearrange("p (b n) -> p b n", n=SEQ)
            v2 = vT[:, :].rearrange("p (b n) -> p b n", n=SEQ)
            step(dve.scalar_tensor_tensor(l2[:, :, 1:SEQ], v2[:, :, 0:SEQ - 1], wl[:, 0:1], l2[:, :, 1:SEQ],
                                          ALU.mult, ALU.add))
            step(dve.scalar_tensor_tensor(l2[:, :, 0:SEQ - 1], v2[:, :, 1:SEQ], wl[:, 2:3], l2[:, :, 0:SEQ - 1],
                                          ALU.mult, ALU.add))
            dve.sem_inc(lT_ready, 1)

        def maximum(b, u):
            g, qt = u // 2, u % 2
            dve.wait_ge(s1_done, b * UNITS + (u + 1))
            if u == 0:
                dve.wait_ge(parts_ready, b + 1)
            dve.tensor_reduce(negmax[:, qt, HG * g:HG * g + HG],
                              core.psum[:, 0:2, :].rearrange("p a (h n) -> p (a h) n", n=SEQ), AX.X, ALU.max,
                              negate=True).then_inc(max_done, 1)

        def split_maxima(b, s):
            dve.wait_ge(max_done, b * UNITS + (UNITS + 1))
            dve.wait_ge(parts_turned, b + 1)
            dve.tensor_copy(parts[:, :, 0:H0], negmax[:, :, :]).then_inc(parts_hi, 1)
            dve.wait_ge(parts_hi, b + 1)
            dve.tensor_tensor(parts[:, :, H0:2 * H0], negmax[:, :, :], parts[:, :, 0:H0], ALU.subtract).then_inc(parts_ready, 1)

        def group(b, s, g):
            dve.wait_ge(pv_done, b * UNITS + (2 * g + 4))
            dve.tensor_copy(OT[:, g % 2, :], bank[6][:, 0:SEQ]).then_inc(o_ready, 1)
            dve.wait_ge(o_turned, b * 4 + (g + 1))
            o = bank[7][:, 0:SEQ].rearrange("p (t j v) -> p t j v", t=2, v=VW)
            dve.reciprocal(rden[:, :, :], o[:, :, :, D0]).then_inc(o_inv, 1)
            dve.wait_ge(o_inv, b * 4 + (g + 1))
            dve.tensor_tensor(attn[:, :, :, :], o[:, :, :, 0:D0], bcast(rden[:, :, :], D0), ALU.mult).then_inc(o_scaled, 1)
            dve.wait_ge(o_scaled, b * 4 + (g + 1))
            xg = core.x[:, ds(b * 2, 2), HG * D0 * g:HG * D0 * g + HG * D0]
            dve.tensor_tensor(xg, xg, attn[:, :, :, :].rearrange("p t j d -> p t (j d)"), ALU.add).then_inc(o_added, 1)

        dve.sem_inc(parts_ready, 1)
        dve.sem_inc(parts_turned, 1)
        for u in range(UNITS):
            maximum(0, u)

        def batch(b, s, following):
            split_maxima(b, s)
            dve.wait_ge(parts_turned, b + 2)
            dve.tensor_copy(shift[s][:, :], bank[7].bitcast(BF16)[:, 0:SEQ]).then_inc(shift_ready, 1)
            for u in range(UNITS):
                if u >= 3 and u % 2:
                    group(b, s, (u - 3) // 2)
                if following:
                    maximum(b + 1, u)
            group(b, s, 3)
            dve.wait_ge(l_turned, b + 1)
            dve.wait_ge(o_added, b * 4 + 5)
            xb = core.x[:, ds(b * 2, 2), :]
            dve.tensor_tensor(xb, xb, bank[7][:, 0:SEQ].rearrange("p (t n) -> p t n", n=P), ALU.add).then_inc(l_added, 1)

        with dve.Fori(0, BATCH // 2 - 1) as bp:
            for s in range(2):
                batch(bp * 2 + s, s, True)
        batch(BATCH - 2, 0, True)
        batch(BATCH - 1, 1, False)

    return dict(sync=sync, gpsimd=gpsimd, tensor=tensor, scalar=scalar, vector=vector)


H1, D1, NB1, SPAN = 16, 64, 10, 128
CH = H1 // 2
RH = 8
ZW = 3 * SPAN
MASKED = 1e9


def attention_one(core, name, ctx, w):
    nc = core.nc
    sb = lambda n, s, d=F32: ctx.enter_context(nc.sbuf_tensor(f"{name}_{n}", s, d))
    ln = LayerNorm(core, ctx, name)
    bank = core.bank
    RSCALE = float(D1) ** -0.5
    wq = sb("wq", [P, H1 * D1])
    wk = sb("wk", [P, H1 * D1])
    wv = sb("wv", [P, H1 * D1])
    wp = sb("wp", [P, CH, P])
    wr = sb("wr", [P, H1 * NB1])
    bq = sb("bq", [P, 2, CH])
    br = sb("br", [RH * NB1, 2])
    bp_row = sb("bp_row", [P, P])
    bnd = sb("bnd", [RH * NB1, RH, SPAN])
    pad = sb("pad", [P, SPAN])
    xs = sb("xs", [P, 2, SEQ])
    RT = sb("RT", [RH * NB1, 2, SEQ])
    G = sb("G", [P, 2, H1, SPAN])
    X0 = [sb(f"X0_{i}", [P, H1, SPAN]) for i in range(2)]
    X1 = [sb(f"X1_{i}", [P, H1, 2 * SPAN]) for i in range(2)]
    Qz = [sb(f"Qz{i}", [P, H1, SEQ]) for i in range(2)]
    KT = [sb(f"KT{i}", [P, CH, SEQ]) for i in range(2)]
    V = [sb(f"V{i}", [P, 2, H1 * D1]) for i in range(2)]
    L = sb("L", [P, 2, 3 * P])
    least = sb("least", [P, 2, 2])
    pr = sb("pr", [P, 4, 3 * P])
    sums = sb("sums", [P, 4, 2])
    rinv = sb("rinv", [P, 4, 2])
    PT = sb("PT", [P, 2, 3 * P])
    AT = sb("AT", [P, CH, SEQ])
    z = [[nc.dram_tensor(f"{name}_z{s}{q}", [P * H1 * ZW], F32) for q in range(2)] for s in range(2)]

    loaded = core.sem(f"{name}_loaded")
    bnd_zero = core.sem(f"{name}_bnd_zero")
    q_zero = core.sem(f"{name}_q_zero")
    prep = core.sem(f"{name}_prep")
    pad_filled = core.sem(f"{name}_pad_filled")
    pads_written = core.sem(f"{name}_pads_written")
    xs_ready = core.sem(f"{name}_xs_ready")
    xs_free = core.sem(f"{name}_xs_free")
    piece_done = core.sem(f"{name}_piece_done")
    piece_read = [core.sem(f"{name}_piece_read{i}") for i in range(2)]
    g_by_act = core.sem(f"{name}_g_by_act")
    g_by_dve = core.sem(f"{name}_g_by_dve")
    z_written = core.sem(f"{name}_z_written")
    x_turned = core.sem(f"{name}_x_turned")
    qkv_act = core.sem(f"{name}_qkv_act")
    qkv_dve = core.sem(f"{name}_qkv_dve")
    s_done = core.sem(f"{name}_s_done")
    l_begun = core.sem(f"{name}_l_begun")
    l_ready = core.sem(f"{name}_l_ready")
    p_ready = core.sem(f"{name}_p_ready")
    inv_ready = core.sem(f"{name}_inv_ready")
    pn_ready = core.sem(f"{name}_pn_ready")
    p_turned = core.sem(f"{name}_p_turned")
    pT_ready = core.sem(f"{name}_pT_ready")
    pv_done = core.sem(f"{name}_pv_done")
    aT_ready = core.sem(f"{name}_aT_ready")
    out_done = core.sem(f"{name}_out_done")
    out_added = core.sem(f"{name}_out_added")
    PIECES = 21
    STEPS = H1 + 3
    plan = [[u] for u in range(H1)] + [[16, 17], [18, 19], [20]]

    def kind(k):
        if k == 0:
            return "R", 0
        if k < 9:
            return "G", k - 1
        if k < 17:
            return "QK", k - 9
        return "V", k - 17

    def by_act(k):
        name_, j = kind(k)
        return name_ != "R" and j % 2 == 0

    N_ACT = sum(by_act(k) and kind(k)[0] in ("QK", "V") for k in range(PIECES))
    N_DVE = sum(not by_act(k) and kind(k)[0] in ("QK", "V") for k in range(PIECES))

    def piece_at(bp, s, k):
        return (s + k) % 2, bp * PIECES + (s * PIECES + k) // 2

    def sync(sp):
        sp.dma_start(wr[:, :], w["Wr"]).then_inc(loaded, 16)
        sp.dma_start(wq[:, :], w["Wq"]).then_inc(loaded, 16)
        sp.dma_start(wk[:, :], w["Wk"]).then_inc(loaded, 16)
        sp.dma_start(wv[:, :], w["Wv"]).then_inc(loaded, 16)
        sp.dma_start(wp[:, :, :], w["Wproj"].rearrange("(c p) n -> p c n", p=P)).then_inc(loaded, 16)
        sp.dma_start(bq[:, 0, :], w["bq"]).then_inc(loaded, 16)
        sp.dma_start(br[:, :], w["br"]).then_inc(loaded, 16)
        sp.dma_start(bp_row[:, :], w["bproj"].unsqueeze(0).to_broadcast([P, P])).then_inc(loaded, 16)
        sp.wait_ge(bnd_zero, 1)
        for h in range(RH):
            sp.dma_start(bnd[NB1 * h:NB1 * h + NB1, h, :], w["b_nd"]).then_inc(loaded, 16)
        sp.wait_ge(pad_filled, 1)
        for s in range(2):
            for q in range(2):
                rows = z[s][q].ap().rearrange("(p h n) -> p h n", h=H1, n=ZW)
                for side in (0, 2 * SPAN):
                    sp.dma_start(rows[:, :, side:side + SPAN],
                                 pad[:, :].unsqueeze(1).to_broadcast([P, H1, SPAN])).then_inc(pads_written, 16)
        sp.wait_ge(pads_written, 8 * 16)
        sp.sem_inc(z_written, 32)
        sp.sem_inc(x_turned, 64)
        for b in range(BATCH):
            s = b % 2
            sp.wait_ge(x_turned, 32 * (b + 1))
            if b >= 2:
                sp.wait_ge(l_ready, H1 * (b - 1) + 2)
            for q in range(2):
                sp.wait_ge(g_by_act, 4 * b + 2 * (q + 1))
                sp.wait_ge(g_by_dve, 4 * b + 2 * (q + 1))
                rows = z[s][q].ap().rearrange("(p h n) -> p h n", h=H1, n=ZW)
                sp.dma_start(rows[:, :, SPAN:2 * SPAN], G[:, q, :, :]).then_inc(z_written, 16)
                sp.wait_ge(z_written, 32 * (b + 1) + 16 * (q + 1))
                turned = bass.AP(z[s][q], 2 * SPAN - 1 - SPAN * q, [[H1 * ZW - 1, P], [ZW, H1], [1, SPAN * (q + 1)]])
                sp.dma_start((X0, X1)[q][s][:, :, :], turned).then_inc(x_turned, 16)
        sp.wait_ge(x_turned, 32 * (BATCH + 2))

    def gpsimd(pool):
        pool.memset(bnd[:, :, :], 0.0).then_inc(bnd_zero, 1)
        pool.memset(pad[:, :], MASKED).then_inc(pad_filled, 1)
        for s in range(2):
            pool.memset(Qz[s][:, :, :], 0.0).then_inc(q_zero, 1)
        pool.wait_ge(ln.xnT_ready, 4)
        pool.sem_inc(xs_free, 2)
        for b in range(BATCH):
            pool.wait_ge(xs_free, b + 1)
            pool.tensor_copy(xs[:, b % 2, :], ln.xnT[:, SEQ * b:SEQ * b + SEQ]).then_inc(xs_ready, 1)

    def tensor(pe):
        ln.tensor(pe)
        pe.wait_ge(loaded, 16 * 16)
        pe.wait_ge(ln.xnT_ready, 4)
        pe.sem_inc(piece_read[0], 1)
        pe.sem_inc(piece_read[1], 1)

        def piece(bp, s, k):
            which, j = kind(k)
            i, used = piece_at(bp, s, k)
            out = bank[5 + i]
            b = bp * 2 + s
            if k == 0:
                pe.wait_ge(xs_ready, b + 1)
            if k == 1:
                pe.wait_ge(piece_read[s % 2], bp * PIECES + (s * PIECES) // 2 + 2)
            pe.wait_ge(piece_read[i], used + 1)
            if which == "R":
                for c in range(2):
                    last = pe.matmul(out[0:RH * NB1, SEQ * c:SEQ * c + SEQ], wr[:, RH * NB1 * c:RH * NB1 * (c + 1)],
                                     xs[:, s, :], start=True, stop=True)
            elif which == "G":
                q, c, half = j // 4, (j % 4) // 2, j % 2
                last = pe.matmul(out, RT[:, c, P * q:P * q + P],
                                 bnd[:, 4 * half:4 * half + 4, :].rearrange("p h n -> p (h n)"), start=True, stop=True)
            elif which == "QK":
                for a, m in enumerate((wq, wk)):
                    last = pe.matmul(out[:, SEQ * a:SEQ * a + SEQ], m[:, P * j:P * j + P], xs[:, s, :],
                                     start=True, stop=True)
            else:
                t, half = j // 2, j % 2
                last = pe.matmul(out, xs[:, s, P * t:P * t + P], wv[:, 512 * half:512 * half + 512],
                                 start=True, stop=True)
            last.then_inc(piece_done, 1)
            if k == PIECES - 1:
                pe.wait_ge(piece_done, b * PIECES + PIECES)
                pe.sem_inc(xs_free, 1)

        def scores(b, s, h):
            pe.wait_ge(l_ready, b * H1 + (h + 1))
            S = bank[h % 2]
            pe.matmul(S[:, 0:P], Qz[s][:, h, 0:P], KT[s][:, h // 2, 0:P], start=True, stop=True)
            pe.matmul(S[:, P:3 * P], Qz[s][:, h, P:2 * P], KT[s][:, h // 2, :], start=True, stop=True).then_inc(s_done, 1)

        def turn(b, h):
            pe.wait_ge(pn_ready, b * H1 + (h + 1))
            pe.wait_ge(pT_ready, b * H1 + (h + 1))
            for i in range(3):
                last = pe.transpose(bank[2 + h % 2][:, P * i:P * i + P], pr[:, h % 4, P * i:P * i + P],
                                    core.ident[:, :])
            last.then_inc(p_turned, 1)

        def values(b, s, h):
            c, half = h // 2, h % 2
            pe.wait_ge(pT_ready, b * H1 + (h + 3))
            if half == 0:
                pe.wait_ge(aT_ready, b * CH + (c + 1))
                if c == 0:
                    pe.wait_ge(out_added, b + 1)
            o = bank[4 + 3 * (c % 2)][D1 * half:D1 * half + D1, 0:SEQ]
            vh = V[s][:, :, D1 * h:D1 * h + D1]
            pe.matmul(o, vh[:, 0, :], PT[:, h % 2, 0:SEQ], start=True, stop=False, skip_group_check=True)
            pe.matmul(o[:, P:2 * P], vh[:, 1, :], PT[:, h % 2, SEQ:SEQ + P], start=False, stop=True,
                      skip_group_check=True).then_inc(pv_done, 1)

        def batch(bp, s, following):
            b = bp * 2 + s
            nbp, ns = (bp, 1) if s == 0 else (bp + 1, 0)
            for u in range(STEPS):
                if u == 0:
                    pe.wait_ge(qkv_act, b * N_ACT + N_ACT)
                    pe.wait_ge(qkv_dve, b * N_DVE + N_DVE)
                if u < H1:
                    scores(b, s, u)
                if 2 <= u < H1 + 2:
                    turn(b, u - 2)
                if u >= 3:
                    values(b, s, u - 3)
                if following:
                    for k in plan[u]:
                        piece(nbp, ns, k)
            pe.wait_ge(aT_ready, b * CH + (CH + 2))
            for q in range(2):
                for c in range(CH):
                    last = pe.matmul(bank[4][:, P * q:P * q + P], AT[:, c, P * q:P * q + P], wp[:, c, :],
                                     start=(c == 0), stop=(c == CH - 1))
            last.then_inc(out_done, 1)

        pe.wait_ge(q_zero, 2)
        for k in range(PIECES):
            piece(0, 0, k)
        pe.sem_inc(pv_done, 2)
        pe.sem_inc(p_turned, 4)
        pe.sem_inc(out_done, 1)
        with pe.Fori(0, BATCH // 2 - 1) as bp:
            for s in range(2):
                batch(bp, s, True)
        batch(BATCH // 2 - 1, 0, True)
        batch(BATCH // 2 - 1, 1, False)

    def store_piece(eng, is_act, bp, s, k):
        which, j = kind(k)
        i, _ = piece_at(bp, s, k)
        out = bank[5 + i]
        b = bp * 2 + s
        eng.wait_ge(piece_done, b * PIECES + (k + 1))
        if which == "R":
            for c in range(2):
                last = eng.tensor_scalar(RT[:, c, :], out[0:RH * NB1, SEQ * c:SEQ * c + SEQ], br[:, c:c + 1], -1.0,
                                         ALU.add, ALU.mult)
            return last
        if which == "G":
            q, c, half = j // 4, (j % 4) // 2, j % 2
            if j % 4 < 2:
                eng.wait_ge(z_written, b * 32 + 16 * (q + 1))
            dst = G[:, q, RH * c + 4 * half:RH * c + 4 * half + 4, :]
            src = out.rearrange("p (h n) -> p h n", n=SPAN)
        elif which == "QK":
            qa = out[0:D1, 0:SEQ], Qz[s][0:D1, 2 * j, :], bq[0:D1, :, j:j + 1]
            qb = out[D1:P, 0:SEQ], Qz[s][D1:P, 2 * j + 1, :], bq[D1:P, :, j:j + 1]
            for src, dst, bias in (qa, qb):
                if is_act:
                    eng.activation(dst, src, ACT.Identity, bias=bias[:, 1, :], scale=-RSCALE)
                else:
                    eng.tensor_scalar(dst, src, bias[:, 0, :], -RSCALE, ALU.add, ALU.mult)
            dst, src = KT[s][:, j, :], out[:, SEQ:2 * SEQ]
        else:
            t, half = j // 2, j % 2
            dst, src = V[s][:, t, 512 * half:512 * half + 512], out
        return eng.activation(dst, src, ACT.Copy) if is_act else eng.tensor_copy(dst, src)

    def stored(eng, is_act, bp, s, k, counts):
        which, _ = kind(k)
        i, _ = piece_at(bp, s, k)
        last = store_piece(eng, is_act, bp, s, k)
        last.then_inc(piece_read[i], 1)
        if which != "R":
            done = {("G", True): g_by_act, ("G", False): g_by_dve}.get((which, is_act), qkv_act if is_act else qkv_dve)
            eng.wait_ge(piece_read[i], piece_at(bp, s, k)[1] + 2)
            eng.sem_inc(done, 1)

    def scalar(act):
        ln.scalar(act)
        act.wait_ge(prep, 2)
        act.wait_ge(q_zero, 2)

        def pieces(bp, s, ks):
            for k in ks:
                if by_act(k):
                    stored(act, True, bp, s, k, None)

        def probabilities(b, h):
            act.wait_ge(l_ready, b * H1 + (h + 3))
            act.wait_ge(p_turned, b * H1 + (h + 1))
            act.activation(pr[:, h % 4, 0:P], L[:, h % 2, 0:P], ACT.Exp, bias=least[:, h % 2, 0:1], scale=-1.0,
                           accum_out=sums[:, h % 4, 0:1])
            act.activation(pr[:, h % 4, P:3 * P], L[:, h % 2, P:3 * P], ACT.Exp, bias=least[:, h % 2, 1:2], scale=-1.0,
                           accum_out=sums[:, h % 4, 1:2]).then_inc(p_ready, 1)

        def batch(bp, s, following):
            b = bp * 2 + s
            nbp, ns = (bp, 1) if s == 0 else (bp + 1, 0)
            for u in range(STEPS + 1):
                if u < H1:
                    probabilities(b, u)
                if 2 <= u < H1 + 2:
                    h = u - 2
                    act.wait_ge(p_turned, b * H1 + (h + 5))
                    act.wait_ge(pv_done, b * H1 + (h + 1))
                    act.activation(PT[:, h % 2, :], bank[2 + h % 2][:, 0:3 * P], ACT.Copy).then_inc(pT_ready, 1)
                if u >= 5 and u % 2:
                    c = (u - 5) // 2
                    act.wait_ge(pv_done, b * H1 + (2 * c + 4))
                    act.wait_ge(out_done, b + 1)
                    act.activation(AT[:, c, :], bank[4 + 3 * (c % 2)][:, 0:SEQ], ACT.Copy).then_inc(aT_ready, 1)
                if following and u < STEPS:
                    pieces(nbp, ns, plan[u])

        act.sem_inc(pT_ready, 2)
        act.sem_inc(aT_ready, 2)
        pieces(0, 0, range(PIECES))
        with act.Fori(0, BATCH // 2 - 1) as bp:
            for s in range(2):
                batch(bp, s, True)
        batch(BATCH // 2 - 1, 0, True)
        batch(BATCH // 2 - 1, 1, False)

    def vector(dve):
        ln.vector(dve)
        dve.wait_ge(loaded, 16 * 16)
        dve.tensor_scalar(bq[:, 1, :], bq[:, 0, :], -RSCALE, None, ALU.mult).then_inc(prep, 1)
        dve.wait_ge(q_zero, 2)
        dve.tensor_tensor(core.x[:, :, :], core.x[:, :, :],
                          bp_row[:, :].unsqueeze(1).to_broadcast([P, TILES, P]), ALU.add).then_inc(prep, 1)
        dve.wait_ge(prep, 2)

        def pieces(bp, s, ks):
            for k in ks:
                if not by_act(k):
                    stored(dve, False, bp, s, k, None)

        def logits(b, s, h):
            dve.wait_ge(s_done, b * H1 + (h + 1))
            dve.wait_ge(p_ready, b * H1 + (h + 1))
            if h == 0:
                dve.wait_ge(x_turned, b * 32 + 96)
            dve.sem_inc(l_begun, 1)
            S = bank[h % 2]
            dve.tensor_tensor_reduce(L[:, h % 2, 0:P], S[:, 0:P], X0[s][:, h, :], 1.0, 3.0e38, ALU.add, ALU.min,
                                     least[:, h % 2, 0:1])
            dve.tensor_tensor_reduce(L[:, h % 2, P:3 * P], S[:, P:3 * P], X1[s][:, h, :], 1.0, 3.0e38, ALU.add, ALU.min,
                                     least[:, h % 2, 1:2]).then_inc(l_ready, 1)

        def normalise(b, h):
            dve.wait_ge(p_ready, b * H1 + (h + 3))
            dve.reciprocal(rinv[:, h % 4, :], sums[:, h % 4, :]).then_inc(inv_ready, 1)
            dve.wait_ge(inv_ready, b * H1 + (h + 1))
            dve.tensor_scalar(pr[:, h % 4, 0:P], pr[:, h % 4, 0:P], rinv[:, h % 4, 0:1], None, ALU.mult)
            dve.tensor_scalar(pr[:, h % 4, P:3 * P], pr[:, h % 4, P:3 * P], rinv[:, h % 4, 1:2], None,
                              ALU.mult).then_inc(pn_ready, 1)

        def batch(bp, s, following):
            b = bp * 2 + s
            nbp, ns = (bp, 1) if s == 0 else (bp + 1, 0)
            for u in range(STEPS):
                if u < H1:
                    logits(b, s, u)
                if 1 <= u < H1 + 1:
                    normalise(b, u - 1)
                if following:
                    pieces(nbp, ns, plan[u])
            dve.wait_ge(out_done, b + 2)
            xb = core.x[:, ds(b * 2, 2), :]
            dve.tensor_tensor(xb, xb, bank[4][:, 0:SEQ].rearrange("p (t n) -> p t n", n=P), ALU.add).then_inc(out_added, 1)

        dve.sem_inc(l_ready, 2)
        dve.sem_inc(p_ready, 2)
        dve.sem_inc(out_added, 1)
        pieces(0, 0, range(PIECES))
        with dve.Fori(0, BATCH // 2 - 1) as bp:
            for s in range(2):
                batch(bp, s, True)
        batch(BATCH // 2 - 1, 0, True)
        batch(BATCH // 2 - 1, 1, False)

    return dict(sync=sync, gpsimd=gpsimd, tensor=tensor, scalar=scalar, vector=vector)


def build(nc, w, out, stages):
    with ExitStack() as ctx:
        core = Core(nc, ctx)
        make_constants = constants(core, "c")
        x_loaded = core.sem("x_loaded")
        stored = core.sem("stored")
        stage_done = core.sem("stage_done")
        stage_cleared = core.sem("stage_cleared")
        made, sems = [], []
        for name, make in stages:
            with ExitStack() as local:
                core.ctx, core.stage_sems = local, []
                made.append(make(core, name, local, w))
                sems.append(core.stage_sems)
        block = ctx.enter_context(nc.Block())
        x_dram = w["x"].rearrange("(t p) d -> p t d", p=P)
        out_dram = out.rearrange("(t p) d -> p t d", p=P)

        def stage_end(eng, n):
            eng.drain().then_inc(stage_done, 1)
            if eng is nc.sync:
                eng.wait_ge(stage_done, 5 * (n + 1))
                for s in sems[n]:
                    eng.sem_clear(s)
                eng.sem_inc(stage_cleared, 1)
            eng.wait_ge(stage_cleared, n + 1)

        @block.sync
        def _(sp):
            sp.dma_start(core.x[:, :, :], x_dram).then_inc(x_loaded, 16)
            for n, st in enumerate(made):
                st["sync"](sp)
                stage_end(sp, n)
            sp.dma_start(out_dram, core.x[:, :, :]).then_inc(stored, 16)
            sp.wait_ge(stored, 16)

        @block.gpsimd
        def _(pool):
            make_constants(pool)
            for n, st in enumerate(made):
                st["gpsimd"](pool)
                stage_end(pool, n)

        @block.tensor
        def _(pe):
            pe.wait_ge(core.const_ready, 4)
            for n, st in enumerate(made):
                st["tensor"](pe)
                stage_end(pe, n)

        @block.scalar
        def _(act):
            for n, st in enumerate(made):
                st["scalar"](act)
                stage_end(act, n)

        @block.vector
        def _(dve):
            dve.wait_ge(x_loaded, 16)
            for n, st in enumerate(made):
                st["vector"](dve)
                stage_end(dve, n)


STAGES = [
    ("f0", mixture_zero), ("a0", attention_zero), ("g0", mixture_zero),
    ("f1", mixture_one), ("a1", attention_one), ("g1", mixture_one),
]


def rotary_tables():
    position = np.arange(SEQ, dtype=np.float32)[:, None]
    step = np.exp(np.arange(0, D0, 2, dtype=np.float32) * np.float32(-np.log(10000.0) / D0))
    angle = (position * step).astype(np.float32)
    sign = np.array([-1.0, 1.0] * (D0 // 2), np.float32)
    cos = np.repeat(np.cos(angle), 2, axis=1).astype(np.float32)
    sin = (np.repeat(np.sin(angle), 2, axis=1) * sign).astype(np.float32)
    lay = lambda a: np.ascontiguousarray(np.concatenate([a.reshape(2, P, D0).transpose(1, 0, 2)] * 2, axis=1))
    return lay(cos), lay(sin)


def kernel(**inputs):
    import concourse.bacc as bacc
    from concourse.bass_utils import run_bass_kernel_spmd

    i = {k: np.asarray(v) for k, v in inputs.items()}
    m, a = "L0_ffn_", "L1_attn_"
    cos, sin = rotary_tables()
    laid = {
        "x": i["L0_attn_x"].reshape(TOKENS, P),
        "router": i[m + "router_w"].T, "ws_gate_up": i[m + "ws_gate_up"], "ws_down": i[m + "ws_down"],
        "gate_up": np.concatenate([i[m + "w_gate"], i[m + "w_up"]], axis=2).transpose(1, 0, 2),
        "down": i[m + "w_down"].transpose(1, 0, 2),
        "w_qkv": i["L0_attn_w_qkv"].T.reshape(P, 3, P), "b_qkv": i["L0_attn_b_qkv"].reshape(3, P),
        "b_v": i["L0_attn_b_qkv"][2 * P:].reshape(P, 1), "w_lepe": i["L0_attn_w_lepe"].reshape(P, 3),
        "b_lepe": i["L0_attn_b_lepe"].reshape(P, 1), "rope_cos": cos, "rope_sin": sin,
        "Wg": i["L1_ffn_Wg"], "bg": i["L1_ffn_bg"], "W1": i["L1_ffn_W1"], "W2": i["L1_ffn_W2"], "b2": i["L1_ffn_b2"],
        "b1": i["L1_ffn_b1"].reshape(E1, FC1, P).transpose(2, 0, 1),
        "Wq": i[a + "Wq"], "Wk": i[a + "Wk"], "Wv": i[a + "Wv"], "Wproj": i[a + "Wproj"], "Wr": i[a + "Wr"],
        "bq": i[a + "bq"].reshape(CH, P).T, "br": i[a + "br"].reshape(2, RH * NB1).T, "bproj": i[a + "bproj"],
        "b_nd": i[a + "b_nd"][:, ::-1],
    }
    nc = bacc.Bacc("TRN2", target_bir_lowering=False, num_devices=1)
    arrays, w = {}, {}
    for name, value in laid.items():
        arrays[f"in_{name}"] = np.ascontiguousarray(value)
        w[name] = nc.dram_tensor(f"in_{name}", value.shape, F32, kind="ExternalInput").ap()
    out = nc.dram_tensor("out", (TOKENS, P), F32, kind="ExternalOutput").ap()
    build(nc, w, out, STAGES)
    r = run_bass_kernel_spmd(nc, [arrays], core_ids=[0])
    return r.results[0]["out"].reshape(BATCH, SEQ, P)
```

```python
from contextlib import ExitStack

import numpy as np
import concourse.bass as bass
from concourse import mybir

F32 = mybir.dt.float32
BF16 = mybir.dt.bfloat16
I32 = mybir.dt.int32
ALU = mybir.AluOpType
ACT = mybir.ActivationFunctionType
AX = mybir.AxisListType
ds = bass.ds

P = 128
BATCH = 8
SEQ = 256
TOKENS = BATCH * SEQ
TILES = TOKENS // P
BLOCK = 512
EPS = 1e-5

E0, TOP0, F0, CAPACITY = 64, 8, 96, 64
E1, F1 = 8, 512
FC1 = F1 // P


class Chain:

    def __init__(self, sem, start=0):
        self.sem, self.n = sem, start

    def on(self, ins):
        self.n += 1
        ins.then_inc(self.sem, 1)
        return self.n


class Core:

    def __init__(self, nc, ctx):
        self.nc, self.ctx = nc, ctx
        self.stage_sems = []

    def sem(self, name):
        s = self.ctx.enter_context(self.nc.semaphore(name))
        self.stage_sems.append(s)
        return s


def bcast(ap, n):
    return ap.unsqueeze(len(ap.shape)).to_broadcast(list(ap.shape) + [n])


def constants(core):
    nc, ctx = core.nc, core.ctx
    core.x = ctx.enter_context(nc.sbuf_tensor("x", [P, TILES, P], F32))
    core.ident = ctx.enter_context(nc.sbuf_tensor("ident", [P, P], F32))
    core.identb = ctx.enter_context(nc.sbuf_tensor("identb", [P, P], BF16))
    core.tri = ctx.enter_context(nc.sbuf_tensor("tri", [P, P], BF16))
    core.ones = ctx.enter_context(nc.sbuf_tensor("ones", [P, P], BF16))
    core.psum = ctx.enter_context(nc.psum_tensor("psum", [P, 8, 512], F32))
    core.bank = [core.psum[:, i, :] for i in range(8)]
    core.const_filled = core.sem("const_filled")
    core.const_ready = core.sem("const_ready")

    def pool(eng):
        eng.memset(core.ident[:, :], 0.0).then_inc(core.const_filled, 1)
        eng.memset(core.identb[:, :], 0.0).then_inc(core.const_filled, 1)
        eng.memset(core.tri[:, :], 1.0).then_inc(core.const_filled, 1)
        eng.memset(core.ones[:, :], 1.0).then_inc(core.const_ready, 1)
        eng.wait_ge(core.const_filled, 3)
        for m in (core.ident, core.identb):
            eng.affine_select(out=m[:, :], in_=m[:, :], compare_op=ALU.not_equal, fill=1.0,
                              base=0, pattern=[[-1, P]], channel_multiplier=1).then_inc(core.const_ready, 1)
        eng.affine_select(out=core.tri[:, :], in_=core.tri[:, :], compare_op=ALU.is_ge, fill=0.0,
                          base=0, pattern=[[1, P]], channel_multiplier=-1).then_inc(core.const_ready, 1)

    return pool


class LayerNorm:

    def __init__(self, core, ctx, name):
        nc = core.nc
        self.core = core
        sb = lambda n, s, d=F32: ctx.enter_context(nc.sbuf_tensor(f"{name}_{n}", s, d))
        self.xn = sb("xn", [P, TILES, P])
        self.xnT = sb("xnT", [P, TOKENS])
        self.moments = sb("moments", [P, TILES, 6])
        self.mean_var = sb("mean_var", [P, TILES, 2])
        self.ve = sb("ve", [P, TILES])
        self.std = sb("std", [P, TILES])
        self.rstd = sb("rstd", [P, TILES])
        self.newton = sb("newton", [P, TILES])
        self.ps = core.bank[0:4]
        self.chain = core.sem(f"{name}_ln_chain")
        self.var_ready = core.sem(f"{name}_var_ready")
        self.std_ready = core.sem(f"{name}_std_ready")
        self.xn_ready = core.sem(f"{name}_xn_ready")
        self.turned = core.sem(f"{name}_turned")
        self.xnT_ready = core.sem(f"{name}_xnT_ready")

    def vector(self, dve):
        c = Chain(self.chain)

        def step(ins):
            dve.wait_ge(c.sem, c.on(ins))

        x = self.core.x
        for t in range(TILES):
            last = dve.bn_stats(self.moments[:, t, :], x[:, t, :])
        step(last)
        for t in range(TILES):
            last = dve.bn_aggr(self.mean_var[:, t, :], self.moments[:, t, :])
        step(last)
        ve, rstd, t = self.ve[:, :], self.rstd[:, :], self.newton[:, :]
        dve.tensor_scalar(ve, self.mean_var[:, :, 1], EPS, None, ALU.add).then_inc(self.var_ready, 1)
        dve.wait_ge(self.std_ready, 1)
        step(dve.reciprocal(rstd, self.std[:, :]))
        step(dve.tensor_tensor(t, rstd, rstd, ALU.mult))
        step(dve.tensor_tensor(t, t, ve, ALU.mult))
        step(dve.tensor_scalar(t, t, -0.5, 1.5, ALU.mult, ALU.add))
        step(dve.tensor_tensor(rstd, rstd, t, ALU.mult))
        for t in range(TILES):
            dve.tensor_scalar(self.xn[:, t, :], x[:, t, :], self.mean_var[:, t, 0:1], self.rstd[:, t:t + 1],
                              ALU.subtract, ALU.mult).then_inc(self.xn_ready, 1)

    def tensor(self, pe):
        for t in range(TILES):
            pe.wait_ge(self.xn_ready, t + 1)
            last = pe.transpose(self.ps[t // 4][:, P * (t % 4):P * (t % 4) + P], self.xn[:, t, :],
                                self.core.ident[:, :])
            if t % 4 == 3:
                last.then_inc(self.turned, 1)

    def scalar(self, act):
        act.wait_ge(self.var_ready, 1)
        act.activation(self.std[:, :], self.ve[:, :], ACT.Sqrt).then_inc(self.std_ready, 1)
        for q in range(4):
            act.wait_ge(self.turned, q + 1)
            act.activation(self.xnT[:, 512 * q:512 * q + 512], self.ps[q][:, :], ACT.Copy).then_inc(self.xnT_ready, 1)


def mixture_one(core, name, ctx, w):
    nc = core.nc
    sb = lambda n, s, d=F32: ctx.enter_context(nc.sbuf_tensor(f"{name}_{n}", s, d))
    ln = LayerNorm(core, ctx, name)
    wg = sb("wg", [P, E1])
    bg = sb("bg", [P, E1])
    w1 = sb("w1", [P, E1, F1])
    w2 = sb("w2", [P, E1, FC1, P])
    b1 = sb("b1", [P, E1, FC1])
    b2 = sb("b2", [E1, P])
    logit = sb("logit", [P, TILES, E1])
    prob = sb("prob", [P, TILES, E1])
    weight = sb("weight", [P, TILES, E1])
    cmp = sb("cmp", [P, TILES, E1, E1])
    eqs = sb("eqs", [P, TILES, E1, E1])
    lower = sb("lower", [P, E1, E1])
    col = sb("col", [P, 3, TILES])
    wT = sb("wT", [E1, TILES, P])
    hT = sb("hT", [P, 2, FC1, BLOCK])
    prod = sb("prod", [P, 4, P])
    ps_h = core.bank[4:6]
    ps_y = [b.rearrange("p (t n) -> p t n", n=P) for b in core.bank[6:8]]
    ps_logit = ps_y[0]
    loaded = core.sem(f"{name}_loaded")
    w_loaded = core.sem(f"{name}_w_loaded")
    lower_filled = core.sem(f"{name}_lower_filled")
    logits_done = core.sem(f"{name}_logits_done")
    shifted = core.sem(f"{name}_shifted")
    exp_done = core.sem(f"{name}_exp_done")
    weights_ready = core.sem(f"{name}_weights_ready")
    chain = core.sem(f"{name}_chain")
    wT_turned = core.sem(f"{name}_wT_turned")
    wT_ready = core.sem(f"{name}_wT_ready")
    bias_done = core.sem(f"{name}_bias_done")
    bias_added = core.sem(f"{name}_bias_added")
    h_done = core.sem(f"{name}_h_done")
    h_ready = core.sem(f"{name}_h_ready")
    y_done = core.sem(f"{name}_y_done")
    y_read = core.sem(f"{name}_y_read")
    y_added = core.sem(f"{name}_y_added")
    NB = TOKENS // BLOCK

    def sync(sp):
        sp.dma_start(wg[:, :], w["Wg"]).then_inc(loaded, 16)
        sp.dma_start(bg[:, :], w["bg"].unsqueeze(0).to_broadcast([P, E1])).then_inc(loaded, 16)
        sp.dma_start(b2[:, :], w["b2"]).then_inc(loaded, 16)
        sp.dma_start(b1[:, :, :], w["b1"]).then_inc(loaded, 16)
        for e in range(E1):
            sp.dma_start(w1[:, e, :], w["W1"][e]).then_inc(w_loaded, 16)
            sp.dma_start(w2[:, e, :, :], w["W2"][e].rearrange("(c p) d -> p c d", p=P)).then_inc(w_loaded, 16)

    def gpsimd(pool):
        pool.memset(lower[:, :, :], 1.0).then_inc(lower_filled, 1)
        pool.wait_ge(lower_filled, 1)
        pool.affine_select(out=lower[:, :, :], in_=lower[:, :, :], compare_op=ALU.is_gt, fill=0.0,
                           base=0, pattern=[[1, E1], [-1, E1]], channel_multiplier=0).then_inc(lower_filled, 1)

    def tensor(pe):
        ln.tensor(pe)
        pe.wait_ge(loaded, 64)
        for q in range(4):
            pe.wait_ge(ln.xnT_ready, q + 1)
            for i in range(4 * q, 4 * q + 4):
                last = pe.matmul(ps_logit[:, i // 4, E1 * (i % 4):E1 * (i % 4) + E1], ln.xnT[:, P * i:P * i + P],
                                 wg[:, :], start=True, stop=True)
        last.then_inc(logits_done, 1)
        pe.wait_ge(w_loaded, 32 * E1)
        pe.sem_inc(y_done, 2)
        with pe.Fori(0, NB) as b:
            moving = ln.xnT[:, ds(b * BLOCK, BLOCK)]

            def hidden(e):
                for c in range(FC1):
                    pe.wait_ge(h_ready, b * (E1 * FC1) + (e * FC1 + c + 1))
                    pe.matmul(ps_h[c % 2][:, :], w1[:, e, P * c:P * c + P], moving,
                              start=True, stop=True).then_inc(h_done, 1)

            hidden(0)
            for e in range(E1):
                if e + 1 < E1:
                    hidden(e + 1)
                pe.wait_ge(h_ready, b * (E1 * FC1) + (e * FC1 + FC1 + 2))
                pe.wait_ge(y_read, b * E1 + (e + 1))
                for t in range(4):
                    for c in range(FC1):
                        last = pe.matmul(ps_y[e % 2][:, t, :], hT[:, e % 2, c, P * t:P * t + P], w2[:, e, c, :],
                                         start=(c == 0), stop=(c == FC1 - 1))
                last.then_inc(y_done, 1)
        pe.wait_ge(weights_ready, 1)
        for q in range(4):
            for i in range(4):
                last = pe.transpose(ln.ps[q][0:E1, P * i:P * i + P], weight[:, 4 * q + i, :], core.ident[:, :])
            last.then_inc(wT_turned, 1)
        for q in range(4):
            pe.wait_ge(wT_ready, q + 1)
            for i in range(4):
                last = pe.matmul(ln.ps[q][:, P * i:P * i + P], wT[:, 4 * q + i, :], b2[:, :], start=True, stop=True)
            last.then_inc(bias_done, 1)

    def scalar(act):
        ln.scalar(act)
        act.wait_ge(shifted, 1)
        act.activation(prob[:, :, :], logit[:, :, :], ACT.Exp).then_inc(exp_done, 1)
        act.sem_inc(h_ready, 2)
        with act.Fori(0, NB) as b:
            for e in range(E1):
                act.wait_ge(y_done, b * E1 + (e + 1))
                for c in range(FC1):
                    act.wait_ge(h_done, b * (E1 * FC1) + (e * FC1 + c + 1))
                    act.activation(hT[:, e % 2, c, :], ps_h[c % 2][:, :], ACT.Relu,
                                   bias=b1[:, e, c:c + 1]).then_inc(h_ready, 1)
        for q in range(4):
            act.wait_ge(wT_turned, q + 1)
            act.activation(wT[:, 4 * q:4 * q + 4, :], ln.ps[q][0:E1, :].rearrange("p (t n) -> p t n", t=4),
                           ACT.Copy).then_inc(wT_ready, 1)

    def vector(dve):
        ln.vector(dve)
        c = Chain(chain)

        def step(ins):
            dve.wait_ge(c.sem, c.on(ins))

        total, den, top = (col[:, i, :] for i in range(3))
        dve.wait_ge(logits_done, 1)
        step(dve.tensor_tensor(logit[:, :, :].rearrange("p (a b) e -> p a b e", b=4),
                               ps_logit[:, :, 0:4 * E1].rearrange("p a (b e) -> p a b e", b=4),
                               bg[:, :].unsqueeze(1).unsqueeze(1).to_broadcast([P, 4, 4, E1]), ALU.add))
        step(dve.tensor_reduce(total, logit[:, :, :], AX.X, ALU.max))
        dve.tensor_tensor(logit[:, :, :], logit[:, :, :], bcast(total, E1), ALU.subtract).then_inc(shifted, 1)
        dve.wait_ge(exp_done, 1)
        step(dve.tensor_reduce(total, prob[:, :, :], AX.X, ALU.add))
        step(dve.reciprocal(den, total))
        step(dve.tensor_tensor(prob[:, :, :], prob[:, :, :], bcast(den, E1), ALU.mult))
        mine = bcast(prob[:, :, :], E1)
        others = prob[:, :, :].unsqueeze(2).to_broadcast([P, TILES, E1, E1])
        step(dve.tensor_tensor(cmp[:, :, :, :], others, mine, ALU.is_gt))
        step(dve.tensor_tensor(eqs[:, :, :, :], others, mine, ALU.is_equal))
        dve.wait_ge(lower_filled, 2)
        step(dve.tensor_tensor(eqs[:, :, :, :], eqs[:, :, :, :],
                               lower[:, :, :].unsqueeze(1).to_broadcast([P, TILES, E1, E1]), ALU.mult))
        step(dve.tensor_tensor(cmp[:, :, :, :], cmp[:, :, :, :], eqs[:, :, :, :], ALU.add))
        step(dve.tensor_reduce(weight[:, :, :], cmp[:, :, :, :], AX.X, ALU.add))
        step(dve.scalar_tensor_tensor(weight[:, :, :], weight[:, :, :], 2.0, prob[:, :, :], ALU.is_lt, ALU.mult))
        step(dve.tensor_reduce(top, weight[:, :, :], AX.X, ALU.add))
        step(dve.tensor_scalar(top, top, 1e-9, None, ALU.add))
        step(dve.reciprocal(den, top))
        step(dve.tensor_scalar(den, den, 0.5, None, ALU.mult))
        step(dve.tensor_tensor(weight[:, :, :], weight[:, :, :], bcast(den, E1), ALU.mult))
        dve.sem_inc(weights_ready, 1)
        dve.sem_inc(y_read, 2)
        dve.sem_inc(y_added, 1)
        with dve.Fori(0, NB) as b:
            for e in range(E1):
                dve.wait_ge(y_done, b * E1 + (e + 3))
                dve.wait_ge(y_added, b * E1 + (e + 1))
                wcol = weight[:, ds(b * 4, 4), e:e + 1].to_broadcast([P, 4, P])
                dve.tensor_tensor(prod[:, :, :], ps_y[e % 2][:, :, :], wcol, ALU.mult).then_inc(y_read, 1)
                dve.wait_ge(y_read, b * E1 + (e + 3))
                xb = core.x[:, ds(b * 4, 4), :]
                dve.tensor_tensor(xb, xb, prod[:, :, :], ALU.add).then_inc(y_added, 1)
        dve.wait_ge(y_added, NB * E1 + 1)
        for q in range(4):
            dve.wait_ge(bias_done, q + 1)
            xq = core.x[:, 4 * q:4 * q + 4, :]
            step(dve.tensor_tensor(xq, xq, ln.ps[q][:, :].rearrange("p (t n) -> p t n", t=4), ALU.add))

    return dict(sync=sync, gpsimd=gpsimd, tensor=tensor, scalar=scalar, vector=vector)


def mixture_zero(core, name, ctx, w):
    nc = core.nc
    sb = lambda n, s, d=F32: ctx.enter_context(nc.sbuf_tensor(f"{name}_{n}", s, d))
    ln = LayerNorm(core, ctx, name)
    bank = core.bank
    PAIRS = E0 // 2
    WE = 8
    WP = WE // 2
    ROUNDS = E0 // (2 * WE)
    CE = BLOCK // CAPACITY
    CHUNKS = E0 // CE
    HALF = CHUNKS // 2
    RING = 4
    wr = sb("wr", [P, E0])
    wsgu = sb("wsgu", [P, 2 * F0])
    wsd = sb("wsd", [F0, P])
    number = sb("number", [P, CAPACITY])
    wgu = [sb(f"wgu{i}", [P, WE, 2 * F0]) for i in range(2)]
    wd = [sb(f"wd{i}", [F0, WE, P]) for i in range(2)]
    ex = sb("ex", [P, TILES, E0])
    repl = sb("repl", [P, TILES, E0])
    mask = sb("mask", [P, TILES, E0], BF16)
    weight = sb("weight", [P, TILES, E0])
    base = sb("base", [P, TILES, E0])
    place = sb("place", [P, TILES + 1, E0], BF16)
    top = sb("top", [P, TILES, TOP0])
    col = sb("col", [P, 2, TILES])
    room = sb("room", [1, 2, TILES])
    count_f = sb("count_f", [1, 1])
    count = sb("count", [1, 1], I32)
    zeros = sb("zeros", [P, BLOCK], BF16)
    xpart = sb("xpart", [P, 3, TILES, P], BF16)
    xrest = sb("xrest", [P, TILES, P])
    wpart = sb("wpart", [P, TILES, E0, 3], BF16)
    wrest = sb("wrest", [P, TILES, E0])
    S = sb("S", [P, RING, BLOCK], BF16)
    XT = sb("XT", [P, E0 * CAPACITY])
    wboth = sb("wboth", [P, PAIRS, 2])
    wslot = sb("wslot", [P, PAIRS])
    act_s = sb("act_s", [F0, 2, BLOCK])
    hT = sb("hT", [F0, 2, BLOCK])
    ys = sb("ys", [P, PAIRS, P])
    yrest = sb("yrest", [P, 2, WP, P])
    ypart = sb("ypart", [P, PAIRS, 3, P], BF16)
    ST = sb("ST", [P, 2, BLOCK], BF16)
    summed = sb("summed", [P, P])
    sem = lambda n: core.sem(f"{name}_{n}")
    loaded = sem("loaded")
    filled = sem("filled")
    logits_done = sem("logits_done")
    shifted = sem("shifted")
    exp_done = sem("exp_done")
    mask_ready = sem("mask_ready")
    counted = sem("counted")
    chain = sem("chain")
    count_ready = sem("count_ready")
    weights_ready = sem("weights_ready")
    cut = sem("cut")
    sh_gu = sem("sh_gu")
    sh_silu = sem("sh_silu")
    sh_h = sem("sh_h")
    sh_y = sem("sh_y")
    sh_added = sem("sh_added")
    s_made = [sem(f"s_made{i}") for i in range(2)]
    s_used = [sem(f"s_used{i}") for i in range(2)]
    gathered = sem("gathered")
    xt_ready = sem("xt_ready")
    wslot_ready = sem("wslot_ready")
    w_loaded = [sem(f"w_loaded{i}") for i in range(2)]
    w_free = sem("w_free")
    gu_done = sem("gu_done")
    silu_done = sem("silu_done")
    h_ready = sem("h_ready")
    y_done = sem("y_done")
    ys_ready = sem("ys_ready")
    y_rounded = sem("y_rounded")
    y_cut = sem("y_cut")
    c_made = sem("c_made")
    c_turned = sem("c_turned")
    st_ready = sem("st_ready")
    combined = sem("combined")
    sum_read = sem("sum_read")
    x_added = sem("x_added")

    def own_slots(ap):
        return ap.rearrange("p (e n) -> p e n", n=CAPACITY)

    def diagonal(ap):
        return ap.rearrange("p (k n) -> p k n", n=CAPACITY)[:, 0::3, :]

    def sync(sp):
        sp.dma_start(wr[:, :], w["router"]).then_inc(loaded, 16)
        sp.dma_start(wsgu[:, :], w["ws_gate_up"]).then_inc(loaded, 16)
        sp.dma_start(wsd[:, :], w["ws_down"]).then_inc(loaded, 16)
        sp.dma_start(number[:, :], w["slot_number"].unsqueeze(0).to_broadcast([P, CAPACITY])).then_inc(loaded, 16)
        sp.sem_inc(w_free, 2)
        with sp.Fori(0, ROUNDS) as r:
            for s in range(2):
                sp.wait_ge(w_free, r * 2 + (s + 1))
                at = r * (2 * WE) + s * WE
                sp.dma_start(wgu[s][:, :, :], w["gate_up"][:, ds(at, WE), :]).then_inc(w_loaded[s], 16)
                sp.dma_start(wd[s][:, :, :], w["down"][:, ds(at, WE), :]).then_inc(w_loaded[s], 16)

    def gpsimd(pool):
        pool.memset(zeros[:, :], 0.0).then_inc(filled, 1)
        pool.memset(place[:, TILES, :], 0.0).then_inc(filled, 1)
        c, y = Chain(cut), Chain(y_cut)

        def three_parts(c, value, rest, parts):
            for step in (
                    lambda: pool.tensor_copy(parts[0], value),
                    lambda: pool.tensor_tensor(rest, value, parts[0], ALU.subtract),
                    lambda: pool.tensor_copy(parts[1], rest),
                    lambda: pool.tensor_tensor(parts[2], rest, parts[1], ALU.subtract)):
                pool.wait_ge(c.sem, c.on(step()))

        pool.wait_ge(ln.xn_ready, TILES)
        three_parts(c, ln.xn[:, :, :], xrest[:, :, :], [xpart[:, i, :, :] for i in range(3)])
        pool.wait_ge(weights_ready, 1)
        three_parts(c, weight[:, :, :], wrest[:, :, :], [wpart[:, :, :, i] for i in range(3)])
        for g in range(PAIRS // WP):
            pool.wait_ge(y_rounded, g + 1)
            p = slice(WP * g, WP * g + WP)
            value, rest, parts = ys[:, p, :], yrest[:, g % 2, :, :], [ypart[:, p, i, :] for i in range(3)]
            pool.wait_ge(y.sem, y.on(pool.tensor_tensor(rest, value, parts[0], ALU.subtract)))
            pool.wait_ge(y.sem, y.on(pool.tensor_copy(parts[1], rest)))
            pool.wait_ge(y.sem, y.on(pool.tensor_tensor(parts[2], rest, parts[1], ALU.subtract)))

    def tensor(pe):
        ln.tensor(pe)
        pe.wait_ge(loaded, 64)
        for q in range(4):
            pe.wait_ge(ln.xnT_ready, q + 1)
            for i in range(4 * q, 4 * q + 4):
                last = pe.matmul(bank[4 + i // 8][:, E0 * (i % 8):E0 * (i % 8) + E0], ln.xnT[:, P * i:P * i + P],
                                 wr[:, :], start=True, stop=True)
        last.then_inc(logits_done, 1)

        def shared(q):
            gate, up = bank[2 * (q % 2)], bank[2 * (q % 2) + 1]
            xq = ln.xnT[:, BLOCK * q:BLOCK * q + BLOCK]
            if q >= 2:
                pe.wait_ge(sh_added, q - 1)
            pe.matmul(gate[0:F0, :], wsgu[:, 0:F0], xq, start=True, stop=True)
            pe.matmul(up[0:F0, :], wsgu[:, F0:2 * F0], xq, start=True, stop=True).then_inc(sh_gu, 1)

        def shared_out(q):
            pe.wait_ge(sh_h, q + 1)
            for t in range(4):
                last = pe.matmul(bank[2 * (q % 2)][:, P * t:P * t + P], hT[:, q % 2, P * t:P * t + P], wsd[:, :],
                                 start=True, stop=True)
            last.then_inc(sh_y, 1)

        shared(0)
        shared(1)
        shared_out(0)
        shared(2)
        shared_out(1)
        pe.wait_ge(mask_ready, 1)
        for h in range(2):
            m = mask[:, 8 * h:8 * h + 8, :].rearrange("p t e -> p (t e)")
            pe.matmul(bank[4 + h], core.tri[:, :], m, start=True, stop=True)
            last = pe.matmul(bank[6 + h], core.ones[:, :], m, start=True, stop=True)
        last.then_inc(counted, 1)
        shared_out(2)
        shared(3)
        shared_out(3)

        pe.wait_ge(sh_added, 4)
        pe.wait_ge(filled, 2)
        pe.wait_ge(cut, 4)
        pe.wait_ge(count_ready, 1)
        n = pe.value_load(count[0:1, 0:1], min_val=1, max_val=TILES)
        lhs0 = zeros[:, 0:P]
        pe.matmul(bank[4], lhs0, zeros[:, :], start=True, stop=False, skip_group_check=True)
        pe.wait_ge(cut, 8)
        for half in range(2):
            for k in range(HALF):
                if half:
                    pe.wait_ge(xt_ready, k + 1)
                pe.matmul(bank[k], lhs0, zeros[:, :], start=True, stop=False, skip_group_check=True)
            pe.sem_inc(s_used[half], RING)
            with pe.Fori(0, n) as t:
                for k in range(HALF):
                    pe.wait_ge(s_made[half], t * HALF + (k + 1))
                    for i in range(3):
                        pe.matmul(bank[k], xpart[:, i, ds(t, 1), :].rearrange("p t n -> p (t n)"), S[:, k, :],
                                  start=False, stop=False, skip_group_check=True)
                    for j in range(WP):
                        p = (half * HALF + k) * WP + j
                        rhs = wpart[:, ds(t, 1), 2 * p:2 * p + 2, :].rearrange("p t e i -> p (t e i)")
                        last = pe.matmul(bank[4][:, 6 * p:6 * p + 6], S[:, k, P * j:P * j + P], rhs,
                                         start=False, stop=False, skip_group_check=True)
                    last.then_inc(s_used[half], 1)
            for k in range(HALF):
                pe.matmul(bank[k], lhs0, zeros[:, :], start=False, stop=True, skip_group_check=True).then_inc(gathered, 1)
        pe.matmul(bank[4], lhs0, zeros[:, :], start=False, stop=True, skip_group_check=True).then_inc(gathered, 1)

        pe.wait_ge(xt_ready, 2 * HALF)
        pe.sem_inc(h_ready, 2)
        pe.sem_inc(y_done, 2)
        pe.sem_inc(ys_ready, 2)
        with pe.Fori(0, ROUNDS) as r:
            at = r * (2 * WP)

            def gate_up(j):
                s = j // WP
                if j % WP == 0:
                    pe.wait_ge(w_loaded[s], r * 32 + 32)
                pe.wait_ge(h_ready, at + (j + 1))
                moving = XT[:, ds(at * P + j * P, P)]
                for i in range(4):
                    lhs = wgu[s][:, 2 * (j % WP) + i % 2, F0 * (i // 2):F0 * (i // 2) + F0]
                    last = pe.matmul(bank[j % 2][0:F0, P * i:P * i + P], lhs, moving, start=True, stop=True)
                last.then_inc(gu_done, 1)

            gate_up(0)
            for j in range(2 * WP):
                if j + 1 < 2 * WP:
                    gate_up(j + 1)
                pe.wait_ge(h_ready, at + (j + 3))
                if j % WP == 0:
                    pe.wait_ge(ys_ready, r * 2 + (j // WP + 1))
                for i in range(2):
                    last = pe.matmul(bank[2 + j // WP][CAPACITY * i:CAPACITY * i + CAPACITY, P * (j % WP):P * (j % WP) + P],
                                     hT[:, j % 2, CAPACITY * i:CAPACITY * i + CAPACITY], wd[j // WP][:, 2 * (j % WP) + i, :],
                                     start=True, stop=True)
                last.then_inc(y_done, 1)
                if j % WP == WP - 1:
                    pe.wait_ge(y_done, at + (j + 3))
                    pe.sem_inc(w_free, 1)

        pe.wait_ge(wslot_ready, 1)
        pe.sem_inc(combined, 2)
        pe.sem_inc(sum_read, 1)
        pe.sem_inc(c_turned, RING)
        pe.sem_inc(st_ready, 2)
        with pe.Fori(0, n) as t:
            def turn(k):
                pe.wait_ge(c_made, t * CHUNKS + (k + 1))
                pe.wait_ge(st_ready, t * CHUNKS + (k + 1))
                for j in range(WP):
                    last = pe.transpose(bank[4 + k % 2].bitcast(BF16)[:, P * j:P * j + P],
                                        S[:, k % RING, P * j:P * j + P], core.identb[:, :])
                last.then_inc(c_turned, 1)

            def combine(k):
                pe.wait_ge(st_ready, t * CHUNKS + (k + 3))
                pe.wait_ge(y_cut, 3 * (k + 1))
                if k == 0:
                    pe.wait_ge(sum_read, t + 1)
                for j in range(WP):
                    p = k * WP + j
                    last = pe.matmul(bank[6][:, 0:3 * P], ST[:, k % 2, P * j:P * j + P],
                                     ypart[:, p, :, :].rearrange("p i n -> p (i n)"),
                                     start=(p == 0), stop=(p == PAIRS - 1))
                last.then_inc(combined, 1)

            turn(0)
            for k in range(CHUNKS):
                if k + 1 < CHUNKS:
                    turn(k + 1)
                combine(k)

    def scalar(act):
        ln.scalar(act)
        act.wait_ge(shifted, 1)
        act.activation(ex[:, :, :], ex[:, :, :], ACT.Exp).then_inc(exp_done, 1)
        for q in range(4):
            act.wait_ge(sh_gu, q + 1)
            if q >= 2:
                act.wait_ge(sh_h, q - 1)
            act.activation(act_s[:, q % 2, :], bank[2 * (q % 2)][0:F0, :], ACT.Silu).then_inc(sh_silu, 1)
        act.wait_ge(count_ready, 1)
        n = act.value_load(count[0:1, 0:1], min_val=1, max_val=TILES)
        for k in range(2 * HALF):
            act.wait_ge(gathered, k + 1)
            act.activation(XT[:, BLOCK * k:BLOCK * k + BLOCK], bank[k % HALF], ACT.Copy).then_inc(xt_ready, 1)

        def round_outputs(r, g):
            act.wait_ge(ys_ready, r * 2 + (g + 3))
            p = ds(r * (2 * WP) + g * WP, WP)
            act.activation(ypart[:, p, 0, :], ys[:, p, :], ACT.Copy).then_inc(y_rounded, 1)

        with act.Fori(0, ROUNDS) as r:
            for j in range(2 * WP):
                at = r * (2 * WP) + j
                act.wait_ge(gu_done, at + 1)
                act.wait_ge(h_ready, at + 1)
                act.activation(own_slots(act_s[:, j % 2, 0:P]), diagonal(bank[j % 2][0:F0, 0:2 * P]),
                               ACT.Silu).then_inc(silu_done, 1)
                if j == WP + 1:
                    round_outputs(r, 0)
            round_outputs(r, 1)
        with act.Fori(0, n) as t:
            for k in range(CHUNKS):
                act.wait_ge(c_turned, t * CHUNKS + (k + RING + 1))
                act.wait_ge(combined, t * CHUNKS + (k + 1))
                act.activation(ST[:, k % 2, :], bank[4 + k % 2].bitcast(BF16)[:, 0:BLOCK], ACT.Copy).then_inc(st_ready, 1)

    def vector(dve):
        ln.vector(dve)
        c = Chain(chain)

        def step(ins):
            dve.wait_ge(c.sem, c.on(ins))

        def shared_hidden(q):
            dve.wait_ge(sh_silu, q + 1)
            if q >= 2:
                dve.wait_ge(sh_y, q - 1)
            dve.tensor_tensor(hT[:, q % 2, :], act_s[:, q % 2, :], bank[2 * (q % 2) + 1][0:F0, :],
                              ALU.mult).then_inc(sh_h, 1)

        def shared_add(q):
            dve.wait_ge(sh_y, q + 1)
            xq = core.x[:, 4 * q:4 * q + 4, :]
            dve.scalar_tensor_tensor(xq, bank[2 * (q % 2)].rearrange("p (t n) -> p t n", n=P), 0.5, xq,
                                     ALU.mult, ALU.add).then_inc(sh_added, 1)

        most, den = (col[:, i, :] for i in range(2))
        dve.wait_ge(logits_done, 1)
        for h in range(2):
            lg = bank[4 + h].rearrange("p (t e) -> p t e", e=E0)
            step(dve.tensor_reduce(most[:, 8 * h:8 * h + 8], lg, AX.X, ALU.max))
            step(dve.tensor_tensor(ex[:, 8 * h:8 * h + 8, :], lg, bcast(most[:, 8 * h:8 * h + 8], E0), ALU.subtract))
        dve.sem_inc(shifted, 1)
        dve.wait_ge(exp_done, 1)
        for i in range(TILES):
            last = dve.max(top[:, i, :], ex[:, i, :])
        step(last)
        shared_hidden(0)
        for i in range(TILES):
            last = dve.match_replace(repl[:, i, :], top[:, i, :], ex[:, i, :], -1.0)
        step(last)
        step(dve.tensor_scalar(mask[:, :, :], repl[:, :, :], 0.0, None, ALU.is_lt))
        dve.sem_inc(mask_ready, 1)
        shared_hidden(1)
        shared_add(0)
        step(dve.scalar_tensor_tensor(weight[:, :, :], repl[:, :, :], 0.0, ex[:, :, :], ALU.is_lt, ALU.mult))
        step(dve.tensor_reduce(den, top[:, :, :], AX.X, ALU.add))
        step(dve.reciprocal(den, den))
        step(dve.tensor_scalar(den, den, 0.5, None, ALU.mult))
        step(dve.tensor_tensor(weight[:, :, :], weight[:, :, :], bcast(den, E0), ALU.mult))
        dve.sem_inc(weights_ready, 1)
        shared_hidden(2)
        shared_add(1)
        dve.wait_ge(counted, 1)
        step(dve.memset(base[:, 0, :], 0.0))
        for i in range(TILES - 1):
            tot = bank[6 + i // 8][:, E0 * (i % 8):E0 * (i % 8) + E0]
            step(dve.tensor_tensor(base[:, i + 1, :], base[:, i, :], tot, ALU.add))
        step(dve.tensor_reduce(room[:, 0, :], base[0:1, :, :], AX.X, ALU.min))
        step(dve.tensor_scalar(room[:, 1, :], room[:, 0, :], float(CAPACITY), None, ALU.is_lt))
        step(dve.tensor_reduce(count_f[:, :], room[:, 1, :], AX.X, ALU.add))
        step(dve.tensor_copy(count[:, :], count_f[:, :]))
        shared_add(2)
        shared_hidden(3)
        for h in range(2):
            cum = bank[4 + h].rearrange("p (t e) -> p t e", e=E0)
            bh = base[:, 8 * h:8 * h + 8, :]
            step(dve.tensor_tensor(bh, bh, cum, ALU.add))
        step(dve.scalar_tensor_tensor(base[:, :, :], base[:, :, :], float(CAPACITY), base[:, :, :], ALU.is_le, ALU.mult))
        step(dve.tensor_tensor(place[:, 0:TILES, :], base[:, :, :], mask[:, :, :], ALU.mult))
        dve.sem_inc(count_ready, 1)
        shared_add(3)
        dve.wait_ge(sh_added, 4)
        n = dve.value_load(count[0:1, 0:1], min_val=1, max_val=TILES)

        def make_chunk(t, k, slot):
            return dve.tensor_tensor(S[:, slot, :].rearrange("p (t e n) -> p t e n", t=1, n=CAPACITY),
                                     bcast(place[:, ds(t, 1), CE * k:CE * k + CE], CAPACITY),
                                     number[:, :].unsqueeze(1).unsqueeze(1).to_broadcast([P, 1, CE, CAPACITY]),
                                     ALU.is_equal)

        for half in range(2):
            if half:
                dve.wait_ge(gathered, HALF)
            with dve.Fori(0, n) as t:
                for k in range(HALF):
                    dve.wait_ge(s_used[half], t * HALF + (k + 1))
                    make_chunk(t, half * HALF + k, k).then_inc(s_made[half], 1)
        dve.wait_ge(gathered, 2 * HALF + 1)
        step(dve.tensor_reduce(wboth[:, :, :], bank[4][:, 0:6 * PAIRS].rearrange("p (q e i) -> p q e i", e=2, i=3),
                               AX.X, ALU.add))
        for i in range(2):
            own = slice(CAPACITY * i, CAPACITY * i + CAPACITY)
            last = dve.tensor_copy(wslot[own, :], wboth[own, :, i])
        step(last)
        dve.sem_inc(wslot_ready, 1)
        with dve.Fori(0, ROUNDS) as r:
            at = r * (2 * WP)

            def hidden(j):
                dve.wait_ge(silu_done, at + (j + 1))
                dve.wait_ge(y_done, at + (j + 1))
                dve.tensor_tensor(own_slots(hT[:, j % 2, 0:P]), own_slots(act_s[:, j % 2, 0:P]),
                                  diagonal(bank[j % 2][0:F0, 2 * P:4 * P]), ALU.mult).then_inc(h_ready, 1)

            def outputs(g):
                dve.wait_ge(y_done, at + (WP * g + WP + 2))
                dve.tensor_tensor(ys[:, ds(at + g * WP, WP), :], bank[2 + g].rearrange("p (q n) -> p q n", n=P),
                                  bcast(wslot[:, ds(at + g * WP, WP)], P), ALU.mult).then_inc(ys_ready, 1)

            for j in range(2 * WP):
                hidden(j)
                if j == WP:
                    outputs(0)
            outputs(1)
        dve.wait_ge(c_turned, RING)
        for k in range(RING):
            make_chunk(0, k, k).then_inc(c_made, 1)
        with dve.Fori(0, n) as t:
            for k in range(RING, CHUNKS + RING):
                dve.wait_ge(c_turned, t * CHUNKS + (k + 1))
                ahead = k // CHUNKS
                make_chunk(t + ahead, k % CHUNKS, k % RING).then_inc(c_made, 1)
            dve.wait_ge(combined, t * CHUNKS + (CHUNKS + 2))
            dve.tensor_reduce(summed[:, :], bank[6][:, 0:3 * P].rearrange("p (i n) -> p n i", i=3), AX.X,
                              ALU.add).then_inc(sum_read, 1)
            dve.wait_ge(sum_read, t + 2)
            xt = core.x[:, ds(t, 1), :].rearrange("p t n -> p (t n)")
            dve.tensor_tensor(xt, xt, summed[:, :], ALU.add).then_inc(x_added, 1)
            dve.wait_ge(x_added, t + 1)

    return dict(sync=sync, gpsimd=gpsimd, tensor=tensor, scalar=scalar, vector=vector)


H0, D0 = 16, 8
HG = 4
VW = 32


def attention_zero(core, name, ctx, w):
    nc = core.nc
    sb = lambda n, s, d=F32: ctx.enter_context(nc.sbuf_tensor(f"{name}_{n}", s, d))
    ln = LayerNorm(core, ctx, name)
    bank = core.bank
    SCALE = float(1.0 / np.sqrt(D0))
    NP = 6
    wqkv = sb("wqkv", [P, 3, P])
    bqkv = sb("bqkv", [P, 3, P])
    bv = sb("bv", [P, 1])
    wl = sb("wl", [P, 3])
    bl = sb("bl", [P, 1])
    cos = sb("cos", [P, 4, D0])
    sin = sb("sin", [P, 4, D0])
    rot = sb("rot", [P, 2, 4, H0, D0 // 2])
    z = sb("z", [P, 2, 4, P])
    e = sb("e", [P, 2, 4, P])
    rest = sb("rest", [P, 2, 4, P])
    part = [sb(f"part{i}", [P, 2, TILES, P], BF16) for i in range(3)]
    V = sb("V", [P, TILES, P])
    vT = sb("vT", [P, BLOCK])
    tap = sb("tap", [P, 2, BLOCK])
    lT = sb("lT", [P, TOKENS])
    stack = [[sb(f"stack{i}{a}", [P, 2, H0, P], BF16) for a in range(2)] for i in range(2)]
    turned = [[sb(f"turned{i}{a}", [P, H0, SEQ], BF16) for a in range(2)] for i in range(2)]
    Vs = [sb(f"Vs{i}", [P, 2, H0, VW]) for i in range(2)]
    lTs = [sb(f"lTs{i}", [P, SEQ]) for i in range(2)]
    select = sb("select", [P, H0, P], BF16)
    negmax = sb("negmax", [P, 2, H0])
    mparts = sb("mparts", [P, 2, P], BF16)
    shift = [sb(f"shift{i}", [P, SEQ], BF16) for i in range(2)]
    PT = sb("PT", [P, 2, HG, SEQ])
    OT = sb("OT", [P, 2, SEQ])
    rden = sb("rden", [P, 2, HG])
    attn = sb("attn", [P, 2, HG, D0])
    loaded = core.sem(f"{name}_loaded")
    filled = core.sem(f"{name}_filled")
    consts = core.sem(f"{name}_consts")
    qkv_done = core.sem(f"{name}_qkv_done")
    qkv_read = core.sem(f"{name}_qkv_read")
    neg_ready = core.sem(f"{name}_neg_ready")
    exp_ready = core.sem(f"{name}_exp_ready")
    rot_ready = core.sem(f"{name}_rot_ready")
    vT_done = core.sem(f"{name}_vT_done")
    vT_ready = core.sem(f"{name}_vT_ready")
    rounded = core.sem(f"{name}_rounded")
    rest_ready = core.sem(f"{name}_rest_ready")
    chain = core.sem(f"{name}_chain")
    stacked = core.sem(f"{name}_stacked")
    v_staged = core.sem(f"{name}_v_staged")
    stack_used = core.sem(f"{name}_stack_used")
    heads_done = core.sem(f"{name}_heads_done")
    st_turned = core.sem(f"{name}_st_turned")
    st_ready = core.sem(f"{name}_st_ready")
    s1_done = core.sem(f"{name}_s1_done")
    max_done = core.sem(f"{name}_max_done")
    parts_ready = core.sem(f"{name}_parts_ready")
    parts_hi = core.sem(f"{name}_parts_hi")
    parts_turned = core.sem(f"{name}_parts_turned")
    shift_ready = core.sem(f"{name}_shift_ready")
    s2_done = core.sem(f"{name}_s2_done")
    p_ready = core.sem(f"{name}_p_ready")
    pv_done = core.sem(f"{name}_pv_done")
    o_ready = core.sem(f"{name}_o_ready")
    o_turned = core.sem(f"{name}_o_turned")
    o_inv = core.sem(f"{name}_o_inv")
    o_scaled = core.sem(f"{name}_o_scaled")
    o_added = core.sem(f"{name}_o_added")
    l_turned = core.sem(f"{name}_l_turned")
    l_added = core.sem(f"{name}_l_added")
    UNITS = 2 * H0 // HG
    MUNITS = H0

    def sync(sp):
        sp.dma_start(wqkv[:, :, :], w["w_qkv"]).then_inc(loaded, 16)
        sp.dma_start(bqkv[:, :, :], w["b_qkv"].unsqueeze(0).to_broadcast([P, 3, P])).then_inc(loaded, 16)
        sp.dma_start(bv[:, :], w["b_v"]).then_inc(loaded, 16)
        sp.dma_start(wl[:, :], w["w_lepe"]).then_inc(loaded, 16)
        sp.dma_start(bl[:, :], w["b_lepe"]).then_inc(loaded, 16)
        sp.dma_start(cos[:, :, :], w["rope_cos"]).then_inc(loaded, 16)
        sp.dma_start(sin[:, :, :], w["rope_sin"]).then_inc(loaded, 16)

    def gpsimd(pool):
        for i in range(2):
            for a in range(2):
                pool.memset(stack[i][a][:, :, :, :], 0.0).then_inc(filled, 1)
            pool.memset(Vs[i][:, :, :, :], 0.0).then_inc(filled, 1)
        pool.memset(select[:, :, :], 0.0).then_inc(filled, 1)
        pool.memset(mparts[:, :, :], 0.0).then_inc(consts, 1)
        pool.wait_ge(filled, 7)
        for i in range(2):
            pool.memset(Vs[i][:, :, :, D0:D0 + 1], 1.0).then_inc(consts, 1)
        pool.affine_select(out=select[:, :, :], in_=select[:, :, :], compare_op=ALU.not_equal, fill=1.0, base=0,
                           pattern=[[-1, H0], [0, P]], channel_multiplier=1).then_inc(filled, 1)
        pool.wait_ge(filled, 8)
        pool.affine_select(out=select[:, :, :], in_=select[:, :, :], compare_op=ALU.not_equal, fill=1.0, base=-H0,
                           pattern=[[-1, H0], [0, P]], channel_multiplier=1).then_inc(consts, 1)
        pool.wait_ge(consts, 4)
        pool.wait_ge(loaded, 7 * 16)
        for q in range(4):
            for i, out in enumerate((rest[:, :, :, :], part[2][:, :, 4 * q:4 * q + 4, :])):
                pool.wait_ge(rounded, 2 * q + (i + 1))
                rounds = part[i][:, :, 4 * q:4 * q + 4, :]
                before = (z, rest)[i]
                for a in range(2):
                    last = pool.tensor_tensor(out[:, a, :, :], before[:, a, :, :], rounds[:, a, :, :], ALU.subtract)
                last.then_inc(rest_ready, 1)
            pool.wait_ge(rest_ready, 2 * q + 2)
        for b in range(BATCH):
            if 2 <= b + 1 < BATCH:
                pool.wait_ge(stack_used, b)
                stack_batch(pool.tensor_copy, b + 1)
            stage_values(pool, b)

    def stack_batch(copy, b):
        s = b % 2
        t = slice(2 * b, 2 * b + 2)
        for a, copies in enumerate((
                ((0, slice(0, 3)), (1, slice(3, 5)), (2, slice(5, 6))),
                ((0, slice(0, 4, 3)), (0, slice(5, 6)), (1, slice(1, 5, 3)), (2, slice(2, 3))))):
            view = stack[s][a][:, :, :, 0:NP * D0].rearrange("p t h (k d) -> p (t h) k d", d=D0)
            for i, slots in copies:
                dst = view[:, :, slots, :]
                n = dst.shape[2]
                src = part[i][:, a, t, :].rearrange("p t (h d) -> p (t h) d", d=D0)
                last = copy(dst, src.unsqueeze(2).to_broadcast([P, 2 * H0, n, D0]))
        last.then_inc(stacked, 1)

    def stage_values(pool, b):
        s = b % 2
        if b >= 2:
            pool.wait_ge(heads_done, b - 1)
        pool.wait_ge(vT_ready, b // 2 + 1)
        pool.tensor_copy(lTs[s][:, :], lT[:, SEQ * b:SEQ * b + SEQ])
        pool.tensor_copy(Vs[s][:, :, :, 0:D0],
                         V[:, 2 * b:2 * b + 2, :].rearrange("p t (h d) -> p t h d", d=D0)).then_inc(v_staged, 1)

    def tensor(pe):
        def turn_stack(b, s, v, ahead=1):
            to = bank[(v + 1) % ahead if ahead > 1 else 1].bitcast(BF16)
            g, a = v // 2, v % 2
            if v == 0:
                pe.wait_ge(stacked, b + 1)
            if v >= ahead or ahead == 1:
                pe.wait_ge(st_ready, b * UNITS + (v + 2 - ahead))
            for j in range(HG):
                for t in range(2):
                    last = pe.transpose(to[:, SEQ * j + P * t:SEQ * j + P * t + P],
                                        stack[s][a][:, t, HG * g + j, :], core.identb[:, :])
            last.then_inc(st_turned, 1)
            if v == UNITS - 1:
                pe.wait_ge(st_turned, b * UNITS + UNITS)
                pe.sem_inc(stack_used, 1)

        def scores_by_query(b, s, m):
            h, qt = 2 * (m // 2), m % 2
            if m == 0:
                pe.wait_ge(st_ready, b * UNITS + (UNITS + 1))
            pe.wait_ge(max_done, b * MUNITS + (m + 1))
            for j in range(2):
                last = pe.matmul(bank[0][:, SEQ * j:SEQ * j + SEQ], turned[s][0][:, h + j, P * qt:P * qt + P],
                                 turned[s][1][:, h + j, :], start=True, stop=True)
            last.then_inc(s1_done, 1)

        def turn_maxima(b, s, former):
            pe.wait_ge(parts_ready, b + 2)
            if former:
                pe.wait_ge(o_added, b * 4)
            for qt in range(2):
                last = pe.transpose(bank[7].bitcast(BF16)[:, P * qt:P * qt + P], mparts[:, qt, :], core.identb[:, :])
            last.then_inc(parts_turned, 1)

        def values(b, s, u):
            g, kt = u // 2, u % 2
            pe.wait_ge(p_ready, b * UNITS + (u + 3))
            if u == 0:
                pe.wait_ge(v_staged, b + 1)
            if kt == 0:
                pe.wait_ge(o_ready, b * 4 + (g + 1))
            for j in range(HG):
                last = pe.matmul(bank[6][VW * j:VW * j + VW, 0:SEQ], Vs[s][:, kt, HG * g + j, :],
                                 PT[:, u % 2, j, :], start=(kt == 0), stop=(kt == 1))
            last.then_inc(pv_done, 1)

        def turn_out(b, s, g, following=False):
            pe.wait_ge(o_ready, b * 4 + (g + 2))
            pe.wait_ge(o_added, b * 4 + (g + 1))
            if g == 0:
                pe.wait_ge(l_added, b + 1)
            if g == 3 and following:
                pe.wait_ge(shift_ready, b + 3)
            for qt in range(2):
                last = pe.transpose(bank[7][:, P * qt:P * qt + P], OT[:, g % 2, P * qt:P * qt + P], core.ident[:, :])
            last.then_inc(o_turned, 1)

        def batch(b, s, next1, next2):
            pe.wait_ge(shift_ready, b + 2)
            for u in range(UNITS):
                g, kt = u // 2, u % 2
                pe.wait_ge(p_ready, b * UNITS + (u + 1))
                for half in range(2):
                    out = bank[2 + 2 * (u % 2) + half]
                    for j in range(2):
                        h = HG * g + 2 * half + j
                        pe.matmul(out[:, SEQ * j:SEQ * j + SEQ], turned[s][1][:, h, P * kt:P * kt + P],
                                  turned[s][0][:, h, :], start=True, stop=False, skip_group_check=True)
                        last = pe.matmul(out[:, SEQ * j:SEQ * j + SEQ], select[:, h, :], shift[s][:, :],
                                         start=False, stop=True, skip_group_check=True)
                last.then_inc(s2_done, 1)
                if next1:
                    scores_by_query(b + 1, 1 - s, 2 * u)
                if u:
                    values(b, s, u - 1)
                if u >= 3 and u % 2:
                    turn_out(b, s, (u - 3) // 2)
                if next2 and u >= 2:
                    turn_stack(b + 2, s, u - 2)
                if next1:
                    scores_by_query(b + 1, 1 - s, 2 * u + 1)
            values(b, s, UNITS - 1)
            if next2:
                turn_stack(b + 2, s, UNITS - 2)
            if next1:
                turn_maxima(b + 1, 1 - s, True)
            turn_out(b, s, 3, following=next1)
            if next2:
                turn_stack(b + 2, s, UNITS - 1)
            pe.wait_ge(o_added, b * 4 + 5)
            for qt in range(2):
                last = pe.transpose(bank[7][:, P * qt:P * qt + P], lTs[s][:, P * qt:P * qt + P], core.ident[:, :])
            last.then_inc(l_turned, 1)
            pe.wait_ge(l_turned, b + 1)
            pe.sem_inc(heads_done, 1)

        ln.tensor(pe)
        pe.wait_ge(loaded, 7 * 16)
        for q in range(4):
            pe.wait_ge(ln.xnT_ready, q + 1)
            if q:
                pe.wait_ge(qkv_read, q)
            for i in range(3):
                for t in range(4):
                    at = P * (4 * q + t)
                    last = pe.matmul(bank[4 + i][:, P * t:P * t + P], ln.xnT[:, at:at + P], wqkv[:, i, :],
                                     start=True, stop=True)
            last.then_inc(qkv_done, 1)
            if q:
                pe.wait_ge(vT_ready, q)
            pe.matmul(bank[7], wqkv[:, 2, :], ln.xnT[:, BLOCK * q:BLOCK * q + BLOCK],
                      start=True, stop=True).then_inc(vT_done, 1)
            if q == 3:
                pe.wait_ge(ln.xnT_ready, 4)
                pe.sem_inc(st_ready, 1)
                for v in range(UNITS):
                    turn_stack(0, 0, v, ahead=4)
        pe.wait_ge(consts, 4)
        pe.wait_ge(vT_ready, 4)
        pe.sem_inc(max_done, 1)
        pe.sem_inc(p_ready, 2)
        pe.sem_inc(pv_done, 2)
        pe.sem_inc(o_ready, 1)
        pe.sem_inc(o_added, 1)
        pe.sem_inc(l_added, 1)
        pe.sem_inc(shift_ready, 1)
        for m in range(MUNITS):
            scores_by_query(0, 0, m)
            if m % 2:
                turn_stack(1, 1, m // 2)
        turn_maxima(0, 0, False)
        with pe.Fori(0, BATCH // 2 - 1) as bp:
            for s in range(2):
                batch(bp * 2 + s, s, True, True)
        batch(BATCH - 2, 0, True, False)
        batch(BATCH - 1, 1, False, False)

    def scalar(act):
        def take_turned(b, s, v, ahead=1):
            g, a = v // 2, v % 2
            act.wait_ge(st_turned, b * UNITS + (v + 1))
            act.activation(turned[s][a][:, HG * g:HG * g + HG, :],
                           bank[(v + 1) % ahead if ahead > 1 else 1].bitcast(BF16).rearrange("p (h n) -> p h n", n=SEQ), ACT.Copy).then_inc(st_ready, 1)

        def batch(b, s, next2):
            for u in range(UNITS):
                act.wait_ge(s2_done, b * UNITS + (u + 1))
                act.wait_ge(pv_done, b * UNITS + (u + 1))
                pair = core.psum[:, 2 + 2 * (u % 2):4 + 2 * (u % 2), :].rearrange("p a (h n) -> p (a h) n", n=SEQ)
                act.activation(PT[:, u % 2, :, :], pair, ACT.Exp, scale=SCALE).then_inc(p_ready, 1)
                if next2 and u >= 2:
                    take_turned(b + 2, s, u - 2)
            if next2:
                take_turned(b + 2, s, UNITS - 2)
                take_turned(b + 2, s, UNITS - 1)

        ln.scalar(act)
        for q in range(4):
            act.wait_ge(neg_ready, q + 1)
            act.activation(e[:, :, :, :], e[:, :, :, :], ACT.Exp).then_inc(exp_ready, 1)
            if q == 3:
                for v in range(UNITS):
                    take_turned(0, 0, v, ahead=4)
            act.wait_ge(rot_ready, q + 1)
            act.activation(part[0][:, :, 4 * q:4 * q + 4, :], z[:, :, :, :], ACT.Copy).then_inc(rounded, 1)
            act.wait_ge(rest_ready, 2 * q + 1)
            act.activation(part[1][:, :, 4 * q:4 * q + 4, :], rest[:, :, :, :], ACT.Copy).then_inc(rounded, 1)
            if q == 0:
                act.wait_ge(rest_ready, 2)
                act.wait_ge(consts, 4)
                for b in range(2):
                    stack_batch(lambda out, in_: act.activation(out, in_, ACT.Copy), b)
        for v in range(UNITS):
            take_turned(1, 1, v)
        with act.Fori(0, BATCH // 2 - 1) as bp:
            for s in range(2):
                batch(bp * 2 + s, s, True)
        batch(BATCH - 2, 0, False)
        batch(BATCH - 1, 1, False)

    def vector(dve):
        ln.vector(dve)
        c = Chain(chain)

        def step(ins):
            dve.wait_ge(c.sem, c.on(ins))

        dve.wait_ge(loaded, 7 * 16)
        for q in range(4):
            dve.wait_ge(qkv_done, q + 1)
            if q:
                dve.wait_ge(rest_ready, 2 * q - 1)
            for i in range(2):
                step(dve.tensor_tensor(z[:, i, :, :], bank[4 + i].rearrange("p (t n) -> p t n", n=P),
                                       bqkv[:, i, :].unsqueeze(1).to_broadcast([P, 4, P]), ALU.add))
            dve.tensor_scalar(e[:, :, :, :], z[:, :, :, :], 0.0, None, ALU.min).then_inc(neg_ready, 1)
            step(dve.tensor_tensor(V[:, 4 * q:4 * q + 4, :], bank[6].rearrange("p (t n) -> p t n", n=P),
                                   bqkv[:, 2, :].unsqueeze(1).to_broadcast([P, 4, P]), ALU.add))
            dve.sem_inc(qkv_read, 1)
            dve.wait_ge(vT_done, q + 1)
            step(dve.tensor_scalar(vT[:, :], bank[7], bv[:, 0:1], None, ALU.add))
            lq = lT[:, BLOCK * q:BLOCK * q + BLOCK]
            step(dve.tensor_scalar(lq, vT[:, :], wl[:, 1:2], bl[:, 0:1], ALU.mult, ALU.add))
            l2 = lq.rearrange("p (b n) -> p b n", n=SEQ)
            v2 = vT[:, :].rearrange("p (b n) -> p b n", n=SEQ)
            step(dve.scalar_tensor_tensor(l2[:, :, 1:SEQ], v2[:, :, 0:SEQ - 1], wl[:, 0:1], l2[:, :, 1:SEQ],
                                          ALU.mult, ALU.add))
            step(dve.scalar_tensor_tensor(l2[:, :, 0:SEQ - 1], v2[:, :, 1:SEQ], wl[:, 2:3], l2[:, :, 0:SEQ - 1],
                                          ALU.mult, ALU.add))
            dve.sem_inc(vT_ready, 1)
            dve.wait_ge(exp_ready, q + 1)
            step(dve.scalar_tensor_tensor(e[:, :, :, :].rearrange("p i t n -> p (i t n)"),
                                          z[:, :, :, :].rearrange("p i t n -> p (i t n)"), 0.0,
                                          e[:, :, :, :].rearrange("p i t n -> p (i t n)"), ALU.max, ALU.add))
            for i in range(2):
                src = e[:, i, :, :].rearrange("p t (h d) -> p t h d", d=D0)
                dst = z[:, i, :, :].rearrange("p t (h d) -> p t h d", d=D0)
                co = cos[:, :, :].unsqueeze(2).to_broadcast([P, 4, H0, D0])
                si = sin[:, :, :].unsqueeze(2).to_broadcast([P, 4, H0, D0])
                c.on(dve.tensor_tensor(dst, src, co, ALU.mult))
                for o in range(2):
                    c.on(dve.tensor_tensor(rot[:, o, :, :, :], src[:, :, :, 1 - o::2], si[:, :, :, o::2], ALU.mult))
                dve.wait_ge(c.sem, c.n)
                for o in range(2):
                    c.on(dve.tensor_tensor(dst[:, :, :, o::2], dst[:, :, :, o::2], rot[:, o, :, :, :], ALU.add))
                dve.wait_ge(c.sem, c.n)
            dve.sem_inc(rot_ready, 1)

        def maximum(b, m):
            h, qt = 2 * (m // 2), m % 2
            dve.wait_ge(s1_done, b * MUNITS + (m + 1))
            if m == 0:
                dve.wait_ge(parts_ready, b + 1)
            dve.tensor_reduce(negmax[:, qt, h:h + 2], bank[0].rearrange("p (h n) -> p h n", n=SEQ), AX.X, ALU.max,
                              negate=True).then_inc(max_done, 1)

        def split_maxima(b, s):
            dve.wait_ge(max_done, b * MUNITS + (MUNITS + 1))
            dve.wait_ge(parts_turned, b + 1)
            dve.tensor_copy(mparts[:, :, 0:H0], negmax[:, :, :]).then_inc(parts_hi, 1)
            dve.wait_ge(parts_hi, b + 1)
            dve.tensor_tensor(mparts[:, :, H0:2 * H0], negmax[:, :, :], mparts[:, :, 0:H0],
                              ALU.subtract).then_inc(parts_ready, 1)

        def take_shift(b, s):
            dve.wait_ge(parts_turned, b + 2)
            dve.tensor_copy(shift[s][:, :], bank[7].bitcast(BF16)[:, 0:SEQ]).then_inc(shift_ready, 1)

        def group(b, s, g):
            dve.wait_ge(pv_done, b * UNITS + (2 * g + 4))
            dve.tensor_copy(OT[:, g % 2, :], bank[6][:, 0:SEQ]).then_inc(o_ready, 1)

        def finish_group(b, s, g):
            dve.wait_ge(o_turned, b * 4 + (g + 1))
            o = bank[7][:, 0:SEQ].rearrange("p (t j v) -> p t j v", t=2, v=VW)
            dve.reciprocal(rden[:, :, :], o[:, :, :, D0]).then_inc(o_inv, 1)
            dve.wait_ge(o_inv, b * 4 + (g + 1))
            dve.tensor_tensor(attn[:, :, :, :], o[:, :, :, 0:D0], bcast(rden[:, :, :], D0), ALU.mult).then_inc(o_scaled, 1)
            dve.wait_ge(o_scaled, b * 4 + (g + 1))
            xg = core.x[:, ds(b * 2, 2), HG * D0 * g:HG * D0 * g + HG * D0]
            dve.tensor_tensor(xg, xg, attn[:, :, :, :].rearrange("p t j d -> p t (j d)"), ALU.add).then_inc(o_added, 1)

        dve.sem_inc(parts_ready, 1)
        dve.sem_inc(parts_turned, 1)
        for m in range(MUNITS):
            maximum(0, m)
        split_maxima(0, 0)
        take_shift(0, 0)

        def batch(b, s, next1):
            for u in range(UNITS):
                if u >= 3 and u % 2:
                    group(b, s, (u - 3) // 2)
                if next1:
                    maximum(b + 1, 2 * u)
                    maximum(b + 1, 2 * u + 1)
                if u >= 3 and u % 2:
                    finish_group(b, s, (u - 3) // 2)
            if next1:
                split_maxima(b + 1, 1 - s)
            group(b, s, 3)
            if next1:
                take_shift(b + 1, 1 - s)
            finish_group(b, s, 3)
            dve.wait_ge(l_turned, b + 1)
            dve.wait_ge(o_added, b * 4 + 5)
            xb = core.x[:, ds(b * 2, 2), :]
            dve.tensor_tensor(xb, xb, bank[7][:, 0:SEQ].rearrange("p (t n) -> p t n", n=P), ALU.add).then_inc(l_added, 1)

        with dve.Fori(0, BATCH // 2 - 1) as bp:
            for s in range(2):
                batch(bp * 2 + s, s, True)
        batch(BATCH - 2, 0, True)
        batch(BATCH - 1, 1, False)

    return dict(sync=sync, gpsimd=gpsimd, tensor=tensor, scalar=scalar, vector=vector)


H1, D1, NB1, SPAN = 16, 64, 10, 128
CH = H1 // 2
RH = 8
ZW = 3 * SPAN
MASKED = 1e9


def attention_one(core, name, ctx, w):
    nc = core.nc
    sb = lambda n, s, d=F32: ctx.enter_context(nc.sbuf_tensor(f"{name}_{n}", s, d))
    ln = LayerNorm(core, ctx, name)
    bank = core.bank
    RSCALE = float(D1) ** -0.5
    wq = sb("wq", [P, H1 * D1])
    wk = sb("wk", [P, H1 * D1])
    wv = sb("wv", [P, H1 * D1])
    wp = sb("wp", [P, CH, P])
    wr = sb("wr", [P, H1 * NB1])
    bq = sb("bq", [P, 2, CH])
    br = sb("br", [RH * NB1, 2])
    bp_row = sb("bp_row", [P, P])
    bnd = sb("bnd", [RH * NB1, RH, SPAN])
    pad = sb("pad", [P, SPAN])
    xs = sb("xs", [P, 2, SEQ])
    RT = sb("RT", [RH * NB1, 2, SEQ])
    G = sb("G", [P, 2, H1, SPAN])
    X0 = [sb(f"X0_{i}", [P, H1, SPAN]) for i in range(2)]
    X1 = [sb(f"X1_{i}", [P, H1, 2 * SPAN]) for i in range(2)]
    Qz = [sb(f"Qz{i}", [P, H1, SEQ]) for i in range(2)]
    KT = [sb(f"KT{i}", [P, CH, SEQ]) for i in range(2)]
    V = [sb(f"V{i}", [P, 2, H1 * D1]) for i in range(2)]
    L = sb("L", [P, 2, 3 * P])
    least = sb("least", [P, 2, 2])
    pr = sb("pr", [P, 4, 3 * P])
    sums = sb("sums", [P, 4, 2])
    rinv = sb("rinv", [P, 4, 2])
    PT = sb("PT", [P, 2, 3 * P])
    AT = sb("AT", [P, CH, SEQ])
    z = [[nc.dram_tensor(f"{name}_z{s}{q}", [P * H1 * ZW], F32) for q in range(2)] for s in range(2)]

    loaded = core.sem(f"{name}_loaded")
    bnd_zero = core.sem(f"{name}_bnd_zero")
    q_zero = core.sem(f"{name}_q_zero")
    prep = core.sem(f"{name}_prep")
    pad_filled = core.sem(f"{name}_pad_filled")
    pads_written = core.sem(f"{name}_pads_written")
    xs_ready = core.sem(f"{name}_xs_ready")
    xs_free = core.sem(f"{name}_xs_free")
    piece_done = core.sem(f"{name}_piece_done")
    piece_read = [core.sem(f"{name}_piece_read{i}") for i in range(2)]
    g_by_act = core.sem(f"{name}_g_by_act")
    g_by_dve = core.sem(f"{name}_g_by_dve")
    z_written = core.sem(f"{name}_z_written")
    x_turned = core.sem(f"{name}_x_turned")
    qkv_act = core.sem(f"{name}_qkv_act")
    qkv_dve = core.sem(f"{name}_qkv_dve")
    s_done = core.sem(f"{name}_s_done")
    l_begun = core.sem(f"{name}_l_begun")
    l_ready = core.sem(f"{name}_l_ready")
    p_ready = core.sem(f"{name}_p_ready")
    inv_ready = core.sem(f"{name}_inv_ready")
    pn_ready = core.sem(f"{name}_pn_ready")
    p_turned = core.sem(f"{name}_p_turned")
    pT_ready = core.sem(f"{name}_pT_ready")
    pv_done = core.sem(f"{name}_pv_done")
    aT_ready = core.sem(f"{name}_aT_ready")
    out_done = core.sem(f"{name}_out_done")
    out_added = core.sem(f"{name}_out_added")
    PIECES = 21
    STEPS = H1 + 3
    plan = [[u] for u in range(H1)] + [[16, 17], [18, 19], [20]]

    def kind(k):
        if k == 0:
            return "R", 0
        if k < 9:
            return "G", k - 1
        if k < 17:
            return "QK", k - 9
        return "V", k - 17

    def by_act(k):
        name_, j = kind(k)
        return name_ != "R" and j % 2 == 0

    N_ACT = sum(by_act(k) and kind(k)[0] in ("QK", "V") for k in range(PIECES))
    N_DVE = sum(not by_act(k) and kind(k)[0] in ("QK", "V") for k in range(PIECES))

    def piece_at(bp, s, k):
        return (s + k) % 2, bp * PIECES + (s * PIECES + k) // 2

    def sync(sp):
        sp.dma_start(wr[:, :], w["Wr"]).then_inc(loaded, 16)
        sp.dma_start(wq[:, :], w["Wq"]).then_inc(loaded, 16)
        sp.dma_start(wk[:, :], w["Wk"]).then_inc(loaded, 16)
        sp.dma_start(wv[:, :], w["Wv"]).then_inc(loaded, 16)
        sp.dma_start(wp[:, :, :], w["Wproj"].rearrange("(c p) n -> p c n", p=P)).then_inc(loaded, 16)
        sp.dma_start(bq[:, 0, :], w["bq"]).then_inc(loaded, 16)
        sp.dma_start(br[:, :], w["br"]).then_inc(loaded, 16)
        sp.dma_start(bp_row[:, :], w["bproj"].unsqueeze(0).to_broadcast([P, P])).then_inc(loaded, 16)
        sp.wait_ge(bnd_zero, 1)
        for h in range(RH):
            sp.dma_start(bnd[NB1 * h:NB1 * h + NB1, h, :], w["b_nd"]).then_inc(loaded, 16)
        sp.wait_ge(pad_filled, 1)
        for s in range(2):
            for q in range(2):
                rows = z[s][q].ap().rearrange("(p h n) -> p h n", h=H1, n=ZW)
                for side in (0, 2 * SPAN):
                    sp.dma_start(rows[:, :, side:side + SPAN],
                                 pad[:, :].unsqueeze(1).to_broadcast([P, H1, SPAN])).then_inc(pads_written, 16)
        sp.wait_ge(pads_written, 8 * 16)
        sp.sem_inc(z_written, 32)
        sp.sem_inc(x_turned, 64)
        for b in range(BATCH):
            s = b % 2
            sp.wait_ge(x_turned, 32 * (b + 1))
            if b >= 2:
                sp.wait_ge(l_ready, H1 * (b - 1) + 2)
            for q in range(2):
                sp.wait_ge(g_by_act, 4 * b + 2 * (q + 1))
                sp.wait_ge(g_by_dve, 4 * b + 2 * (q + 1))
                rows = z[s][q].ap().rearrange("(p h n) -> p h n", h=H1, n=ZW)
                sp.dma_start(rows[:, :, SPAN:2 * SPAN], G[:, q, :, :]).then_inc(z_written, 16)
                sp.wait_ge(z_written, 32 * (b + 1) + 16 * (q + 1))
                turned = bass.AP(z[s][q], 2 * SPAN - 1 - SPAN * q, [[H1 * ZW - 1, P], [ZW, H1], [1, SPAN * (q + 1)]])
                sp.dma_start((X0, X1)[q][s][:, :, :], turned).then_inc(x_turned, 16)
        sp.wait_ge(x_turned, 32 * (BATCH + 2))

    def gpsimd(pool):
        pool.memset(bnd[:, :, :], 0.0).then_inc(bnd_zero, 1)
        pool.memset(pad[:, :], MASKED).then_inc(pad_filled, 1)
        for s in range(2):
            pool.memset(Qz[s][:, :, :], 0.0).then_inc(q_zero, 1)
        pool.wait_ge(ln.xnT_ready, 4)
        pool.sem_inc(xs_free, 2)
        for b in range(BATCH):
            pool.wait_ge(xs_free, b + 1)
            pool.tensor_copy(xs[:, b % 2, :], ln.xnT[:, SEQ * b:SEQ * b + SEQ]).then_inc(xs_ready, 1)

    def tensor(pe):
        ln.tensor(pe)
        pe.wait_ge(loaded, 16 * 16)
        pe.wait_ge(ln.xnT_ready, 4)
        pe.sem_inc(piece_read[0], 1)
        pe.sem_inc(piece_read[1], 1)

        def piece(bp, s, k):
            which, j = kind(k)
            i, used = piece_at(bp, s, k)
            out = bank[5 + i]
            b = bp * 2 + s
            if k == 0:
                pe.wait_ge(xs_ready, b + 1)
            if k == 1:
                pe.wait_ge(piece_read[s % 2], bp * PIECES + (s * PIECES) // 2 + 2)
            pe.wait_ge(piece_read[i], used + 1)
            if which == "R":
                for c in range(2):
                    last = pe.matmul(out[0:RH * NB1, SEQ * c:SEQ * c + SEQ], wr[:, RH * NB1 * c:RH * NB1 * (c + 1)],
                                     xs[:, s, :], start=True, stop=True)
            elif which == "G":
                q, c, half = j // 4, (j % 4) // 2, j % 2
                last = pe.matmul(out, RT[:, c, P * q:P * q + P],
                                 bnd[:, 4 * half:4 * half + 4, :].rearrange("p h n -> p (h n)"), start=True, stop=True)
            elif which == "QK":
                for a, m in enumerate((wq, wk)):
                    last = pe.matmul(out[:, SEQ * a:SEQ * a + SEQ], m[:, P * j:P * j + P], xs[:, s, :],
                                     start=True, stop=True)
            else:
                t, half = j // 2, j % 2
                last = pe.matmul(out, xs[:, s, P * t:P * t + P], wv[:, 512 * half:512 * half + 512],
                                 start=True, stop=True)
            last.then_inc(piece_done, 1)
            if k == PIECES - 1:
                pe.wait_ge(piece_done, b * PIECES + PIECES)
                pe.sem_inc(xs_free, 1)

        def scores(b, s, h):
            pe.wait_ge(l_ready, b * H1 + (h + 1))
            S = bank[h % 2]
            pe.matmul(S[:, 0:P], Qz[s][:, h, 0:P], KT[s][:, h // 2, 0:P], start=True, stop=True)
            pe.matmul(S[:, P:3 * P], Qz[s][:, h, P:2 * P], KT[s][:, h // 2, :], start=True, stop=True).then_inc(s_done, 1)

        def turn(b, h):
            pe.wait_ge(pn_ready, b * H1 + (h + 1))
            pe.wait_ge(pT_ready, b * H1 + (h + 1))
            for i in range(3):
                last = pe.transpose(bank[2 + h % 2][:, P * i:P * i + P], pr[:, h % 4, P * i:P * i + P],
                                    core.ident[:, :])
            last.then_inc(p_turned, 1)

        def values(b, s, h):
            c, half = h // 2, h % 2
            pe.wait_ge(pT_ready, b * H1 + (h + 3))
            if half == 0:
                pe.wait_ge(aT_ready, b * CH + (c + 1))
                if c == 0:
                    pe.wait_ge(out_added, b + 1)
            o = bank[4 + 3 * (c % 2)][D1 * half:D1 * half + D1, 0:SEQ]
            vh = V[s][:, :, D1 * h:D1 * h + D1]
            pe.matmul(o, vh[:, 0, :], PT[:, h % 2, 0:SEQ], start=True, stop=False, skip_group_check=True)
            pe.matmul(o[:, P:2 * P], vh[:, 1, :], PT[:, h % 2, SEQ:SEQ + P], start=False, stop=True,
                      skip_group_check=True).then_inc(pv_done, 1)

        def batch(bp, s, following):
            b = bp * 2 + s
            nbp, ns = (bp, 1) if s == 0 else (bp + 1, 0)
            for u in range(STEPS):
                if u == 0:
                    pe.wait_ge(qkv_act, b * N_ACT + N_ACT)
                    pe.wait_ge(qkv_dve, b * N_DVE + N_DVE)
                if u < H1:
                    scores(b, s, u)
                if 2 <= u < H1 + 2:
                    turn(b, u - 2)
                if u >= 3:
                    values(b, s, u - 3)
                if following:
                    for k in plan[u]:
                        piece(nbp, ns, k)
            pe.wait_ge(aT_ready, b * CH + (CH + 2))
            for q in range(2):
                for c in range(CH):
                    last = pe.matmul(bank[4][:, P * q:P * q + P], AT[:, c, P * q:P * q + P], wp[:, c, :],
                                     start=(c == 0), stop=(c == CH - 1))
            last.then_inc(out_done, 1)

        pe.wait_ge(q_zero, 2)
        for k in range(PIECES):
            piece(0, 0, k)
        pe.sem_inc(pv_done, 2)
        pe.sem_inc(p_turned, 4)
        pe.sem_inc(out_done, 1)
        with pe.Fori(0, BATCH // 2 - 1) as bp:
            for s in range(2):
                batch(bp, s, True)
        batch(BATCH // 2 - 1, 0, True)
        batch(BATCH // 2 - 1, 1, False)

    def store_piece(eng, is_act, bp, s, k):
        which, j = kind(k)
        i, _ = piece_at(bp, s, k)
        out = bank[5 + i]
        b = bp * 2 + s
        eng.wait_ge(piece_done, b * PIECES + (k + 1))
        if which == "R":
            for c in range(2):
                last = eng.tensor_scalar(RT[:, c, :], out[0:RH * NB1, SEQ * c:SEQ * c + SEQ], br[:, c:c + 1], -1.0,
                                         ALU.add, ALU.mult)
            return last
        if which == "G":
            q, c, half = j // 4, (j % 4) // 2, j % 2
            if j % 4 < 2:
                eng.wait_ge(z_written, b * 32 + 16 * (q + 1))
            dst = G[:, q, RH * c + 4 * half:RH * c + 4 * half + 4, :]
            src = out.rearrange("p (h n) -> p h n", n=SPAN)
        elif which == "QK":
            qa = out[0:D1, 0:SEQ], Qz[s][0:D1, 2 * j, :], bq[0:D1, :, j:j + 1]
            qb = out[D1:P, 0:SEQ], Qz[s][D1:P, 2 * j + 1, :], bq[D1:P, :, j:j + 1]
            for src, dst, bias in (qa, qb):
                if is_act:
                    eng.activation(dst, src, ACT.Identity, bias=bias[:, 1, :], scale=-RSCALE)
                else:
                    eng.tensor_scalar(dst, src, bias[:, 0, :], -RSCALE, ALU.add, ALU.mult)
            dst, src = KT[s][:, j, :], out[:, SEQ:2 * SEQ]
        else:
            t, half = j // 2, j % 2
            dst, src = V[s][:, t, 512 * half:512 * half + 512], out
        return eng.activation(dst, src, ACT.Copy) if is_act else eng.tensor_copy(dst, src)

    def stored(eng, is_act, bp, s, k):
        which, _ = kind(k)
        i, _ = piece_at(bp, s, k)
        last = store_piece(eng, is_act, bp, s, k)
        last.then_inc(piece_read[i], 1)
        if which != "R":
            done = {("G", True): g_by_act, ("G", False): g_by_dve}.get((which, is_act), qkv_act if is_act else qkv_dve)
            eng.wait_ge(piece_read[i], piece_at(bp, s, k)[1] + 2)
            eng.sem_inc(done, 1)

    def scalar(act):
        ln.scalar(act)
        act.wait_ge(prep, 2)
        act.wait_ge(q_zero, 2)

        def pieces(bp, s, ks):
            for k in ks:
                if by_act(k):
                    stored(act, True, bp, s, k)

        def probabilities(b, h):
            act.wait_ge(l_ready, b * H1 + (h + 3))
            act.wait_ge(p_turned, b * H1 + (h + 1))
            act.activation(pr[:, h % 4, 0:P], L[:, h % 2, 0:P], ACT.Exp, bias=least[:, h % 2, 0:1], scale=-1.0,
                           accum_out=sums[:, h % 4, 0:1])
            act.activation(pr[:, h % 4, P:3 * P], L[:, h % 2, P:3 * P], ACT.Exp, bias=least[:, h % 2, 1:2], scale=-1.0,
                           accum_out=sums[:, h % 4, 1:2]).then_inc(p_ready, 1)

        def batch(bp, s, following):
            b = bp * 2 + s
            nbp, ns = (bp, 1) if s == 0 else (bp + 1, 0)
            for u in range(STEPS + 1):
                if u < H1:
                    probabilities(b, u)
                if 2 <= u < H1 + 2:
                    h = u - 2
                    act.wait_ge(p_turned, b * H1 + (h + 5))
                    act.wait_ge(pv_done, b * H1 + (h + 1))
                    act.activation(PT[:, h % 2, :], bank[2 + h % 2][:, 0:3 * P], ACT.Copy).then_inc(pT_ready, 1)
                if u >= 5 and u % 2:
                    c = (u - 5) // 2
                    act.wait_ge(pv_done, b * H1 + (2 * c + 4))
                    act.wait_ge(out_done, b + 1)
                    act.activation(AT[:, c, :], bank[4 + 3 * (c % 2)][:, 0:SEQ], ACT.Copy).then_inc(aT_ready, 1)
                if following and u < STEPS:
                    pieces(nbp, ns, plan[u])

        act.sem_inc(pT_ready, 2)
        act.sem_inc(aT_ready, 2)
        pieces(0, 0, range(PIECES))
        with act.Fori(0, BATCH // 2 - 1) as bp:
            for s in range(2):
                batch(bp, s, True)
        batch(BATCH // 2 - 1, 0, True)
        batch(BATCH // 2 - 1, 1, False)

    def vector(dve):
        ln.vector(dve)
        dve.wait_ge(loaded, 16 * 16)
        dve.tensor_scalar(bq[:, 1, :], bq[:, 0, :], -RSCALE, None, ALU.mult).then_inc(prep, 1)
        dve.wait_ge(q_zero, 2)
        dve.wait_ge(ln.xn_ready, TILES)
        dve.tensor_tensor(core.x[:, :, :], core.x[:, :, :],
                          bp_row[:, :].unsqueeze(1).to_broadcast([P, TILES, P]), ALU.add).then_inc(prep, 1)
        dve.wait_ge(prep, 2)

        def pieces(bp, s, ks):
            for k in ks:
                if not by_act(k):
                    stored(dve, False, bp, s, k)

        def logits(b, s, h):
            dve.wait_ge(s_done, b * H1 + (h + 1))
            dve.wait_ge(p_ready, b * H1 + (h + 1))
            if h == 0:
                dve.wait_ge(x_turned, b * 32 + 96)
            dve.sem_inc(l_begun, 1)
            S = bank[h % 2]
            dve.tensor_tensor_reduce(L[:, h % 2, 0:P], S[:, 0:P], X0[s][:, h, :], 1.0, 3.0e38, ALU.add, ALU.min,
                                     least[:, h % 2, 0:1])
            dve.tensor_tensor_reduce(L[:, h % 2, P:3 * P], S[:, P:3 * P], X1[s][:, h, :], 1.0, 3.0e38, ALU.add, ALU.min,
                                     least[:, h % 2, 1:2]).then_inc(l_ready, 1)

        def normalise(b, h):
            dve.wait_ge(p_ready, b * H1 + (h + 3))
            dve.reciprocal(rinv[:, h % 4, :], sums[:, h % 4, :]).then_inc(inv_ready, 1)
            dve.wait_ge(inv_ready, b * H1 + (h + 1))
            dve.tensor_scalar(pr[:, h % 4, 0:P], pr[:, h % 4, 0:P], rinv[:, h % 4, 0:1], None, ALU.mult)
            dve.tensor_scalar(pr[:, h % 4, P:3 * P], pr[:, h % 4, P:3 * P], rinv[:, h % 4, 1:2], None,
                              ALU.mult).then_inc(pn_ready, 1)

        def batch(bp, s, following):
            b = bp * 2 + s
            nbp, ns = (bp, 1) if s == 0 else (bp + 1, 0)
            for u in range(STEPS):
                if u < H1:
                    logits(b, s, u)
                if 1 <= u < H1 + 1:
                    normalise(b, u - 1)
                if following:
                    pieces(nbp, ns, plan[u])
            dve.wait_ge(out_done, b + 2)
            xb = core.x[:, ds(b * 2, 2), :]
            dve.tensor_tensor(xb, xb, bank[4][:, 0:SEQ].rearrange("p (t n) -> p t n", n=P), ALU.add).then_inc(out_added, 1)

        dve.sem_inc(l_ready, 2)
        dve.sem_inc(p_ready, 2)
        dve.sem_inc(out_added, 1)
        pieces(0, 0, range(PIECES))
        with dve.Fori(0, BATCH // 2 - 1) as bp:
            for s in range(2):
                batch(bp, s, True)
        batch(BATCH // 2 - 1, 0, True)
        batch(BATCH // 2 - 1, 1, False)

    return dict(sync=sync, gpsimd=gpsimd, tensor=tensor, scalar=scalar, vector=vector)


def build(nc, w, out, stages):
    with ExitStack() as ctx:
        core = Core(nc, ctx)
        make_constants = constants(core)
        x_loaded = core.sem("x_loaded")
        stored = core.sem("stored")
        stage_done = core.sem("stage_done")
        stage_cleared = core.sem("stage_cleared")
        made, sems = [], []
        for name, make in stages:
            with ExitStack() as local:
                core.ctx, core.stage_sems = local, []
                made.append(make(core, name, local, w))
                sems.append(core.stage_sems)
        block = ctx.enter_context(nc.Block())
        x_dram = w["x"].rearrange("(t p) d -> p t d", p=P)
        out_dram = out.rearrange("(t p) d -> p t d", p=P)

        def stage_end(eng, n):
            eng.drain().then_inc(stage_done, 1)
            if eng is nc.sync:
                eng.wait_ge(stage_done, 5 * (n + 1))
                for s in sems[n]:
                    eng.sem_clear(s)
                eng.sem_inc(stage_cleared, 1)
            eng.wait_ge(stage_cleared, n + 1)

        @block.sync
        def _(sp):
            sp.dma_start(core.x[:, :, :], x_dram).then_inc(x_loaded, 16)
            for n, st in enumerate(made):
                st["sync"](sp)
                stage_end(sp, n)
            sp.dma_start(out_dram, core.x[:, :, :]).then_inc(stored, 16)
            sp.wait_ge(stored, 16)

        @block.gpsimd
        def _(pool):
            make_constants(pool)
            for n, st in enumerate(made):
                st["gpsimd"](pool)
                stage_end(pool, n)

        @block.tensor
        def _(pe):
            pe.wait_ge(core.const_ready, 4)
            for n, st in enumerate(made):
                st["tensor"](pe)
                stage_end(pe, n)

        @block.scalar
        def _(act):
            for n, st in enumerate(made):
                st["scalar"](act)
                stage_end(act, n)

        @block.vector
        def _(dve):
            dve.wait_ge(x_loaded, 16)
            for n, st in enumerate(made):
                st["vector"](dve)
                stage_end(dve, n)


STAGES = [
    ("f0", mixture_zero), ("a0", attention_zero), ("g0", mixture_zero),
    ("f1", mixture_one), ("a1", attention_one), ("g1", mixture_one),
]


def rotary_tables():
    position = np.arange(SEQ, dtype=np.float32)[:, None]
    step = np.exp(np.arange(0, D0, 2, dtype=np.float32) * np.float32(-np.log(10000.0) / D0))
    angle = (position * step).astype(np.float32)
    sign = np.array([-1.0, 1.0] * (D0 // 2), np.float32)
    cos = np.repeat(np.cos(angle), 2, axis=1).astype(np.float32)
    sin = (np.repeat(np.sin(angle), 2, axis=1) * sign).astype(np.float32)
    lay = lambda a: np.ascontiguousarray(np.concatenate([a.reshape(2, P, D0).transpose(1, 0, 2)] * 2, axis=1))
    return lay(cos), lay(sin)


def kernel(**inputs):
    import concourse.bacc as bacc
    from concourse.bass_utils import run_bass_kernel_spmd

    i = {k: np.asarray(v) for k, v in inputs.items()}
    m, a = "L0_ffn_", "L1_attn_"
    cos, sin = rotary_tables()
    laid = {
        "x": i["L0_attn_x"].reshape(TOKENS, P),
        "router": i[m + "router_w"].T, "slot_number": np.arange(1, CAPACITY + 1, dtype=np.float32),
        "ws_gate_up": i[m + "ws_gate_up"], "ws_down": i[m + "ws_down"],
        "gate_up": np.concatenate([i[m + "w_gate"], i[m + "w_up"]], axis=2).transpose(1, 0, 2),
        "down": i[m + "w_down"].transpose(1, 0, 2),
        "w_qkv": i["L0_attn_w_qkv"].T.reshape(P, 3, P), "b_qkv": i["L0_attn_b_qkv"].reshape(3, P),
        "b_v": i["L0_attn_b_qkv"][2 * P:].reshape(P, 1), "w_lepe": i["L0_attn_w_lepe"].reshape(P, 3),
        "b_lepe": i["L0_attn_b_lepe"].reshape(P, 1), "rope_cos": cos, "rope_sin": sin,
        "Wg": i["L1_ffn_Wg"], "bg": i["L1_ffn_bg"], "W1": i["L1_ffn_W1"], "W2": i["L1_ffn_W2"], "b2": i["L1_ffn_b2"],
        "b1": i["L1_ffn_b1"].reshape(E1, FC1, P).transpose(2, 0, 1),
        "Wq": i[a + "Wq"], "Wk": i[a + "Wk"], "Wv": i[a + "Wv"], "Wproj": i[a + "Wproj"], "Wr": i[a + "Wr"],
        "bq": i[a + "bq"].reshape(CH, P).T, "br": i[a + "br"].reshape(2, RH * NB1).T, "bproj": i[a + "bproj"],
        "b_nd": i[a + "b_nd"][:, ::-1],
    }
    nc = bacc.Bacc("TRN2", target_bir_lowering=False, num_devices=1)
    arrays, w = {}, {}
    for name, value in laid.items():
        arrays[f"in_{name}"] = np.ascontiguousarray(value)
        w[name] = nc.dram_tensor(f"in_{name}", value.shape, F32, kind="ExternalInput").ap()
    out = nc.dram_tensor("out", (TOKENS, P), F32, kind="ExternalOutput").ap()
    build(nc, w, out, STAGES)
    r = run_bass_kernel_spmd(nc, [arrays], core_ids=[0])
    return r.results[0]["out"].reshape(BATCH, SEQ, P)
```

```python
from contextlib import ExitStack

import numpy as np
import concourse.bass as bass
from concourse import mybir

F32 = mybir.dt.float32
BF16 = mybir.dt.bfloat16
I32 = mybir.dt.int32
F32R = mybir.dt.float32r
ALU = mybir.AluOpType
ACT = mybir.ActivationFunctionType
AX = mybir.AxisListType
ds = bass.ds

P = 128
BATCH = 8
SEQ = 256
TOKENS = BATCH * SEQ
TILES = TOKENS // P
BLOCK = 512
EPS = 1e-5

E0, TOP0, F0, CAPACITY = 64, 8, 96, 64
E1, F1 = 8, 512
FC1 = F1 // P


class Chain:

    def __init__(self, sem, start=0):
        self.sem, self.n = sem, start

    def on(self, ins):
        self.n += 1
        ins.then_inc(self.sem, 1)
        return self.n


class Core:

    def __init__(self, nc, ctx):
        self.nc, self.ctx = nc, ctx
        self.stage_sems = []

    def sem(self, name):
        s = self.ctx.enter_context(self.nc.semaphore(name))
        self.stage_sems.append(s)
        return s


def bcast(ap, n):
    return ap.unsqueeze(len(ap.shape)).to_broadcast(list(ap.shape) + [n])


def constants(core):
    nc, ctx = core.nc, core.ctx
    core.x = ctx.enter_context(nc.sbuf_tensor("x", [P, TILES, P], F32))
    core.ident = ctx.enter_context(nc.sbuf_tensor("ident", [P, P], F32))
    core.identb = ctx.enter_context(nc.sbuf_tensor("identb", [P, P], BF16))
    core.tri = ctx.enter_context(nc.sbuf_tensor("tri", [P, P], BF16))
    core.ones = ctx.enter_context(nc.sbuf_tensor("ones", [P, P], BF16))
    core.psum = ctx.enter_context(nc.psum_tensor("psum", [P, 8, 512], F32))
    core.bank = [core.psum[:, i, :] for i in range(8)]
    core.const_filled = core.sem("const_filled")
    core.const_ready = core.sem("const_ready")

    def pool(eng):
        eng.memset(core.ident[:, :], 0.0).then_inc(core.const_filled, 1)
        eng.memset(core.identb[:, :], 0.0).then_inc(core.const_filled, 1)
        eng.memset(core.tri[:, :], 1.0).then_inc(core.const_filled, 1)
        eng.memset(core.ones[:, :], 1.0).then_inc(core.const_ready, 1)
        eng.wait_ge(core.const_filled, 3)
        for m in (core.ident, core.identb):
            eng.affine_select(out=m[:, :], in_=m[:, :], compare_op=ALU.not_equal, fill=1.0,
                              base=0, pattern=[[-1, P]], channel_multiplier=1).then_inc(core.const_ready, 1)
        eng.affine_select(out=core.tri[:, :], in_=core.tri[:, :], compare_op=ALU.is_ge, fill=0.0,
                          base=0, pattern=[[1, P]], channel_multiplier=-1).then_inc(core.const_ready, 1)

    return pool


class LayerNorm:

    def __init__(self, core, ctx, name):
        nc = core.nc
        self.core = core
        sb = lambda n, s, d=F32: ctx.enter_context(nc.sbuf_tensor(f"{name}_{n}", s, d))
        self.xn = sb("xn", [P, TILES, P])
        self.xnT = sb("xnT", [P, TOKENS])
        self.moments = sb("moments", [P, TILES, 6])
        self.mean_var = sb("mean_var", [P, TILES, 2])
        self.ve = sb("ve", [P, TILES])
        self.std = sb("std", [P, TILES])
        self.rstd = sb("rstd", [P, TILES])
        self.newton = sb("newton", [P, TILES])
        self.ps = core.bank[0:4]
        self.chain = core.sem(f"{name}_ln_chain")
        self.var_ready = core.sem(f"{name}_var_ready")
        self.std_ready = core.sem(f"{name}_std_ready")
        self.xn_ready = core.sem(f"{name}_xn_ready")
        self.turned = core.sem(f"{name}_turned")
        self.xnT_ready = core.sem(f"{name}_xnT_ready")

    def vector(self, dve):
        c = Chain(self.chain)

        def step(ins):
            dve.wait_ge(c.sem, c.on(ins))

        x = self.core.x
        for t in range(TILES):
            last = dve.bn_stats(self.moments[:, t, :], x[:, t, :])
        step(last)
        for t in range(TILES):
            last = dve.bn_aggr(self.mean_var[:, t, :], self.moments[:, t, :])
        step(last)
        ve, rstd, t = self.ve[:, :], self.rstd[:, :], self.newton[:, :]
        dve.tensor_scalar(ve, self.mean_var[:, :, 1], EPS, None, ALU.add).then_inc(self.var_ready, 1)
        dve.wait_ge(self.std_ready, 1)
        step(dve.reciprocal(rstd, self.std[:, :]))
        step(dve.tensor_tensor(t, rstd, rstd, ALU.mult))
        step(dve.tensor_tensor(t, t, ve, ALU.mult))
        step(dve.tensor_scalar(t, t, -0.5, 1.5, ALU.mult, ALU.add))
        step(dve.tensor_tensor(rstd, rstd, t, ALU.mult))
        for t in range(TILES):
            dve.tensor_scalar(self.xn[:, t, :], x[:, t, :], self.mean_var[:, t, 0:1], self.rstd[:, t:t + 1],
                              ALU.subtract, ALU.mult).then_inc(self.xn_ready, 1)

    def tensor(self, pe):
        for t in range(TILES):
            pe.wait_ge(self.xn_ready, t + 1)
            last = pe.transpose(self.ps[t // 4][:, P * (t % 4):P * (t % 4) + P], self.xn[:, t, :],
                                self.core.ident[:, :])
            if t % 4 == 3:
                last.then_inc(self.turned, 1)

    def scalar(self, act):
        act.wait_ge(self.var_ready, 1)
        act.activation(self.std[:, :], self.ve[:, :], ACT.Sqrt).then_inc(self.std_ready, 1)
        for q in range(4):
            act.wait_ge(self.turned, q + 1)
            act.activation(self.xnT[:, 512 * q:512 * q + 512], self.ps[q][:, :], ACT.Copy).then_inc(self.xnT_ready, 1)


def high_part(copy, out, value):
    return copy(out.bitcast(F32R), value)


def rest_part(eng, out, value, high):
    return eng.tensor_tensor(out.bitcast(F32R), value, high, ALU.subtract)


def matmul_by_parts(pe, out, lhs, rhs, start, stop):
    lhs, rhs = [a.bitcast(F32R) for a in lhs], [a.bitcast(F32R) for a in rhs]
    pe.matmul(out, lhs[1], rhs[0], start=start, stop=False)
    pe.matmul(out, lhs[0], rhs[1], start=False, stop=False)
    return pe.matmul(out, lhs[0], rhs[0], start=False, stop=stop)


def mixture_one(core, name, ctx, w):
    nc = core.nc
    sb = lambda n, s, d=F32: ctx.enter_context(nc.sbuf_tensor(f"{name}_{n}", s, d))
    ln = LayerNorm(core, ctx, name)
    bank = core.bank
    NB = TOKENS // BLOCK
    SLOTS = 2
    LAG = 1
    RAW = 4
    W3 = 3 * E1
    wg = sb("wg", [P, E1])
    bg = sb("bg", [P, E1])
    w1 = sb("w1", [P, RAW, F1])
    w1h = sb("w1h", [P, E1, F1])
    w1l = sb("w1l", [P, E1, F1])
    w2 = sb("w2", [P, RAW, FC1 * P])
    w2h = sb("w2h", [P, E1, FC1 * P])
    w2l = sb("w2l", [P, E1, FC1 * P])
    xh = sb("xh", [P, TOKENS])
    xl = sb("xl", [P, TOKENS])
    b1 = sb("b1", [P, E1, FC1])
    b2 = sb("b2", [W3, P])
    b2rest = sb("b2rest", [W3, P])
    b2part = sb("b2part", [P, 3, P], BF16)
    logit = sb("logit", [P, TILES, E1])
    prob = sb("prob", [P, TILES, E1])
    weight = sb("weight", [P, TILES, E1])
    wrest = sb("wrest", [P, TILES, E1])
    wpart = sb("wpart", [P, TILES, W3], BF16)
    wT = sb("wT", [P, TOKENS], BF16)
    select = sb("select", [P, E1, P], BF16)
    cmp = sb("cmp", [P, TILES, E1, E1])
    eqs = sb("eqs", [P, TILES, E1, E1])
    lower = sb("lower", [P, E1, E1])
    col = sb("col", [P, 3, TILES])
    h = sb("h", [P, SLOTS, FC1, BLOCK])
    hh = sb("hh", [P, SLOTS, FC1, BLOCK])
    hl = sb("hl", [P, SLOTS, FC1, BLOCK])
    yT = sb("yT", [P, BLOCK])
    ps_w, ps_y, ps_t = bank[4:6], bank[6], bank[7]
    ps_logit = bank[7].rearrange("p (a n) -> p a n", a=4)
    sem = lambda n: core.sem(f"{name}_{n}")
    loaded = sem("loaded")
    w_loaded = [sem(f"w_loaded{e}") for e in range(E1)]
    w_high = sem("w_high")
    w_rest = sem("w_rest")
    x_cut = sem("x_cut")
    filled = sem("filled")
    consts = sem("consts")
    logits_done = sem("logits_done")
    shifted = sem("shifted")
    exp_done = sem("exp_done")
    weights_ready = sem("weights_ready")
    chain = sem("chain")
    wT_turned = sem("wT_turned")
    wT_ready = sem("wT_ready")
    w_spread = sem("w_spread")
    h_done = sem("h_done")
    relu_done = sem("relu_done")
    h_weighted = sem("h_weighted")
    h_high = sem("h_high")
    rest_pool = sem("rest_pool")
    rest_dve = sem("rest_dve")
    down_done = sem("down_done")
    y_copied = sem("y_copied")
    y_turned = sem("y_turned")
    y_added = sem("y_added")
    POOLED = FC1 - 1

    def following(b, e):
        return (b, e + LAG) if e + LAG < E1 else (b + 1, e + LAG - E1)

    def sync(sp):
        sp.dma_start(wg[:, :], w["Wg"]).then_inc(loaded, 16)
        sp.dma_start(bg[:, :], w["bg"].unsqueeze(0).to_broadcast([P, E1])).then_inc(loaded, 16)
        sp.dma_start(b1[:, :, :], w["b1"]).then_inc(loaded, 16)
        for i in range(3):
            sp.dma_start(b2[E1 * i:E1 * i + E1, :], w["b2"]).then_inc(loaded, 16)
        for e in range(E1):
            if e >= RAW:
                sp.wait_ge(w_rest, 2 * (e - RAW + 1))
            sp.dma_start(w1[:, e % RAW, :], w["W1"][e]).then_inc(w_loaded[e], 16)
            sp.dma_start(w2[:, e % RAW, :].rearrange("p (c d) -> p c d", d=P),
                         w["W2"][e].rearrange("(c p) d -> p c d", p=P)).then_inc(w_loaded[e], 16)

    def gpsimd(pool):
        pool.memset(lower[:, :, :], 1.0).then_inc(filled, 1)
        pool.memset(select[:, :, :], 0.0).then_inc(filled, 1)
        pool.memset(wT[:, :], 0.0).then_inc(consts, 1)
        pool.memset(b2part[:, :, :], 0.0).then_inc(consts, 1)
        pool.wait_ge(filled, 2)
        pool.affine_select(out=lower[:, :, :], in_=lower[:, :, :], compare_op=ALU.is_gt, fill=0.0,
                           base=0, pattern=[[1, E1], [-1, E1]], channel_multiplier=0).then_inc(consts, 1)
        for i in range(3):
            pool.wait_ge(filled, 2 + i)
            pool.affine_select(out=select[:, :, :], in_=select[:, :, :], compare_op=ALU.not_equal, fill=1.0,
                               base=-E1 * i, pattern=[[-1, E1], [0, P]], channel_multiplier=1).then_inc(filled, 1)
        for e in range(E1):
            pool.wait_ge(w_high, e + 1)
            for full, high, low in ((w1, w1h, w1l), (w2, w2h, w2l)):
                rest_part(pool, low[:, e, :], full[:, e % RAW, :], high[:, e, :]).then_inc(w_rest, 1)

        def rest(b, e):
            for c in range(POOLED):
                pool.wait_ge(h_high, b * (E1 * FC1) + (e * FC1 + c + 1))
                rest_part(pool, hl[:, e % SLOTS, c, :], h[:, e % SLOTS, c, :],
                          hh[:, e % SLOTS, c, :]).then_inc(rest_pool, 1)

        for e in range(LAG):
            rest(0, e)
        with pool.Fori(0, NB - 1) as b:
            for e in range(E1):
                rest(*following(b, e))
        for e in range(LAG, E1):
            rest(NB - 1, e)

    def tensor(pe):
        ln.tensor(pe)
        pe.wait_ge(loaded, 6 * 16)
        for q in range(4):
            pe.wait_ge(ln.xnT_ready, q + 1)
            for i in range(4 * q, 4 * q + 4):
                last = pe.matmul(ps_logit[:, i // 4, E1 * (i % 4):E1 * (i % 4) + E1], ln.xnT[:, P * i:P * i + P],
                                 wg[:, :], start=True, stop=True)
        last.then_inc(logits_done, 1)

        def hidden(b, e):
            if isinstance(b, int) and b == 0:
                pe.wait_ge(w_rest, 2 * e + 1)
            x = [t[:, ds(b * BLOCK, BLOCK)] for t in (xh, xl)]
            for c in range(FC1):
                pe.wait_ge(relu_done, b * (E1 * FC1) + (e * FC1 + c + 1))
                wc = [t[:, e, P * c:P * c + P] for t in (w1h, w1l)]
                matmul_by_parts(pe, bank[c], wc, x, True, True).then_inc(h_done, 1)

        def spread(b, e):
            pe.wait_ge(h_weighted, b * (E1 * FC1) + (e * FC1 + FC1))
            pe.matmul(ps_w[e % 2], select[:, e, :], wT[:, ds(b * BLOCK, BLOCK)], start=True, stop=True).then_inc(w_spread, 1)

        def down(b, e):
            if e == 0:
                pe.wait_ge(y_copied, b + 1)
                for i in range(3):
                    pe.matmul(ps_y, b2part[:, i, :], wT[:, ds(b * BLOCK, BLOCK)], start=(i == 0), stop=False)
            for c in range(FC1):
                if c < POOLED:
                    pe.wait_ge(rest_pool, b * (E1 * POOLED) + (e * POOLED + c + 1))
                else:
                    pe.wait_ge(rest_dve, b * E1 + (e + 1))
                wc = [t[:, e, P * c:P * c + P] for t in (w2h, w2l)]
                hc = [t[:, e % SLOTS, c, :] for t in (hh, hl)]
                last = matmul_by_parts(pe, ps_y, wc, hc, False, e == E1 - 1 and c == FC1 - 1)
            last.then_inc(down_done, 1)

        def turn(b):
            pe.wait_ge(y_copied, b + 2)
            pe.wait_ge(y_added, b + 1)
            for t in range(4):
                last = pe.transpose(ps_t[:, P * t:P * t + P], yT[:, P * t:P * t + P], core.ident[:, :])
            last.then_inc(y_turned, 1)

        pe.sem_inc(relu_done, 4)
        pe.sem_inc(down_done, SLOTS)
        pe.sem_inc(h_weighted, 2 * FC1)
        pe.sem_inc(y_copied, 1)
        pe.sem_inc(y_turned, 1)
        pe.sem_inc(y_added, 1)
        pe.wait_ge(x_cut, 2)
        for e in range(LAG):
            hidden(0, e)
        pe.wait_ge(weights_ready, 1)
        for q in range(4):
            for i in range(4):
                last = pe.transpose(bank[4 + q].bitcast(BF16)[0:W3, P * i:P * i + P], wpart[:, 4 * q + i, :],
                                    core.identb[:, :])
            last.then_inc(wT_turned, 1)
        pe.wait_ge(filled, 5)
        pe.wait_ge(wT_ready, 4)
        for e in range(LAG):
            spread(0, e)
        pe.wait_ge(w_rest, 2 * E1)

        def block(b, first, last):
            for e in range(E1):
                if not last or e + LAG < E1:
                    spread(*following(b, e))
                    hidden(*following(b, e))
                if e == 0 and not first:
                    turn(b - 1)
                down(b, e)

        block(0, True, False)
        with pe.Fori(0, NB - 2) as i:
            block(i + 1, False, False)
        block(NB - 1, False, True)
        turn(NB - 1)

    def scalar(act):
        def copy(out, in_):
            return act.activation(out, in_, ACT.Copy)

        def high_parts(experts):
            for e in experts:
                act.wait_ge(w_loaded[e], 32)
                high_part(copy, w1h[:, e, :], w1[:, e % RAW, :])
                high_part(copy, w2h[:, e, :], w2[:, e % RAW, :]).then_inc(w_high, 1)

        ln.scalar(act)
        act.wait_ge(ln.xnT_ready, 4)
        high_part(copy, xh[:, :], ln.xnT[:, :]).then_inc(x_cut, 1)
        high_parts(range(1))
        act.wait_ge(shifted, 1)
        act.activation(prob[:, :, :], logit[:, :, :], ACT.Exp).then_inc(exp_done, 1)
        high_parts(range(1, RAW))

        def relu(b, e):
            act.wait_ge(down_done, b * E1 + (e + 1))
            for c in range(FC1):
                act.wait_ge(h_done, b * (E1 * FC1) + (e * FC1 + c + 1))
                act.activation(h[:, e % SLOTS, c, :], bank[c], ACT.Relu, bias=b1[:, e, c:c + 1]).then_inc(relu_done, 1)

        def copy_out(b):
            act.wait_ge(down_done, b * E1 + (E1 + SLOTS))
            act.wait_ge(y_turned, b + 1)
            act.activation(yT[:, :], ps_y, ACT.Copy).then_inc(y_copied, 1)

        for e in range(LAG):
            relu(0, e)
        high_parts(range(RAW, E1))
        act.wait_ge(consts, 3)
        for q in range(4):
            act.wait_ge(wT_turned, q + 1)
            act.activation(wT[0:W3, BLOCK * q:BLOCK * q + BLOCK], bank[4 + q].bitcast(BF16)[0:W3, 0:BLOCK],
                           ACT.Copy).then_inc(wT_ready, 1)
        with act.Fori(0, NB - 1) as b:
            for e in range(E1):
                relu(*following(b, e))
            copy_out(b)
        for e in range(LAG, E1):
            relu(NB - 1, e)
        copy_out(NB - 1)

    def vector(dve):
        ln.vector(dve)
        c_ = Chain(chain)

        def step(ins):
            dve.wait_ge(c_.sem, c_.on(ins))

        total, den, top = (col[:, i, :] for i in range(3))
        dve.wait_ge(logits_done, 1)
        step(dve.tensor_tensor(logit[:, :, :].rearrange("p (a b) e -> p a b e", b=4),
                               ps_logit[:, :, 0:4 * E1].rearrange("p a (b e) -> p a b e", b=4),
                               bg[:, :].unsqueeze(1).unsqueeze(1).to_broadcast([P, 4, 4, E1]), ALU.add))
        step(dve.tensor_reduce(total, logit[:, :, :], AX.X, ALU.max))
        dve.tensor_tensor(logit[:, :, :], logit[:, :, :], bcast(total, E1), ALU.subtract).then_inc(shifted, 1)
        dve.wait_ge(x_cut, 1)
        rest_part(dve, xl[:, :], ln.xnT[:, :], xh[:, :]).then_inc(x_cut, 1)
        dve.wait_ge(exp_done, 1)
        step(dve.tensor_reduce(total, prob[:, :, :], AX.X, ALU.add))
        step(dve.reciprocal(den, total))
        step(dve.tensor_tensor(prob[:, :, :], prob[:, :, :], bcast(den, E1), ALU.mult))
        mine = bcast(prob[:, :, :], E1)
        others = prob[:, :, :].unsqueeze(2).to_broadcast([P, TILES, E1, E1])
        step(dve.tensor_tensor(cmp[:, :, :, :], others, mine, ALU.is_gt))
        step(dve.tensor_tensor(eqs[:, :, :, :], others, mine, ALU.is_equal))
        dve.wait_ge(consts, 3)
        step(dve.tensor_tensor(eqs[:, :, :, :], eqs[:, :, :, :],
                               lower[:, :, :].unsqueeze(1).to_broadcast([P, TILES, E1, E1]), ALU.mult))
        step(dve.tensor_tensor(cmp[:, :, :, :], cmp[:, :, :, :], eqs[:, :, :, :], ALU.add))
        step(dve.tensor_reduce(weight[:, :, :], cmp[:, :, :, :], AX.X, ALU.add))
        step(dve.scalar_tensor_tensor(weight[:, :, :], weight[:, :, :], 2.0, prob[:, :, :], ALU.is_lt, ALU.mult))
        step(dve.tensor_reduce(top, weight[:, :, :], AX.X, ALU.add))
        step(dve.tensor_scalar(top, top, 1e-9, None, ALU.add))
        step(dve.reciprocal(den, top))
        step(dve.tensor_scalar(den, den, 0.5, None, ALU.mult))
        step(dve.tensor_tensor(weight[:, :, :], weight[:, :, :], bcast(den, E1), ALU.mult))
        dve.wait_ge(loaded, 6 * 16)
        for value, rest, parts in (
                (weight[:, :, :], wrest[:, :, :], [wpart[:, :, E1 * i:E1 * i + E1] for i in range(3)]),
                (b2[:, :], b2rest[:, :], [b2part[0:W3, i, :] for i in range(3)])):
            step(dve.tensor_copy(parts[0], value))
            step(dve.tensor_tensor(rest, value, parts[0], ALU.subtract))
            step(dve.tensor_copy(parts[1], rest))
            step(dve.tensor_tensor(parts[2], rest, parts[1], ALU.subtract))
        dve.sem_inc(weights_ready, 1)

        def weigh_and_cut(b, e):
            at = b * (E1 * FC1)
            dve.wait_ge(w_spread, b * E1 + (e + 1))

            def weigh(c):
                dve.wait_ge(relu_done, at + (e * FC1 + c + 5))
                hc = h[:, e % SLOTS, c, :]
                dve.tensor_tensor(hc, hc, ps_w[e % 2], ALU.mult).then_inc(h_weighted, 1)

            def cut(c):
                dve.wait_ge(h_weighted, at + (e * FC1 + c + 1 + 2 * FC1))
                high_part(dve.tensor_copy, hh[:, e % SLOTS, c, :], h[:, e % SLOTS, c, :]).then_inc(h_high, 1)

            weigh(0)
            for c in range(FC1):
                if c + 1 < FC1:
                    weigh(c + 1)
                cut(c)
            dve.wait_ge(h_high, at + (e * FC1 + FC1))
            c = FC1 - 1
            rest_part(dve, hl[:, e % SLOTS, c, :], h[:, e % SLOTS, c, :], hh[:, e % SLOTS, c, :]).then_inc(rest_dve, 1)

        def add(b):
            dve.wait_ge(y_turned, b + 2)
            xb = core.x[:, ds(b * 4, 4), :]
            dve.tensor_tensor(xb, xb, ps_t.rearrange("p (t n) -> p t n", n=P), ALU.add).then_inc(y_added, 1)

        for e in range(LAG):
            weigh_and_cut(0, e)

        def block(b, first, last):
            for e in range(E1):
                if not last or e + LAG < E1:
                    weigh_and_cut(*following(b, e))
                if e == 0 and not first:
                    add(b - 1)

        block(0, True, False)
        with dve.Fori(0, NB - 2) as i:
            block(i + 1, False, False)
        block(NB - 1, False, True)
        add(NB - 1)

    return dict(sync=sync, gpsimd=gpsimd, tensor=tensor, scalar=scalar, vector=vector)


def mixture_zero(core, name, ctx, w):
    nc = core.nc
    sb = lambda n, s, d=F32: ctx.enter_context(nc.sbuf_tensor(f"{name}_{n}", s, d))
    ln = LayerNorm(core, ctx, name)
    bank = core.bank
    PAIRS = E0 // 2
    WP = 4
    ROUNDS = PAIRS // (2 * WP)
    WE = 4
    WSLOTS = 4 * WP // WE
    CE = BLOCK // CAPACITY
    CHUNKS = E0 // CE
    HALF = CHUNKS // 2
    DEPTH = 4
    RING = 4
    wr = sb("wr", [P, E0])
    wsgu = sb("wsgu", [P, 2 * F0])
    wsd = sb("wsd", [F0, P])
    number = sb("number", [P, CAPACITY])
    wgu = [sb(f"wgu{i}", [P, WE, 2 * F0]) for i in range(WSLOTS)]
    wd = [sb(f"wd{i}", [F0, WE, P]) for i in range(WSLOTS)]
    ex = sb("ex", [P, TILES, E0])
    repl = sb("repl", [P, TILES, E0])
    mask = sb("mask", [P, TILES, E0], BF16)
    weight = sb("weight", [P, TILES, E0])
    base = sb("base", [P, TILES, E0])
    place = sb("place", [P, TILES + 1, E0], BF16)
    top = sb("top", [P, TILES, TOP0])
    col = sb("col", [P, 2, TILES])
    room = sb("room", [1, 2, TILES])
    count_f = sb("count_f", [1, 1])
    count = sb("count", [1, 1], I32)
    zeros = sb("zeros", [P, BLOCK], BF16)
    xpart = sb("xpart", [P, 3, TILES, P], BF16)
    xrest = sb("xrest", [P, TILES, P])
    wpart = sb("wpart", [P, TILES, E0, 3], BF16)
    wrest = sb("wrest", [P, TILES, E0])
    S = sb("S", [P, RING, BLOCK], BF16)
    XT = sb("XT", [P, E0 * CAPACITY])
    wboth = sb("wboth", [P, PAIRS, 2])
    wslot = sb("wslot", [P, PAIRS])
    act_s = sb("act_s", [F0, 2, BLOCK])
    hT = sb("hT", [F0, 2, BLOCK])
    ys = sb("ys", [P, PAIRS, P])
    ypart = sb("ypart", [P, PAIRS, 2, P])
    ST = sb("ST", [P, RING, BLOCK])
    summed = sb("summed", [P, P])
    sem = lambda n: core.sem(f"{name}_{n}")
    loaded = sem("loaded")
    filled = sem("filled")
    logits_done = sem("logits_done")
    shifted = sem("shifted")
    exp_done = sem("exp_done")
    mask_ready = sem("mask_ready")
    counted = sem("counted")
    chain = sem("chain")
    count_ready = sem("count_ready")
    weights_ready = sem("weights_ready")
    rounded = sem("rounded")
    cut = sem("cut")
    sh_gu = sem("sh_gu")
    sh_silu = sem("sh_silu")
    sh_h = sem("sh_h")
    sh_y = sem("sh_y")
    sh_added = sem("sh_added")
    s_made = [sem(f"s_made{i}") for i in range(2)]
    s_used = [sem(f"s_used{i}") for i in range(2)]
    gathered = sem("gathered")
    xt_ready = sem("xt_ready")
    wslot_ready = sem("wslot_ready")
    w_loaded = [sem(f"w_loaded{i}") for i in range(WSLOTS)]
    gu_done = sem("gu_done")
    silu_done = sem("silu_done")
    h_ready = sem("h_ready")
    y_done = sem("y_done")
    ys_ready = sem("ys_ready")
    y_rounded = sem("y_rounded")
    y_cut = sem("y_cut")
    c_made = sem("c_made")
    c_turned = sem("c_turned")
    st_ready = sem("st_ready")
    combined = sem("combined")
    sum_read = sem("sum_read")
    x_added = sem("x_added")

    three_parts = ((ln.xn[:, :, :], xrest[:, :, :], [xpart[:, i, :, :] for i in range(3)]),
                   (weight[:, :, :], wrest[:, :, :], [wpart[:, :, :, i] for i in range(3)]))

    def gu_bank(j):
        return bank[(0, 1, 5, 6)[j % DEPTH]]

    def slot(buffer, j):
        return buffer[:, 0, P * (j % DEPTH):P * (j % DEPTH) + P]

    def own_slots(ap):
        return ap.rearrange("p (e n) -> p e n", n=CAPACITY)

    def diagonal(ap):
        return ap.rearrange("p (k n) -> p k n", n=CAPACITY)[:, 0::3, :]

    def sync(sp):
        sp.dma_start(wr[:, :], w["router"]).then_inc(loaded, 16)
        sp.dma_start(wsgu[:, :], w["ws_gate_up"]).then_inc(loaded, 16)
        sp.dma_start(wsd[:, :], w["ws_down"]).then_inc(loaded, 16)
        sp.dma_start(number[:, :], w["slot_number"].unsqueeze(0).to_broadcast([P, CAPACITY])).then_inc(loaded, 16)
        LP = WE // 2

        def load(r, s):
            at = r * (WSLOTS * WE) + s * WE
            sp.dma_start(wgu[s][:, :, :], w["gate_up"][:, ds(at, WE), :]).then_inc(w_loaded[s], 16)
            sp.dma_start(wd[s][:, :, :], w["down"][:, ds(at, WE), :]).then_inc(w_loaded[s], 16)

        for s in range(WSLOTS):
            load(0, s)
        with sp.Fori(0, ROUNDS - 1) as r:
            for s in range(WSLOTS):
                sp.wait_ge(y_done, r * (2 * WP) + (LP * (s + 1) + DEPTH))
                load(r + 1, s)

    def gpsimd(pool):
        pool.memset(zeros[:, :], 0.0).then_inc(filled, 1)
        pool.memset(place[:, TILES, :], 0.0).then_inc(filled, 1)
        for i, (value, rest, parts) in enumerate(three_parts):
            for k, (full, out) in enumerate(((value, rest), (rest, parts[2]))):
                pool.wait_ge(rounded, 2 * i + (k + 1))
                pool.tensor_tensor(out, full, parts[k], ALU.subtract).then_inc(cut, 1)

        for g in range(PAIRS // WP):
            pool.wait_ge(y_rounded, g + 1)
            p = slice(WP * g, WP * g + WP)
            rest_part(pool, ypart[:, p, 1, :], ys[:, p, :], ypart[:, p, 0, :]).then_inc(y_cut, 1)

    def tensor(pe):
        ln.tensor(pe)
        pe.wait_ge(loaded, 64)
        for q in range(4):
            pe.wait_ge(ln.xnT_ready, q + 1)
            for i in range(4 * q, 4 * q + 4):
                last = pe.matmul(bank[4 + i // 8][:, E0 * (i % 8):E0 * (i % 8) + E0], ln.xnT[:, P * i:P * i + P],
                                 wr[:, :], start=True, stop=True)
        last.then_inc(logits_done, 1)

        def shared(q):
            gate, up = bank[2 * (q % 2)], bank[2 * (q % 2) + 1]
            xq = ln.xnT[:, BLOCK * q:BLOCK * q + BLOCK]
            if q >= 2:
                pe.wait_ge(sh_added, q - 1)
            pe.matmul(gate[0:F0, :], wsgu[:, 0:F0], xq, start=True, stop=True)
            pe.matmul(up[0:F0, :], wsgu[:, F0:2 * F0], xq, start=True, stop=True).then_inc(sh_gu, 1)

        def shared_out(q):
            pe.wait_ge(sh_h, q + 1)
            for t in range(4):
                last = pe.matmul(bank[2 * (q % 2)][:, P * t:P * t + P], hT[:, q % 2, P * t:P * t + P], wsd[:, :],
                                 start=True, stop=True)
            last.then_inc(sh_y, 1)

        shared(0)
        shared(1)
        shared_out(0)
        shared(2)
        shared_out(1)
        pe.wait_ge(mask_ready, 1)
        for h in range(2):
            m = mask[:, 8 * h:8 * h + 8, :].rearrange("p t e -> p (t e)")
            pe.matmul(bank[4 + h], core.tri[:, :], m, start=True, stop=True)
            last = pe.matmul(bank[6 + h], core.ones[:, :], m, start=True, stop=True)
        last.then_inc(counted, 1)
        shared_out(2)
        shared(3)
        shared_out(3)

        pe.wait_ge(sh_added, 4)
        pe.wait_ge(filled, 2)
        pe.wait_ge(cut, 2)
        pe.wait_ge(count_ready, 1)
        n = pe.value_load(count[0:1, 0:1], min_val=1, max_val=TILES)
        lhs0 = zeros[:, 0:P]
        pe.matmul(bank[4], lhs0, zeros[:, :], start=True, stop=False, skip_group_check=True)
        pe.wait_ge(cut, 4)
        for half in range(2):
            for k in range(HALF):
                if half:
                    pe.wait_ge(xt_ready, k + 1)
                pe.matmul(bank[k], lhs0, zeros[:, :], start=True, stop=False, skip_group_check=True)
            pe.sem_inc(s_used[half], RING)
            with pe.Fori(0, n) as t:
                for k in range(HALF):
                    pe.wait_ge(s_made[half], t * HALF + (k + 1))
                    for i in range(3):
                        pe.matmul(bank[k], xpart[:, i, ds(t, 1), :].rearrange("p t n -> p (t n)"), S[:, k, :],
                                  start=False, stop=False, skip_group_check=True)
                    for j in range(WP):
                        p = (half * HALF + k) * WP + j
                        rhs = wpart[:, ds(t, 1), 2 * p:2 * p + 2, :].rearrange("p t e i -> p (t e i)")
                        last = pe.matmul(bank[4][:, 6 * p:6 * p + 6], S[:, k, P * j:P * j + P], rhs,
                                         start=False, stop=False, skip_group_check=True)
                    last.then_inc(s_used[half], 1)
            for k in range(HALF):
                pe.matmul(bank[k], lhs0, zeros[:, :], start=False, stop=True, skip_group_check=True).then_inc(gathered, 1)
        pe.matmul(bank[4], lhs0, zeros[:, :], start=False, stop=True, skip_group_check=True).then_inc(gathered, 1)

        pe.wait_ge(xt_ready, 2 * HALF)
        pe.sem_inc(h_ready, DEPTH)
        pe.sem_inc(y_done, DEPTH)
        pe.sem_inc(ys_ready, 2)
        with pe.Fori(0, ROUNDS) as r:
            at = r * (2 * WP)

            def gate_up(j):
                s, e = 2 * j // WE, 2 * j % WE
                if e == 0:
                    pe.wait_ge(w_loaded[s], r * 32 + 32)
                pe.wait_ge(h_ready, at + (j + 1))
                moving = XT[:, ds(at * P + j * P, P)]
                for i in range(4):
                    lhs = wgu[s][:, e + i % 2, F0 * (i // 2):F0 * (i // 2) + F0]
                    last = pe.matmul(gu_bank(j)[0:F0, P * i:P * i + P], lhs, moving, start=True, stop=True)
                last.then_inc(gu_done, 1)

            gate_up(0)
            gate_up(1)
            for j in range(2 * WP):
                if j + 2 < 2 * WP:
                    gate_up(j + 2)
                pe.wait_ge(h_ready, at + (j + DEPTH + 1))
                if j % WP == 0:
                    pe.wait_ge(ys_ready, r * 2 + (j // WP + 1))
                for i in range(2):
                    last = pe.matmul(bank[2 + j // WP][CAPACITY * i:CAPACITY * i + CAPACITY, P * (j % WP):P * (j % WP) + P],
                                     slot(hT, j)[:, CAPACITY * i:CAPACITY * i + CAPACITY],
                                     wd[2 * j // WE][:, 2 * j % WE + i, :],
                                     start=True, stop=True)
                last.then_inc(y_done, 1)

        pe.wait_ge(wslot_ready, 1)
        pe.wait_ge(ys_ready, PAIRS // WP + 2)
        pe.sem_inc(combined, RING)
        pe.sem_inc(sum_read, 1)
        pe.sem_inc(c_turned, RING)
        pe.sem_inc(st_ready, RING)
        with pe.Fori(0, n) as t:
            def turn(k):
                pe.wait_ge(c_made, t * CHUNKS + (k + 1))
                pe.wait_ge(st_ready, t * CHUNKS + (k + 1))
                for j in range(WP):
                    last = pe.transpose(bank[k % RING].bitcast(BF16)[:, P * j:P * j + P],
                                        S[:, k % RING, P * j:P * j + P], core.identb[:, :])
                last.then_inc(c_turned, 1)

            def combine(k):
                pe.wait_ge(st_ready, t * CHUNKS + (k + RING + 1))
                pe.wait_ge(y_cut, k + 1)
                if k == 0:
                    pe.wait_ge(sum_read, t + 1)
                for j in range(WP):
                    p = k * WP + j
                    last = pe.matmul(bank[6][:, 0:2 * P], ST[:, k % RING, P * j:P * j + P].bitcast(F32R),
                                     ypart[:, p, :, :].rearrange("p i n -> p (i n)").bitcast(F32R),
                                     start=(p == 0), stop=(p == PAIRS - 1))
                last.then_inc(combined, 1)

            turn(0)
            turn(1)
            for k in range(CHUNKS):
                if k + 2 < CHUNKS:
                    turn(k + 2)
                combine(k)

    def scalar(act):
        def copy(out, in_):
            return act.activation(out, in_, ACT.Copy)

        ln.scalar(act)
        act.wait_ge(ln.xn_ready, TILES)
        copy(xpart[:, 0, :, :], ln.xn[:, :, :]).then_inc(rounded, 1)
        act.wait_ge(shifted, 1)
        act.activation(ex[:, :, :], ex[:, :, :], ACT.Exp).then_inc(exp_done, 1)

        def round_part(i, k):
            value, rest, parts = three_parts[i]
            if k == 1:
                act.wait_ge(cut, 2 * i + 1)
            copy(parts[k], (value, rest)[k]).then_inc(rounded, 1)

        for q in range(4):
            act.wait_ge(sh_gu, q + 1)
            if q >= 2:
                act.wait_ge(sh_h, q - 1)
            act.activation(act_s[:, q % 2, :], bank[2 * (q % 2)][0:F0, :], ACT.Silu).then_inc(sh_silu, 1)
            if q == 1:
                round_part(0, 1)
                act.wait_ge(weights_ready, 1)
                round_part(1, 0)
            if q == 2:
                round_part(1, 1)
        act.wait_ge(count_ready, 1)
        n = act.value_load(count[0:1, 0:1], min_val=1, max_val=TILES)
        for k in range(2 * HALF):
            act.wait_ge(gathered, k + 1)
            act.activation(XT[:, BLOCK * k:BLOCK * k + BLOCK], bank[k % HALF], ACT.Copy).then_inc(xt_ready, 1)

        def round_outputs(r, g):
            act.wait_ge(ys_ready, r * 2 + (g + 3))
            p = ds(r * (2 * WP) + g * WP, WP)
            high_part(copy, ypart[:, p, 0, :], ys[:, p, :]).then_inc(y_rounded, 1)

        with act.Fori(0, ROUNDS) as r:
            for j in range(2 * WP):
                at = r * (2 * WP) + j
                act.wait_ge(gu_done, at + 1)
                act.wait_ge(h_ready, at + 1)
                act.activation(own_slots(slot(act_s, j)), diagonal(gu_bank(j)[0:F0, 0:2 * P]),
                               ACT.Silu).then_inc(silu_done, 1)
                if j == WP + 1:
                    round_outputs(r, 0)
            round_outputs(r, 1)
        with act.Fori(0, n) as t:
            for k in range(CHUNKS):
                act.wait_ge(c_turned, t * CHUNKS + (k + RING + 1))
                act.wait_ge(combined, t * CHUNKS + (k + 1))
                copy(ST[:, k % RING, :].bitcast(F32R), bank[k % RING].bitcast(BF16)[:, 0:BLOCK]).then_inc(st_ready, 1)

    def vector(dve):
        ln.vector(dve)
        c = Chain(chain)

        def step(ins):
            dve.wait_ge(c.sem, c.on(ins))

        def shared_hidden(q):
            dve.wait_ge(sh_silu, q + 1)
            if q >= 2:
                dve.wait_ge(sh_y, q - 1)
            dve.tensor_tensor(hT[:, q % 2, :], act_s[:, q % 2, :], bank[2 * (q % 2) + 1][0:F0, :],
                              ALU.mult).then_inc(sh_h, 1)

        def shared_add(q):
            dve.wait_ge(sh_y, q + 1)
            xq = core.x[:, 4 * q:4 * q + 4, :]
            dve.scalar_tensor_tensor(xq, bank[2 * (q % 2)].rearrange("p (t n) -> p t n", n=P), 0.5, xq,
                                     ALU.mult, ALU.add).then_inc(sh_added, 1)

        most, den = (col[:, i, :] for i in range(2))
        dve.wait_ge(logits_done, 1)
        for h in range(2):
            lg = bank[4 + h].rearrange("p (t e) -> p t e", e=E0)
            step(dve.tensor_reduce(most[:, 8 * h:8 * h + 8], lg, AX.X, ALU.max))
            step(dve.tensor_tensor(ex[:, 8 * h:8 * h + 8, :], lg, bcast(most[:, 8 * h:8 * h + 8], E0), ALU.subtract))
        dve.sem_inc(shifted, 1)
        dve.wait_ge(exp_done, 1)
        for i in range(TILES):
            last = dve.max(top[:, i, :], ex[:, i, :])
        step(last)
        shared_hidden(0)
        for i in range(TILES):
            last = dve.match_replace(repl[:, i, :], top[:, i, :], ex[:, i, :], -1.0)
        step(last)
        step(dve.tensor_scalar(mask[:, :, :], repl[:, :, :], 0.0, None, ALU.is_lt))
        dve.sem_inc(mask_ready, 1)
        shared_hidden(1)
        shared_add(0)
        step(dve.scalar_tensor_tensor(weight[:, :, :], repl[:, :, :], 0.0, ex[:, :, :], ALU.is_lt, ALU.mult))
        step(dve.tensor_reduce(den, top[:, :, :], AX.X, ALU.add))
        step(dve.reciprocal(den, den))
        step(dve.tensor_scalar(den, den, 0.5, None, ALU.mult))
        step(dve.tensor_tensor(weight[:, :, :], weight[:, :, :], bcast(den, E0), ALU.mult))
        dve.sem_inc(weights_ready, 1)
        shared_hidden(2)
        shared_add(1)
        dve.wait_ge(counted, 1)
        step(dve.memset(base[:, 0, :], 0.0))
        for i in range(TILES - 1):
            tot = bank[6 + i // 8][:, E0 * (i % 8):E0 * (i % 8) + E0]
            step(dve.tensor_tensor(base[:, i + 1, :], base[:, i, :], tot, ALU.add))
        step(dve.tensor_reduce(room[:, 0, :], base[0:1, :, :], AX.X, ALU.min))
        step(dve.tensor_scalar(room[:, 1, :], room[:, 0, :], float(CAPACITY), None, ALU.is_lt))
        step(dve.tensor_reduce(count_f[:, :], room[:, 1, :], AX.X, ALU.add))
        step(dve.tensor_copy(count[:, :], count_f[:, :]))
        shared_add(2)
        shared_hidden(3)
        for h in range(2):
            cum = bank[4 + h].rearrange("p (t e) -> p t e", e=E0)
            bh = base[:, 8 * h:8 * h + 8, :]
            step(dve.tensor_tensor(bh, bh, cum, ALU.add))
        step(dve.scalar_tensor_tensor(base[:, :, :], base[:, :, :], float(CAPACITY), base[:, :, :], ALU.is_le, ALU.mult))
        step(dve.tensor_tensor(place[:, 0:TILES, :], base[:, :, :], mask[:, :, :], ALU.mult))
        dve.sem_inc(count_ready, 1)
        shared_add(3)
        dve.wait_ge(sh_added, 4)
        n = dve.value_load(count[0:1, 0:1], min_val=1, max_val=TILES)

        def make_chunk(t, k, slot):
            return dve.tensor_tensor(S[:, slot, :].rearrange("p (t e n) -> p t e n", t=1, n=CAPACITY),
                                     bcast(place[:, ds(t, 1), CE * k:CE * k + CE], CAPACITY),
                                     number[:, :].unsqueeze(1).unsqueeze(1).to_broadcast([P, 1, CE, CAPACITY]),
                                     ALU.is_equal)

        for half in range(2):
            if half:
                dve.wait_ge(gathered, HALF)
            with dve.Fori(0, n) as t:
                for k in range(HALF):
                    dve.wait_ge(s_used[half], t * HALF + (k + 1))
                    make_chunk(t, half * HALF + k, k).then_inc(s_made[half], 1)
        dve.wait_ge(gathered, 2 * HALF + 1)
        step(dve.tensor_reduce(wboth[:, :, :], bank[4][:, 0:6 * PAIRS].rearrange("p (q e i) -> p q e i", e=2, i=3),
                               AX.X, ALU.add))
        for i in range(2):
            own = slice(CAPACITY * i, CAPACITY * i + CAPACITY)
            last = dve.tensor_copy(wslot[own, :], wboth[own, :, i])
        step(last)
        dve.sem_inc(wslot_ready, 1)
        with dve.Fori(0, ROUNDS) as r:
            at = r * (2 * WP)

            def hidden(j):
                dve.wait_ge(silu_done, at + (j + 1))
                dve.wait_ge(y_done, at + (j + 1))
                dve.tensor_tensor(own_slots(slot(hT, j)), own_slots(slot(act_s, j)),
                                  diagonal(gu_bank(j)[0:F0, 2 * P:4 * P]), ALU.mult).then_inc(h_ready, 1)

            def outputs(g):
                dve.wait_ge(y_done, at + (WP * g + WP + DEPTH))
                dve.tensor_tensor(ys[:, ds(at + g * WP, WP), :], bank[2 + g].rearrange("p (q n) -> p q n", n=P),
                                  bcast(wslot[:, ds(at + g * WP, WP)], P), ALU.mult).then_inc(ys_ready, 1)

            for j in range(2 * WP):
                hidden(j)
                if j == WP:
                    outputs(0)
            outputs(1)
        dve.wait_ge(c_turned, RING)
        for k in range(RING):
            make_chunk(0, k, k).then_inc(c_made, 1)
        with dve.Fori(0, n) as t:
            for k in range(RING, CHUNKS + RING):
                dve.wait_ge(c_turned, t * CHUNKS + (k + 1))
                ahead = k // CHUNKS
                make_chunk(t + ahead, k % CHUNKS, k % RING).then_inc(c_made, 1)
            dve.wait_ge(combined, t * CHUNKS + (CHUNKS + RING))
            dve.tensor_reduce(summed[:, :], bank[6][:, 0:2 * P].rearrange("p (i n) -> p n i", i=2), AX.X,
                              ALU.add).then_inc(sum_read, 1)
            dve.wait_ge(sum_read, t + 2)
            xt = core.x[:, ds(t, 1), :].rearrange("p t n -> p (t n)")
            dve.tensor_tensor(xt, xt, summed[:, :], ALU.add).then_inc(x_added, 1)
            dve.wait_ge(x_added, t + 1)

    return dict(sync=sync, gpsimd=gpsimd, tensor=tensor, scalar=scalar, vector=vector)


H0, D0 = 16, 8
HG = 4
VW = 32


def attention_zero(core, name, ctx, w):
    nc = core.nc
    sb = lambda n, s, d=F32: ctx.enter_context(nc.sbuf_tensor(f"{name}_{n}", s, d))
    ln = LayerNorm(core, ctx, name)
    bank = core.bank
    SCALE = float(1.0 / np.sqrt(D0))
    NP = 6
    wqkv = sb("wqkv", [P, 3, P])
    bqkv = sb("bqkv", [P, 3, P])
    bv = sb("bv", [P, 1])
    wl = sb("wl", [P, 3])
    bl = sb("bl", [P, 1])
    cos = sb("cos", [P, 4, D0])
    sin = sb("sin", [P, 4, D0])
    rot = sb("rot", [P, 2, 4, H0, D0 // 2])
    z = sb("z", [P, 2, 4, P])
    e = sb("e", [P, 2, 4, P])
    rest = sb("rest", [P, 2, 4, P])
    part = [sb(f"part{i}", [P, 2, TILES, P], BF16) for i in range(3)]
    V = sb("V", [P, TILES, P])
    vT = sb("vT", [P, BLOCK])
    lT = sb("lT", [P, TOKENS])
    stack = [[sb(f"stack{i}{a}", [P, 2, H0, P], BF16) for a in range(2)] for i in range(2)]
    turned = [[sb(f"turned{i}{a}", [P, H0, SEQ], BF16) for a in range(2)] for i in range(2)]
    Vs = [sb(f"Vs{i}", [P, 2, H0, VW]) for i in range(2)]
    lTs = [sb(f"lTs{i}", [P, SEQ]) for i in range(2)]
    select = sb("select", [P, H0, P], BF16)
    negmax = sb("negmax", [P, 2, H0])
    mparts = sb("mparts", [P, 2, P], BF16)
    shift = [sb(f"shift{i}", [P, SEQ], BF16) for i in range(2)]
    PT = sb("PT", [P, 2, HG, SEQ])
    OT = sb("OT", [P, 2, SEQ])
    rden = sb("rden", [P, 2, HG])
    attn = sb("attn", [P, 2, HG, D0])
    loaded = core.sem(f"{name}_loaded")
    filled = core.sem(f"{name}_filled")
    consts = core.sem(f"{name}_consts")
    qkv_done = core.sem(f"{name}_qkv_done")
    qkv_read = core.sem(f"{name}_qkv_read")
    neg_ready = core.sem(f"{name}_neg_ready")
    exp_ready = core.sem(f"{name}_exp_ready")
    rot_ready = core.sem(f"{name}_rot_ready")
    vT_done = core.sem(f"{name}_vT_done")
    vT_ready = core.sem(f"{name}_vT_ready")
    rounded = core.sem(f"{name}_rounded")
    rest_ready = core.sem(f"{name}_rest_ready")
    chain = core.sem(f"{name}_chain")
    stacked = core.sem(f"{name}_stacked")
    v_staged = core.sem(f"{name}_v_staged")
    st_turned = core.sem(f"{name}_st_turned")
    st_ready = core.sem(f"{name}_st_ready")
    s1_done = core.sem(f"{name}_s1_done")
    max_done = core.sem(f"{name}_max_done")
    parts_ready = core.sem(f"{name}_parts_ready")
    parts_hi = core.sem(f"{name}_parts_hi")
    parts_turned = core.sem(f"{name}_parts_turned")
    shift_ready = core.sem(f"{name}_shift_ready")
    s2_done = core.sem(f"{name}_s2_done")
    p_ready = core.sem(f"{name}_p_ready")
    pv_done = core.sem(f"{name}_pv_done")
    o_ready = core.sem(f"{name}_o_ready")
    o_turned = core.sem(f"{name}_o_turned")
    o_inv = core.sem(f"{name}_o_inv")
    o_scaled = core.sem(f"{name}_o_scaled")
    o_added = core.sem(f"{name}_o_added")
    l_turned = core.sem(f"{name}_l_turned")
    l_added = core.sem(f"{name}_l_added")
    UNITS = 2 * H0 // HG
    MUNITS = H0

    def sync(sp):
        sp.dma_start(wqkv[:, :, :], w["w_qkv"]).then_inc(loaded, 16)
        sp.dma_start(bqkv[:, :, :], w["b_qkv"].unsqueeze(0).to_broadcast([P, 3, P])).then_inc(loaded, 16)
        sp.dma_start(bv[:, :], w["b_v"]).then_inc(loaded, 16)
        sp.dma_start(wl[:, :], w["w_lepe"]).then_inc(loaded, 16)
        sp.dma_start(bl[:, :], w["b_lepe"]).then_inc(loaded, 16)
        sp.dma_start(cos[:, :, :], w["rope_cos"]).then_inc(loaded, 16)
        sp.dma_start(sin[:, :, :], w["rope_sin"]).then_inc(loaded, 16)

    def gpsimd(pool):
        for i in range(2):
            for a in range(2):
                pool.memset(stack[i][a][:, :, :, :], 0.0).then_inc(filled, 1)
            pool.memset(Vs[i][:, :, :, :], 0.0).then_inc(filled, 1)
        pool.memset(select[:, :, :], 0.0).then_inc(filled, 1)
        pool.memset(mparts[:, :, :], 0.0).then_inc(consts, 1)
        pool.wait_ge(filled, 7)
        for i in range(2):
            pool.memset(Vs[i][:, :, :, D0:D0 + 1], 1.0).then_inc(consts, 1)
        pool.affine_select(out=select[:, :, :], in_=select[:, :, :], compare_op=ALU.not_equal, fill=1.0, base=0,
                           pattern=[[-1, H0], [0, P]], channel_multiplier=1).then_inc(filled, 1)
        pool.wait_ge(filled, 8)
        pool.affine_select(out=select[:, :, :], in_=select[:, :, :], compare_op=ALU.not_equal, fill=1.0, base=-H0,
                           pattern=[[-1, H0], [0, P]], channel_multiplier=1).then_inc(consts, 1)
        pool.wait_ge(consts, 4)
        pool.wait_ge(loaded, 7 * 16)
        for q in range(4):
            for i, out in enumerate((rest[:, :, :, :], part[2][:, :, 4 * q:4 * q + 4, :])):
                pool.wait_ge(rounded, 2 * q + (i + 1))
                rounds = part[i][:, :, 4 * q:4 * q + 4, :]
                before = (z, rest)[i]
                for a in range(2):
                    last = pool.tensor_tensor(out[:, a, :, :], before[:, a, :, :], rounds[:, a, :, :], ALU.subtract)
                last.then_inc(rest_ready, 1)
            pool.wait_ge(rest_ready, 2 * q + 2)
        for b in range(BATCH):
            if 2 <= b + 1 < BATCH:
                pool.wait_ge(st_turned, UNITS * b)
                stack_batch(pool.tensor_copy, b + 1)
            stage_values(pool, b)

    def stack_batch(copy, b):
        s = b % 2
        t = slice(2 * b, 2 * b + 2)
        for a, copies in enumerate((
                ((0, slice(0, 3)), (1, slice(3, 5)), (2, slice(5, 6))),
                ((0, slice(0, 4, 3)), (0, slice(5, 6)), (1, slice(1, 5, 3)), (2, slice(2, 3))))):
            view = stack[s][a][:, :, :, 0:NP * D0].rearrange("p t h (k d) -> p (t h) k d", d=D0)
            for i, slots in copies:
                dst = view[:, :, slots, :]
                n = dst.shape[2]
                src = part[i][:, a, t, :].rearrange("p t (h d) -> p (t h) d", d=D0)
                last = copy(dst, src.unsqueeze(2).to_broadcast([P, 2 * H0, n, D0]))
        last.then_inc(stacked, 1)

    def stage_values(pool, b):
        s = b % 2
        if b >= 2:
            pool.wait_ge(pv_done, UNITS * (b - 1) + 2)
            pool.wait_ge(l_turned, b - 1)
        pool.wait_ge(vT_ready, b // 2 + 1)
        pool.tensor_copy(lTs[s][:, :], lT[:, SEQ * b:SEQ * b + SEQ])
        pool.tensor_copy(Vs[s][:, :, :, 0:D0],
                         V[:, 2 * b:2 * b + 2, :].rearrange("p t (h d) -> p t h d", d=D0)).then_inc(v_staged, 1)

    def tensor(pe):
        def turn_stack(b, s, v, ahead=1):
            to = bank[(v + 1) % ahead if ahead > 1 else 1].bitcast(BF16)
            g, a = v // 2, v % 2
            if v == 0:
                pe.wait_ge(stacked, b + 1)
            if v >= ahead or ahead == 1:
                pe.wait_ge(st_ready, b * UNITS + (v + 2 - ahead))
            for j in range(HG):
                for t in range(2):
                    last = pe.transpose(to[:, SEQ * j + P * t:SEQ * j + P * t + P],
                                        stack[s][a][:, t, HG * g + j, :], core.identb[:, :])
            last.then_inc(st_turned, 1)

        def scores_by_query(b, s, m):
            h, qt = 2 * (m // 2), m % 2
            if h % HG == 0 and qt == 0:
                pe.wait_ge(st_ready, b * UNITS + (2 * (h // HG) + 3))
            pe.wait_ge(max_done, b * MUNITS + (m + 1))
            for j in range(2):
                last = pe.matmul(bank[0][:, SEQ * j:SEQ * j + SEQ], turned[s][0][:, h + j, P * qt:P * qt + P],
                                 turned[s][1][:, h + j, :], start=True, stop=True)
            last.then_inc(s1_done, 1)

        def turn_maxima(b, s, former):
            pe.wait_ge(parts_ready, b + 2)
            if former:
                pe.wait_ge(o_added, b * 4)
            for qt in range(2):
                last = pe.transpose(bank[7].bitcast(BF16)[:, P * qt:P * qt + P], mparts[:, qt, :], core.identb[:, :])
            last.then_inc(parts_turned, 1)

        def values(b, s, u):
            g, kt = u // 2, u % 2
            pe.wait_ge(p_ready, b * UNITS + (u + 3))
            if u == 0:
                pe.wait_ge(v_staged, b + 1)
            if kt == 0:
                pe.wait_ge(o_ready, b * 4 + (g + 1))
            for j in range(HG):
                last = pe.matmul(bank[6][VW * j:VW * j + VW, 0:SEQ], Vs[s][:, kt, HG * g + j, :],
                                 PT[:, u % 2, j, :], start=(kt == 0), stop=(kt == 1))
            last.then_inc(pv_done, 1)

        def turn_out(b, s, g, following=False):
            pe.wait_ge(o_ready, b * 4 + (g + 2))
            pe.wait_ge(o_added, b * 4 + (g + 1))
            if g == 0:
                pe.wait_ge(l_added, b + 2)
            if g == 3 and following:
                pe.wait_ge(shift_ready, b + 3)
            for qt in range(2):
                last = pe.transpose(bank[7][:, P * qt:P * qt + P], OT[:, g % 2, P * qt:P * qt + P], core.ident[:, :])
            last.then_inc(o_turned, 1)

        def turn_convolution(b, s):
            pe.wait_ge(o_added, b * 4 + 1)
            pe.wait_ge(v_staged, b + 1)
            for qt in range(2):
                last = pe.transpose(bank[7][:, P * qt:P * qt + P], lTs[s][:, P * qt:P * qt + P], core.ident[:, :])
            last.then_inc(l_turned, 1)

        def batch(b, s, next1, next2):
            pe.wait_ge(shift_ready, b + 2)
            for u in range(UNITS):
                g, kt = u // 2, u % 2
                pe.wait_ge(p_ready, b * UNITS + (u + 1))
                for half in range(2):
                    out = bank[2 + 2 * (u % 2) + half]
                    for j in range(2):
                        h = HG * g + 2 * half + j
                        pe.matmul(out[:, SEQ * j:SEQ * j + SEQ], turned[s][1][:, h, P * kt:P * kt + P],
                                  turned[s][0][:, h, :], start=True, stop=False, skip_group_check=True)
                        last = pe.matmul(out[:, SEQ * j:SEQ * j + SEQ], select[:, h, :], shift[s][:, :],
                                         start=False, stop=True, skip_group_check=True)
                last.then_inc(s2_done, 1)
                if next1:
                    scores_by_query(b + 1, 1 - s, 2 * u)
                if next1 and u < 2:
                    turn_stack(b + 1, 1 - s, UNITS - 2 + u)
                if next2 and u >= 2:
                    turn_stack(b + 2, s, u - 2)
                if u:
                    values(b, s, u - 1)
                if u == 1:
                    turn_convolution(b, s)
                if u >= 3 and u % 2:
                    turn_out(b, s, (u - 3) // 2)
                if next1:
                    scores_by_query(b + 1, 1 - s, 2 * u + 1)
            values(b, s, UNITS - 1)
            if next1:
                turn_maxima(b + 1, 1 - s, True)
            turn_out(b, s, 3, following=next1)

        ln.tensor(pe)
        pe.wait_ge(loaded, 7 * 16)
        for q in range(4):
            pe.wait_ge(ln.xnT_ready, q + 1)
            if q:
                pe.wait_ge(qkv_read, q)
            for i in range(3):
                for t in range(4):
                    at = P * (4 * q + t)
                    last = pe.matmul(bank[4 + i][:, P * t:P * t + P], ln.xnT[:, at:at + P], wqkv[:, i, :],
                                     start=True, stop=True)
            last.then_inc(qkv_done, 1)
            if q:
                pe.wait_ge(vT_ready, q)
            pe.matmul(bank[7], wqkv[:, 2, :], ln.xnT[:, BLOCK * q:BLOCK * q + BLOCK],
                      start=True, stop=True).then_inc(vT_done, 1)
            if q == 3:
                pe.wait_ge(ln.xnT_ready, 4)
                pe.sem_inc(st_ready, 1)
                for v in range(UNITS):
                    turn_stack(0, 0, v, ahead=4)
        pe.wait_ge(consts, 4)
        pe.wait_ge(vT_ready, 4)
        pe.sem_inc(max_done, 1)
        pe.sem_inc(p_ready, 2)
        pe.sem_inc(pv_done, 2)
        pe.sem_inc(o_ready, 1)
        pe.sem_inc(o_added, 1)
        pe.sem_inc(l_added, 1)
        pe.sem_inc(shift_ready, 1)
        pe.wait_ge(st_ready, UNITS + 1)
        for m in range(MUNITS):
            scores_by_query(0, 0, m)
            if m % 2 and m // 2 < UNITS - 2:
                turn_stack(1, 1, m // 2)
        turn_maxima(0, 0, False)
        with pe.Fori(0, BATCH // 2 - 1) as bp:
            for s in range(2):
                batch(bp * 2 + s, s, True, True)
        batch(BATCH - 2, 0, True, False)
        batch(BATCH - 1, 1, False, False)

    def scalar(act):
        def copy(out, in_):
            return act.activation(out, in_, ACT.Copy)

        def take_turned(b, s, v, ahead=1):
            g, a = v // 2, v % 2
            act.wait_ge(st_turned, b * UNITS + (v + 1))
            out = bank[(v + 1) % ahead if ahead > 1 else 1].bitcast(BF16)
            copy(turned[s][a][:, HG * g:HG * g + HG, :],
                 out.rearrange("p (h n) -> p h n", n=SEQ)).then_inc(st_ready, 1)

        def batch(b, s, next1, next2):
            for u in range(UNITS):
                act.wait_ge(s2_done, b * UNITS + (u + 1))
                act.wait_ge(pv_done, b * UNITS + (u + 1))
                pair = core.psum[:, 2 + 2 * (u % 2):4 + 2 * (u % 2), :].rearrange("p a (h n) -> p (a h) n", n=SEQ)
                act.activation(PT[:, u % 2, :, :], pair, ACT.Exp, scale=SCALE).then_inc(p_ready, 1)
                if next1 and u < 2:
                    take_turned(b + 1, 1 - s, UNITS - 2 + u)
                if next2 and u >= 2:
                    take_turned(b + 2, s, u - 2)

        ln.scalar(act)
        for q in range(4):
            act.wait_ge(neg_ready, q + 1)
            act.activation(e[:, :, :, :], e[:, :, :, :], ACT.Exp).then_inc(exp_ready, 1)
            if q == 3:
                for v in range(UNITS):
                    take_turned(0, 0, v, ahead=4)
            act.wait_ge(rot_ready, q + 1)
            act.activation(part[0][:, :, 4 * q:4 * q + 4, :], z[:, :, :, :], ACT.Copy).then_inc(rounded, 1)
            act.wait_ge(rest_ready, 2 * q + 1)
            act.activation(part[1][:, :, 4 * q:4 * q + 4, :], rest[:, :, :, :], ACT.Copy).then_inc(rounded, 1)
            if q == 0:
                act.wait_ge(rest_ready, 2)
                act.wait_ge(consts, 4)
                stack_batch(copy, 0)
                stack_batch(copy, 1)
        for v in range(UNITS - 2):
            take_turned(1, 1, v)
        with act.Fori(0, BATCH // 2 - 1) as bp:
            for s in range(2):
                batch(bp * 2 + s, s, True, True)
        batch(BATCH - 2, 0, True, False)
        batch(BATCH - 1, 1, False, False)

    def vector(dve):
        ln.vector(dve)
        c = Chain(chain)

        def step(ins):
            dve.wait_ge(c.sem, c.on(ins))

        dve.wait_ge(loaded, 7 * 16)
        for q in range(4):
            dve.wait_ge(qkv_done, q + 1)
            if q:
                dve.wait_ge(rest_ready, 2 * q - 1)
            for i in range(2):
                step(dve.tensor_tensor(z[:, i, :, :], bank[4 + i].rearrange("p (t n) -> p t n", n=P),
                                       bqkv[:, i, :].unsqueeze(1).to_broadcast([P, 4, P]), ALU.add))
            dve.tensor_scalar(e[:, :, :, :], z[:, :, :, :], 0.0, None, ALU.min).then_inc(neg_ready, 1)
            step(dve.tensor_tensor(V[:, 4 * q:4 * q + 4, :], bank[6].rearrange("p (t n) -> p t n", n=P),
                                   bqkv[:, 2, :].unsqueeze(1).to_broadcast([P, 4, P]), ALU.add))
            dve.sem_inc(qkv_read, 1)
            dve.wait_ge(vT_done, q + 1)
            step(dve.tensor_scalar(vT[:, :], bank[7], bv[:, 0:1], None, ALU.add))
            lq = lT[:, BLOCK * q:BLOCK * q + BLOCK]
            step(dve.tensor_scalar(lq, vT[:, :], wl[:, 1:2], bl[:, 0:1], ALU.mult, ALU.add))
            l2 = lq.rearrange("p (b n) -> p b n", n=SEQ)
            v2 = vT[:, :].rearrange("p (b n) -> p b n", n=SEQ)
            step(dve.scalar_tensor_tensor(l2[:, :, 1:SEQ], v2[:, :, 0:SEQ - 1], wl[:, 0:1], l2[:, :, 1:SEQ],
                                          ALU.mult, ALU.add))
            step(dve.scalar_tensor_tensor(l2[:, :, 0:SEQ - 1], v2[:, :, 1:SEQ], wl[:, 2:3], l2[:, :, 0:SEQ - 1],
                                          ALU.mult, ALU.add))
            dve.sem_inc(vT_ready, 1)
            dve.wait_ge(exp_ready, q + 1)
            step(dve.scalar_tensor_tensor(e[:, :, :, :].rearrange("p i t n -> p (i t n)"),
                                          z[:, :, :, :].rearrange("p i t n -> p (i t n)"), 0.0,
                                          e[:, :, :, :].rearrange("p i t n -> p (i t n)"), ALU.max, ALU.add))
            for i in range(2):
                src = e[:, i, :, :].rearrange("p t (h d) -> p t h d", d=D0)
                dst = z[:, i, :, :].rearrange("p t (h d) -> p t h d", d=D0)
                co = cos[:, :, :].unsqueeze(2).to_broadcast([P, 4, H0, D0])
                si = sin[:, :, :].unsqueeze(2).to_broadcast([P, 4, H0, D0])
                c.on(dve.tensor_tensor(dst, src, co, ALU.mult))
                for o in range(2):
                    c.on(dve.tensor_tensor(rot[:, o, :, :, :], src[:, :, :, 1 - o::2], si[:, :, :, o::2], ALU.mult))
                dve.wait_ge(c.sem, c.n)
                for o in range(2):
                    c.on(dve.tensor_tensor(dst[:, :, :, o::2], dst[:, :, :, o::2], rot[:, o, :, :, :], ALU.add))
                dve.wait_ge(c.sem, c.n)
            dve.sem_inc(rot_ready, 1)

        def maximum(b, m):
            h, qt = 2 * (m // 2), m % 2
            dve.wait_ge(s1_done, b * MUNITS + (m + 1))
            if m == 0:
                dve.wait_ge(parts_ready, b + 1)
            dve.tensor_reduce(negmax[:, qt, h:h + 2], bank[0].rearrange("p (h n) -> p h n", n=SEQ), AX.X, ALU.max,
                              negate=True).then_inc(max_done, 1)

        def split_maxima(b, s):
            dve.wait_ge(max_done, b * MUNITS + (MUNITS + 1))
            dve.wait_ge(parts_turned, b + 1)
            dve.tensor_copy(mparts[:, :, 0:H0], negmax[:, :, :]).then_inc(parts_hi, 1)
            dve.wait_ge(parts_hi, b + 1)
            dve.tensor_tensor(mparts[:, :, H0:2 * H0], negmax[:, :, :], mparts[:, :, 0:H0],
                              ALU.subtract).then_inc(parts_ready, 1)

        def take_shift(b, s):
            dve.wait_ge(parts_turned, b + 2)
            dve.tensor_copy(shift[s][:, :], bank[7].bitcast(BF16)[:, 0:SEQ]).then_inc(shift_ready, 1)

        def add_convolution(b):
            dve.wait_ge(l_turned, b + 1)
            xb = core.x[:, ds(b * 2, 2), :]
            dve.tensor_tensor(xb, xb, bank[7][:, 0:SEQ].rearrange("p (t n) -> p t n", n=P), ALU.add).then_inc(l_added, 1)

        def group(b, s, g):
            dve.wait_ge(pv_done, b * UNITS + (2 * g + 4))
            dve.tensor_copy(OT[:, g % 2, :], bank[6][:, 0:SEQ]).then_inc(o_ready, 1)

        def finish_group(b, s, g):
            dve.wait_ge(o_turned, b * 4 + (g + 1))
            o = bank[7][:, 0:SEQ].rearrange("p (t j v) -> p t j v", t=2, v=VW)
            dve.reciprocal(rden[:, :, :], o[:, :, :, D0]).then_inc(o_inv, 1)
            dve.wait_ge(o_inv, b * 4 + (g + 1))
            dve.tensor_tensor(attn[:, :, :, :], o[:, :, :, 0:D0], bcast(rden[:, :, :], D0), ALU.mult).then_inc(o_scaled, 1)
            dve.wait_ge(o_scaled, b * 4 + (g + 1))
            if g == 0:
                dve.wait_ge(l_added, b + 2)
            xg = core.x[:, ds(b * 2, 2), HG * D0 * g:HG * D0 * g + HG * D0]
            dve.tensor_tensor(xg, xg, attn[:, :, :, :].rearrange("p t j d -> p t (j d)"), ALU.add).then_inc(o_added, 1)

        dve.sem_inc(parts_ready, 1)
        dve.sem_inc(parts_turned, 1)
        for m in range(MUNITS):
            maximum(0, m)
        split_maxima(0, 0)
        take_shift(0, 0)

        def batch(b, s, next1):
            for u in range(UNITS):
                if u == 2:
                    add_convolution(b)
                if u >= 3 and u % 2:
                    group(b, s, (u - 3) // 2)
                if next1:
                    maximum(b + 1, 2 * u)
                    maximum(b + 1, 2 * u + 1)
                if u >= 3 and u % 2:
                    finish_group(b, s, (u - 3) // 2)
            if next1:
                split_maxima(b + 1, 1 - s)
            group(b, s, 3)
            if next1:
                take_shift(b + 1, 1 - s)
            finish_group(b, s, 3)

        with dve.Fori(0, BATCH // 2 - 1) as bp:
            for s in range(2):
                batch(bp * 2 + s, s, True)
        batch(BATCH - 2, 0, True)
        batch(BATCH - 1, 1, False)

    return dict(sync=sync, gpsimd=gpsimd, tensor=tensor, scalar=scalar, vector=vector)


H1, D1, NB1, SPAN = 16, 64, 10, 128
CH = H1 // 2
RH = 8
ZW = 3 * SPAN
MASKED = 1e9


def attention_one(core, name, ctx, w):
    nc = core.nc
    sb = lambda n, s, d=F32: ctx.enter_context(nc.sbuf_tensor(f"{name}_{n}", s, d))
    ln = LayerNorm(core, ctx, name)
    bank = core.bank
    RSCALE = float(D1) ** -0.5
    sizes = dict(wr=H1 * NB1, wq=H1 * D1, wk=H1 * D1, wv=H1 * D1)
    wr, wq, wk, wv = ([sb(f"{n}_{part}", [P, size]) for part in ("high", "rest")] for n, size in sizes.items())
    wp = sb("wp", [P, CH, P])
    bq = sb("bq", [P, 2, CH])
    br = sb("br", [RH * NB1, 2])
    bp_row = sb("bp_row", [P, P])
    bnd = sb("bnd", [RH * NB1, RH, SPAN])
    pad = sb("pad", [P, SPAN])
    xs = [sb(f"xs_{part}", [P, 2, SEQ]) for part in ("high", "rest")]
    RT = sb("RT", [RH * NB1, 2, SEQ])
    G = sb("G", [P, 2, H1, SPAN])
    X0 = [sb(f"X0_{i}", [P, H1, SPAN]) for i in range(2)]
    X1 = [sb(f"X1_{i}", [P, H1, 2 * SPAN]) for i in range(2)]
    Qz = [sb(f"Qz{i}", [P, H1, SEQ]) for i in range(2)]
    KT = [sb(f"KT{i}", [P, CH, SEQ]) for i in range(2)]
    V = [sb(f"V{i}", [P, 2, H1 * D1]) for i in range(2)]
    L = sb("L", [P, 2, 3 * P])
    least = sb("least", [P, 2, 2])
    pr = sb("pr", [P, 4, 3 * P])
    sums = sb("sums", [P, 4, 2])
    rinv = sb("rinv", [P, 4, 2])
    PT = sb("PT", [P, 2, 3 * P])
    AT = ln.xn[:, :, :].rearrange("p a n -> p (a n)").rearrange("p (c n) -> p c n", n=SEQ)
    flat = X1[0][:, :, :].rearrange("p h n -> p (h n)")
    raw_wq, raw_wk, raw_wv = (flat[:, H1 * D1 * i:H1 * D1 * (i + 1)] for i in range(3))
    raw_wr = flat[:, 3 * H1 * D1:3 * H1 * D1 + H1 * NB1]
    cuts = ((raw_wr, wr), (raw_wq, wq), (raw_wk, wk), (raw_wv, wv))
    z = [[nc.dram_tensor(f"{name}_z{s}{q}", [P * H1 * ZW], F32) for q in range(2)] for s in range(2)]

    loaded = core.sem(f"{name}_loaded")
    bnd_zero = core.sem(f"{name}_bnd_zero")
    q_zero = core.sem(f"{name}_q_zero")
    prep = core.sem(f"{name}_prep")
    pad_filled = core.sem(f"{name}_pad_filled")
    pads_written = core.sem(f"{name}_pads_written")
    w_high = core.sem(f"{name}_w_high")
    w_rest = core.sem(f"{name}_w_rest")
    xs_high = core.sem(f"{name}_xs_high")
    xs_ready = core.sem(f"{name}_xs_ready")
    xs_free = core.sem(f"{name}_xs_free")
    piece_done = core.sem(f"{name}_piece_done")
    piece_read = [core.sem(f"{name}_piece_read{i}") for i in range(2)]
    g_by_act = core.sem(f"{name}_g_by_act")
    g_by_dve = core.sem(f"{name}_g_by_dve")
    z_written = core.sem(f"{name}_z_written")
    x_turned = core.sem(f"{name}_x_turned")
    qkv_act = core.sem(f"{name}_qkv_act")
    qkv_dve = core.sem(f"{name}_qkv_dve")
    s_done = core.sem(f"{name}_s_done")
    l_begun = core.sem(f"{name}_l_begun")
    l_ready = core.sem(f"{name}_l_ready")
    p_ready = core.sem(f"{name}_p_ready")
    inv_ready = core.sem(f"{name}_inv_ready")
    pn_ready = core.sem(f"{name}_pn_ready")
    p_turned = core.sem(f"{name}_p_turned")
    pT_ready = core.sem(f"{name}_pT_ready")
    pv_done = core.sem(f"{name}_pv_done")
    aT_ready = core.sem(f"{name}_aT_ready")
    out_done = core.sem(f"{name}_out_done")
    out_added = core.sem(f"{name}_out_added")
    PIECES = 21
    STEPS = H1 + 3
    plan = [[u] for u in range(H1)] + [[16, 17], [18, 19], [20]]

    def kind(k):
        if k == 0:
            return "R", 0
        if k < 9:
            return "G", k - 1
        if k < 17:
            return "QK", k - 9
        return "V", k - 17

    def by_act(k):
        name_, j = kind(k)
        return name_ != "R" and j % 2 == 0

    N_ACT = sum(by_act(k) and kind(k)[0] in ("QK", "V") for k in range(PIECES))
    N_DVE = sum(not by_act(k) and kind(k)[0] in ("QK", "V") for k in range(PIECES))

    def piece_at(bp, s, k):
        return (s + k) % 2, bp * PIECES + (s * PIECES + k) // 2

    def sync(sp):
        sp.dma_start(raw_wr, w["Wr"]).then_inc(loaded, 16)
        sp.dma_start(raw_wq, w["Wq"]).then_inc(loaded, 16)
        sp.dma_start(raw_wk, w["Wk"]).then_inc(loaded, 16)
        sp.dma_start(raw_wv, w["Wv"]).then_inc(loaded, 16)
        sp.dma_start(wp[:, :, :], w["Wproj"].rearrange("(c p) n -> p c n", p=P)).then_inc(loaded, 16)
        sp.dma_start(bq[:, 0, :], w["bq"]).then_inc(loaded, 16)
        sp.dma_start(br[:, :], w["br"]).then_inc(loaded, 16)
        sp.dma_start(bp_row[:, :], w["bproj"].unsqueeze(0).to_broadcast([P, P])).then_inc(loaded, 16)
        sp.wait_ge(bnd_zero, 1)
        for h in range(RH):
            sp.dma_start(bnd[NB1 * h:NB1 * h + NB1, h, :], w["b_nd"]).then_inc(loaded, 16)
        sp.sem_inc(z_written, 32)
        sp.sem_inc(x_turned, 64)
        sp.wait_ge(pad_filled, 1)
        for s in range(2):
            for q in range(2):
                rows = z[s][q].ap().rearrange("(p h n) -> p h n", h=H1, n=ZW)
                for side in ((2 * SPAN,), (0, 2 * SPAN))[q]:
                    sp.dma_start(rows[:, :, side:side + SPAN],
                                 pad[:, :].unsqueeze(1).to_broadcast([P, H1, SPAN])).then_inc(pads_written, 16)
        for b in range(BATCH):
            s = b % 2
            sp.wait_ge(x_turned, 32 * (b + 1))
            if b >= 2:
                sp.wait_ge(l_ready, H1 * (b - 1) + 2)
            for q in range(2):
                sp.wait_ge(g_by_act, 4 * b + 2 * (q + 1))
                sp.wait_ge(g_by_dve, 4 * b + 2 * (q + 1))
                rows = z[s][q].ap().rearrange("(p h n) -> p h n", h=H1, n=ZW)
                sp.dma_start(rows[:, :, SPAN:2 * SPAN], G[:, q, :, :]).then_inc(z_written, 16)
                sp.wait_ge(z_written, 32 * (b + 1) + 16 * (q + 1))
                if b == 0 and q == 0:
                    sp.wait_ge(pads_written, 6 * 16)
                    sp.wait_ge(w_rest, 4)
                turned = bass.AP(z[s][q], 2 * SPAN - 1 - SPAN * q, [[H1 * ZW - 1, P], [ZW, H1], [1, SPAN * (q + 1)]])
                sp.dma_start((X0, X1)[q][s][:, :, :], turned).then_inc(x_turned, 16)
        sp.wait_ge(x_turned, 32 * (BATCH + 2))

    def gpsimd(pool):
        pool.memset(bnd[:, :, :], 0.0).then_inc(bnd_zero, 1)
        pool.memset(pad[:, :], MASKED).then_inc(pad_filled, 1)
        for s in range(2):
            pool.memset(Qz[s][:, :, :], 0.0).then_inc(q_zero, 1)
        pool.wait_ge(ln.xnT_ready, 4)
        pool.sem_inc(xs_free, 2)
        for b in range(BATCH):
            pool.wait_ge(xs_free, b + 1)
            full, high, rest = ln.xnT[:, SEQ * b:SEQ * b + SEQ], xs[0][:, b % 2, :], xs[1][:, b % 2, :]
            high_part(pool.tensor_copy, high, full).then_inc(xs_high, 1)
            pool.wait_ge(xs_high, b + 1)
            rest_part(pool, rest, full, high).then_inc(xs_ready, 1)

    def tensor(pe):
        ln.tensor(pe)
        pe.wait_ge(loaded, 16 * 16)
        pe.wait_ge(ln.xnT_ready, 4)
        pe.sem_inc(piece_read[0], 1)
        pe.sem_inc(piece_read[1], 1)

        def piece(bp, s, k):
            which, j = kind(k)
            i, used = piece_at(bp, s, k)
            out = bank[5 + i]
            b = bp * 2 + s
            if k == 0:
                pe.wait_ge(xs_ready, b + 1)
            if k == 1:
                pe.wait_ge(piece_read[s % 2], bp * PIECES + (s * PIECES) // 2 + 2)
            pe.wait_ge(piece_read[i], used + 1)
            if which == "R":
                for c in range(2):
                    last = matmul_by_parts(pe, out[0:RH * NB1, SEQ * c:SEQ * c + SEQ],
                                           [m[:, RH * NB1 * c:RH * NB1 * (c + 1)] for m in wr],
                                           [m[:, s, :] for m in xs], True, True)
            elif which == "G":
                q, c, half = j // 4, (j % 4) // 2, j % 2
                last = pe.matmul(out, RT[:, c, P * q:P * q + P],
                                 bnd[:, 4 * half:4 * half + 4, :].rearrange("p h n -> p (h n)"), start=True, stop=True)
            elif which == "QK":
                for a, m in enumerate((wq, wk)):
                    last = matmul_by_parts(pe, out[:, SEQ * a:SEQ * a + SEQ], [i[:, P * j:P * j + P] for i in m],
                                           [i[:, s, :] for i in xs], True, True)
            else:
                t, half = j // 2, j % 2
                last = matmul_by_parts(pe, out, [m[:, s, P * t:P * t + P] for m in xs],
                                       [m[:, 512 * half:512 * half + 512] for m in wv], True, True)
            last.then_inc(piece_done, 1)
            if k == PIECES - 1:
                pe.wait_ge(piece_done, b * PIECES + PIECES)
                pe.sem_inc(xs_free, 1)

        def scores(b, s, h):
            pe.wait_ge(l_ready, b * H1 + (h + 1))
            S = bank[h % 2]
            pe.matmul(S[:, 0:P], Qz[s][:, h, 0:P], KT[s][:, h // 2, 0:P], start=True, stop=True)
            pe.matmul(S[:, P:3 * P], Qz[s][:, h, P:2 * P], KT[s][:, h // 2, :], start=True, stop=True).then_inc(s_done, 1)

        def turn(b, h):
            pe.wait_ge(pn_ready, b * H1 + (h + 1))
            pe.wait_ge(pT_ready, b * H1 + (h + 1))
            for i in range(3):
                last = pe.transpose(bank[2 + h % 2][:, P * i:P * i + P], pr[:, h % 4, P * i:P * i + P],
                                    core.ident[:, :])
            last.then_inc(p_turned, 1)

        def values(b, s, h):
            c, half = h // 2, h % 2
            pe.wait_ge(pT_ready, b * H1 + (h + 3))
            if half == 0:
                pe.wait_ge(aT_ready, b * CH + (c + 1))
                if c == 0:
                    pe.wait_ge(out_added, b + 1)
            o = bank[4 + 3 * (c % 2)][D1 * half:D1 * half + D1, 0:SEQ]
            vh = V[s][:, :, D1 * h:D1 * h + D1]
            pe.matmul(o, vh[:, 0, :], PT[:, h % 2, 0:SEQ], start=True, stop=False, skip_group_check=True)
            pe.matmul(o[:, P:2 * P], vh[:, 1, :], PT[:, h % 2, SEQ:SEQ + P], start=False, stop=True,
                      skip_group_check=True).then_inc(pv_done, 1)

        def batch(bp, s, following):
            b = bp * 2 + s
            nbp, ns = (bp, 1) if s == 0 else (bp + 1, 0)
            for u in range(STEPS):
                if u == 0:
                    pe.wait_ge(qkv_act, b * N_ACT + N_ACT)
                    pe.wait_ge(qkv_dve, b * N_DVE + N_DVE)
                if u < H1:
                    scores(b, s, u)
                if 2 <= u < H1 + 2:
                    turn(b, u - 2)
                if u >= 3:
                    values(b, s, u - 3)
                if following:
                    for k in plan[u]:
                        piece(nbp, ns, k)
            pe.wait_ge(aT_ready, b * CH + (CH + 2))
            for q in range(2):
                for c in range(CH):
                    last = pe.matmul(bank[4][:, P * q:P * q + P], AT[:, c, P * q:P * q + P], wp[:, c, :],
                                     start=(c == 0), stop=(c == CH - 1))
            last.then_inc(out_done, 1)

        pe.wait_ge(q_zero, 2)
        pe.wait_ge(w_rest, 4)
        for k in range(PIECES):
            piece(0, 0, k)
        pe.sem_inc(pv_done, 2)
        pe.sem_inc(p_turned, 4)
        pe.sem_inc(out_done, 1)
        with pe.Fori(0, BATCH // 2 - 1) as bp:
            for s in range(2):
                batch(bp, s, True)
        batch(BATCH // 2 - 1, 0, True)
        batch(BATCH // 2 - 1, 1, False)

    def store_piece(eng, is_act, bp, s, k):
        which, j = kind(k)
        i, _ = piece_at(bp, s, k)
        out = bank[5 + i]
        b = bp * 2 + s
        eng.wait_ge(piece_done, b * PIECES + (k + 1))
        if which == "R":
            for c in range(2):
                last = eng.tensor_scalar(RT[:, c, :], out[0:RH * NB1, SEQ * c:SEQ * c + SEQ], br[:, c:c + 1], -1.0,
                                         ALU.add, ALU.mult)
            return last
        if which == "G":
            q, c, half = j // 4, (j % 4) // 2, j % 2
            if j % 4 < 2:
                eng.wait_ge(z_written, b * 32 + 16 * (q + 1))
            dst = G[:, q, RH * c + 4 * half:RH * c + 4 * half + 4, :]
            src = out.rearrange("p (h n) -> p h n", n=SPAN)
        elif which == "QK":
            qa = out[0:D1, 0:SEQ], Qz[s][0:D1, 2 * j, :], bq[0:D1, :, j:j + 1]
            qb = out[D1:P, 0:SEQ], Qz[s][D1:P, 2 * j + 1, :], bq[D1:P, :, j:j + 1]
            for src, dst, bias in (qa, qb):
                if is_act:
                    eng.activation(dst, src, ACT.Identity, bias=bias[:, 1, :], scale=-RSCALE)
                else:
                    eng.tensor_scalar(dst, src, bias[:, 0, :], -RSCALE, ALU.add, ALU.mult)
            dst, src = KT[s][:, j, :], out[:, SEQ:2 * SEQ]
        else:
            t, half = j // 2, j % 2
            dst, src = V[s][:, t, 512 * half:512 * half + 512], out
        return eng.activation(dst, src, ACT.Copy) if is_act else eng.tensor_copy(dst, src)

    def stored(eng, is_act, bp, s, k):
        which, _ = kind(k)
        i, _ = piece_at(bp, s, k)
        last = store_piece(eng, is_act, bp, s, k)
        last.then_inc(piece_read[i], 1)
        if which != "R":
            done = {("G", True): g_by_act, ("G", False): g_by_dve}.get((which, is_act), qkv_act if is_act else qkv_dve)
            eng.wait_ge(piece_read[i], piece_at(bp, s, k)[1] + 2)
            eng.sem_inc(done, 1)

    def scalar(act):
        ln.scalar(act)
        act.wait_ge(loaded, 16 * 16)
        for raw, parts in cuts:
            high_part(lambda out, in_: act.activation(out, in_, ACT.Copy), parts[0][:, :], raw).then_inc(w_high, 1)
        act.wait_ge(prep, 2)
        act.wait_ge(q_zero, 2)

        def pieces(bp, s, ks):
            for k in ks:
                if by_act(k):
                    stored(act, True, bp, s, k)

        def probabilities(b, h):
            act.wait_ge(l_ready, b * H1 + (h + 3))
            act.wait_ge(p_turned, b * H1 + (h + 1))
            act.activation(pr[:, h % 4, 0:P], L[:, h % 2, 0:P], ACT.Exp, bias=least[:, h % 2, 0:1], scale=-1.0,
                           accum_out=sums[:, h % 4, 0:1])
            act.activation(pr[:, h % 4, P:3 * P], L[:, h % 2, P:3 * P], ACT.Exp, bias=least[:, h % 2, 1:2], scale=-1.0,
                           accum_out=sums[:, h % 4, 1:2]).then_inc(p_ready, 1)

        def batch(bp, s, following):
            b = bp * 2 + s
            nbp, ns = (bp, 1) if s == 0 else (bp + 1, 0)
            for u in range(STEPS + 1):
                if 2 <= u < H1 + 2:
                    h = u - 2
                    act.wait_ge(p_turned, b * H1 + (h + 5))
                    act.wait_ge(pv_done, b * H1 + (h + 1))
                    act.activation(PT[:, h % 2, :], bank[2 + h % 2][:, 0:3 * P], ACT.Copy).then_inc(pT_ready, 1)
                if u >= 5 and u % 2:
                    c = (u - 5) // 2
                    act.wait_ge(pv_done, b * H1 + (2 * c + 4))
                    act.wait_ge(out_done, b + 1)
                    act.activation(AT[:, c, :], bank[4 + 3 * (c % 2)][:, 0:SEQ], ACT.Copy).then_inc(aT_ready, 1)
                if u < H1:
                    probabilities(b, u)
                if following and u < STEPS:
                    pieces(nbp, ns, plan[u])

        act.sem_inc(pT_ready, 2)
        act.sem_inc(aT_ready, 2)
        pieces(0, 0, range(PIECES))
        with act.Fori(0, BATCH // 2 - 1) as bp:
            for s in range(2):
                batch(bp, s, True)
        batch(BATCH // 2 - 1, 0, True)
        batch(BATCH // 2 - 1, 1, False)

    def vector(dve):
        ln.vector(dve)
        dve.wait_ge(loaded, 16 * 16)
        dve.tensor_scalar(bq[:, 1, :], bq[:, 0, :], -RSCALE, None, ALU.mult).then_inc(prep, 1)
        for i, (raw, parts) in enumerate(cuts):
            dve.wait_ge(w_high, i + 1)
            rest_part(dve, parts[1][:, :], raw, parts[0][:, :]).then_inc(w_rest, 1)
        dve.wait_ge(q_zero, 2)
        dve.wait_ge(ln.xn_ready, TILES)
        dve.tensor_tensor(core.x[:, :, :], core.x[:, :, :],
                          bp_row[:, :].unsqueeze(1).to_broadcast([P, TILES, P]), ALU.add).then_inc(prep, 1)
        dve.wait_ge(prep, 2)

        def pieces(bp, s, ks):
            for k in ks:
                if not by_act(k):
                    stored(dve, False, bp, s, k)

        def logits(b, s, h):
            dve.wait_ge(s_done, b * H1 + (h + 1))
            dve.wait_ge(p_ready, b * H1 + (h + 1))
            if h == 0:
                dve.wait_ge(x_turned, b * 32 + 96)
            dve.sem_inc(l_begun, 1)
            S = bank[h % 2]
            dve.tensor_tensor_reduce(L[:, h % 2, 0:P], S[:, 0:P], X0[s][:, h, :], 1.0, 3.0e38, ALU.add, ALU.min,
                                     least[:, h % 2, 0:1])
            dve.tensor_tensor_reduce(L[:, h % 2, P:3 * P], S[:, P:3 * P], X1[s][:, h, :], 1.0, 3.0e38, ALU.add, ALU.min,
                                     least[:, h % 2, 1:2]).then_inc(l_ready, 1)

        def normalise(b, h):
            dve.wait_ge(p_ready, b * H1 + (h + 3))
            dve.reciprocal(rinv[:, h % 4, :], sums[:, h % 4, :]).then_inc(inv_ready, 1)
            dve.wait_ge(inv_ready, b * H1 + (h + 1))
            dve.tensor_scalar(pr[:, h % 4, 0:P], pr[:, h % 4, 0:P], rinv[:, h % 4, 0:1], None, ALU.mult)
            dve.tensor_scalar(pr[:, h % 4, P:3 * P], pr[:, h % 4, P:3 * P], rinv[:, h % 4, 1:2], None,
                              ALU.mult).then_inc(pn_ready, 1)

        def batch(bp, s, following):
            b = bp * 2 + s
            nbp, ns = (bp, 1) if s == 0 else (bp + 1, 0)
            for u in range(STEPS):
                if u < H1:
                    logits(b, s, u)
                if 1 <= u < H1 + 1:
                    normalise(b, u - 1)
                if following:
                    pieces(nbp, ns, plan[u])
            dve.wait_ge(out_done, b + 2)
            xb = core.x[:, ds(b * 2, 2), :]
            dve.tensor_tensor(xb, xb, bank[4][:, 0:SEQ].rearrange("p (t n) -> p t n", n=P), ALU.add).then_inc(out_added, 1)

        dve.sem_inc(l_ready, 2)
        dve.sem_inc(p_ready, 2)
        dve.sem_inc(out_added, 1)
        pieces(0, 0, range(PIECES))
        with dve.Fori(0, BATCH // 2 - 1) as bp:
            for s in range(2):
                batch(bp, s, True)
        batch(BATCH // 2 - 1, 0, True)
        batch(BATCH // 2 - 1, 1, False)

    return dict(sync=sync, gpsimd=gpsimd, tensor=tensor, scalar=scalar, vector=vector)


def build(nc, w, out, stages):
    with ExitStack() as ctx:
        core = Core(nc, ctx)
        make_constants = constants(core)
        x_loaded = core.sem("x_loaded")
        stored = core.sem("stored")
        stage_done = core.sem("stage_done")
        stage_cleared = core.sem("stage_cleared")
        made, sems = [], []
        for name, make in stages:
            with ExitStack() as local:
                core.ctx, core.stage_sems = local, []
                made.append(make(core, name, local, w))
                sems.append(core.stage_sems)
        block = ctx.enter_context(nc.Block())
        x_dram = w["x"].rearrange("(t p) d -> p t d", p=P)
        out_dram = out.rearrange("(t p) d -> p t d", p=P)

        def stage_end(eng, n):
            eng.drain().then_inc(stage_done, 1)
            if eng is nc.sync:
                eng.wait_ge(stage_done, 5 * (n + 1))
                for s in sems[n]:
                    eng.sem_clear(s)
                eng.sem_inc(stage_cleared, 1)
            eng.wait_ge(stage_cleared, n + 1)

        @block.sync
        def _(sp):
            sp.dma_start(core.x[:, :, :], x_dram).then_inc(x_loaded, 16)
            for n, st in enumerate(made):
                st["sync"](sp)
                stage_end(sp, n)
            sp.dma_start(out_dram, core.x[:, :, :]).then_inc(stored, 16)
            sp.wait_ge(stored, 16)

        @block.gpsimd
        def _(pool):
            make_constants(pool)
            for n, st in enumerate(made):
                st["gpsimd"](pool)
                stage_end(pool, n)

        @block.tensor
        def _(pe):
            pe.wait_ge(core.const_ready, 4)
            for n, st in enumerate(made):
                st["tensor"](pe)
                stage_end(pe, n)

        @block.scalar
        def _(act):
            for n, st in enumerate(made):
                st["scalar"](act)
                stage_end(act, n)

        @block.vector
        def _(dve):
            dve.wait_ge(x_loaded, 16)
            for n, st in enumerate(made):
                st["vector"](dve)
                stage_end(dve, n)


STAGES = [
    ("f0", mixture_zero), ("a0", attention_zero), ("g0", mixture_zero),
    ("f1", mixture_one), ("a1", attention_one), ("g1", mixture_one),
]


def rotary_tables():
    position = np.arange(SEQ, dtype=np.float32)[:, None]
    step = np.exp(np.arange(0, D0, 2, dtype=np.float32) * np.float32(-np.log(10000.0) / D0))
    angle = (position * step).astype(np.float32)
    sign = np.array([-1.0, 1.0] * (D0 // 2), np.float32)
    cos = np.repeat(np.cos(angle), 2, axis=1).astype(np.float32)
    sin = (np.repeat(np.sin(angle), 2, axis=1) * sign).astype(np.float32)
    lay = lambda a: np.ascontiguousarray(np.concatenate([a.reshape(2, P, D0).transpose(1, 0, 2)] * 2, axis=1))
    return lay(cos), lay(sin)


def kernel(**inputs):
    import concourse.bacc as bacc
    from concourse.bass_utils import run_bass_kernel_spmd

    i = {k: np.asarray(v) for k, v in inputs.items()}
    m, a = "L0_ffn_", "L1_attn_"
    cos, sin = rotary_tables()
    laid = {
        "x": i["L0_attn_x"].reshape(TOKENS, P),
        "router": i[m + "router_w"].T, "slot_number": np.arange(1, CAPACITY + 1, dtype=np.float32),
        "ws_gate_up": i[m + "ws_gate_up"], "ws_down": i[m + "ws_down"],
        "gate_up": np.concatenate([i[m + "w_gate"], i[m + "w_up"]], axis=2).transpose(1, 0, 2),
        "down": i[m + "w_down"].transpose(1, 0, 2),
        "w_qkv": i["L0_attn_w_qkv"].T.reshape(P, 3, P), "b_qkv": i["L0_attn_b_qkv"].reshape(3, P),
        "b_v": i["L0_attn_b_qkv"][2 * P:].reshape(P, 1), "w_lepe": i["L0_attn_w_lepe"].reshape(P, 3),
        "b_lepe": i["L0_attn_b_lepe"].reshape(P, 1), "rope_cos": cos, "rope_sin": sin,
        "Wg": i["L1_ffn_Wg"], "bg": i["L1_ffn_bg"], "W1": i["L1_ffn_W1"], "W2": i["L1_ffn_W2"], "b2": i["L1_ffn_b2"],
        "b1": i["L1_ffn_b1"].reshape(E1, FC1, P).transpose(2, 0, 1),
        "Wq": i[a + "Wq"], "Wk": i[a + "Wk"], "Wv": i[a + "Wv"], "Wproj": i[a + "Wproj"], "Wr": i[a + "Wr"],
        "bq": i[a + "bq"].reshape(CH, P).T, "br": i[a + "br"].reshape(2, RH * NB1).T, "bproj": i[a + "bproj"],
        "b_nd": i[a + "b_nd"][:, ::-1],
    }
    nc = bacc.Bacc("TRN2", target_bir_lowering=False, num_devices=1)
    arrays, w = {}, {}
    for name, value in laid.items():
        arrays[f"in_{name}"] = np.ascontiguousarray(value)
        w[name] = nc.dram_tensor(f"in_{name}", value.shape, F32, kind="ExternalInput").ap()
    out = nc.dram_tensor("out", (TOKENS, P), F32, kind="ExternalOutput").ap()
    build(nc, w, out, STAGES)
    r = run_bass_kernel_spmd(nc, [arrays], core_ids=[0])
    return r.results[0]["out"].reshape(BATCH, SEQ, P)
```
